# Optimizing a Trainium2 kernel written in Bass

```python
import numpy as np
import jax
import jax.numpy as jnp

def _softmax(x, axis=-1):
    return jax.nn.softmax(x, axis=axis)

def _gelu(x):
    return jax.nn.gelu(x, approximate=True)

def _silu(x):
    return jax.nn.silu(x)

def _sigmoid(x):
    return jax.nn.sigmoid(x)

def _layernorm(x, axis=-1, eps=1e-05):
    m = jnp.mean(x, axis=axis, keepdims=True)
    v = jnp.var(x, axis=axis, keepdims=True)
    return (x - m) / jnp.sqrt(v + eps)

def _scatter_add(tgt, idx, src, axis=0):
    return tgt.at[idx].add(src)

def _segment_sum(src, seg, n):
    return jax.ops.segment_sum(src, seg, n)
kernel_name = 'mk_vit_tower_cls_d1_tok_img768_r4_acf3f7'

def setup_inputs(seed: int=0):
    np.random.seed(seed)
    _w = jnp.asarray

    def _rec_inputs():
        import jax
        import jax.numpy as jnp
        _rk = jax.random.key(seed)
        x = -9.30917e-05 + 1.0002 * jax.random.normal(jax.random.fold_in(_rk, 1), (64, 3, 224, 224), jnp.float32)
        cls_tok = 0.02 * jax.random.normal(jax.random.fold_in(_rk, 5), (1, 1, 192), jnp.float32)
        return (x, cls_tok)
    x, cls_tok = _rec_inputs()

    def _L0_tok_setup():
        import jax, jax.numpy as jnp
        import numpy as np
        PATCH = 16
        EPS = 1e-05

        def _shift(x, pad_spec):
            l, r, t, b = pad_spec
            H, W = (x.shape[2], x.shape[3])
            xp = jnp.pad(x, ((0, 0), (0, 0), (max(t, 0), max(b, 0)), (max(l, 0), max(r, 0))))
            h0 = -t if t < 0 else 0
            w0 = -l if l < 0 else 0
            return xp[:, :, h0:h0 + H, w0:w0 + W]
        key = jax.random.key(seed)
        k1, k2 = jax.random.split(key)
        B, C, H, Wd = (32, 3, 224, 224)
        patch_dim = PATCH * PATCH * 5 * C
        dim = 192
        x = jax.random.normal(k1, (B, C, H, Wd), dtype=jnp.float32)
        ln_gamma = jnp.ones((patch_dim,), dtype=jnp.float32)
        ln_beta = jnp.zeros((patch_dim,), dtype=jnp.float32)
        W = jax.random.normal(k2, (patch_dim, dim), dtype=jnp.float32) * patch_dim ** (-0.5)
        b = jnp.zeros((dim,), dtype=jnp.float32)
        return {'x': x, 'ln_gamma': ln_gamma, 'ln_beta': ln_beta, 'W': W, 'b': b}
    _L0_tok_all = _L0_tok_setup()
    _L0_tok_in = {k: v for k, v in _L0_tok_all.items() if k in ('ln_gamma', 'ln_beta', 'W', 'b')}
    del _L0_tok_all

    def _L0_attn_setup():
        import jax, jax.numpy as jnp
        import numpy as np
        NUM_HEADS = 12

        def rotate_every_two(x):
            x1 = x[..., ::2]
            x2 = x[..., 1::2]
            return jnp.stack((-x2, x1), axis=-1).reshape(x.shape)

        def rope_cos_sin(seq_len, dim):
            inv_freq = 1.0 / 10000.0 ** (jnp.arange(0, dim, 2, dtype=jnp.float32) / dim)
            t = jnp.arange(seq_len, dtype=jnp.float32)
            freqs = t[:, None] * inv_freq[None, :]
            emb = jnp.concatenate([freqs, freqs], axis=-1)
            return (jnp.cos(emb)[None, None], jnp.sin(emb)[None, None])
        key = jax.random.key(seed)
        kx, k1, k2, k3, k4 = jax.random.split(key, 5)
        B, S, D = (1, 1024, 192)
        scale = 1.0 / np.sqrt(D)
        x = jax.random.normal(kx, (B, S, D), dtype=jnp.float32)
        W_qkv = jax.random.normal(k1, (D, 3 * D), dtype=jnp.float32) * scale
        b_qkv = jax.random.normal(k2, (3 * D,), dtype=jnp.float32) * 0.01
        W_out = jax.random.normal(k3, (D, D), dtype=jnp.float32) * scale
        b_out = jax.random.normal(k4, (D,), dtype=jnp.float32) * 0.01
        return {'x': x, 'W_qkv': W_qkv, 'b_qkv': b_qkv, 'W_out': W_out, 'b_out': b_out}
    _L0_attn_all = _L0_attn_setup()
    _L0_attn_in = {k: v for k, v in _L0_attn_all.items() if k in ('W_qkv', 'b_qkv', 'W_out', 'b_out')}
    del _L0_attn_all

    def _L0_ffn_setup():
        import jax, jax.numpy as jnp
        import numpy as np
        CAPACITY_FACTOR = 1.25
        key = jax.random.key(seed)
        ks = jax.random.split(key, 5)
        B, S, D, F, E = (8, 512, 192, 768, 8)
        return {'x': jax.random.normal(ks[0], (B, S, D), jnp.float32), 'switch_w': jax.random.normal(ks[1], (D, E), jnp.float32) * 0.02, 'switch_b': jnp.zeros((E,), jnp.float32), 'w1': jax.random.normal(ks[2], (E, D, F), jnp.float32) * 0.02, 'b1': jnp.zeros((E, F), jnp.float32), 'w2': jax.random.normal(ks[3], (E, F, D), jnp.float32) * 0.02, 'b2': jnp.zeros((E, D), jnp.float32)}
    _L0_ffn_all = _L0_ffn_setup()
    _L0_ffn_in = {k: v for k, v in _L0_ffn_all.items() if k in ('switch_w', 'switch_b', 'w1', 'b1', 'w2', 'b2')}
    del _L0_ffn_all
    return {'x': x, 'cls_tok': cls_tok, 'L0_tok_ln_gamma': _L0_tok_in['ln_gamma'], 'L0_tok_ln_beta': _L0_tok_in['ln_beta'], 'L0_tok_W': _L0_tok_in['W'], 'L0_tok_b': _L0_tok_in['b'], 'L0_attn_W_qkv': _L0_attn_in['W_qkv'], 'L0_attn_b_qkv': _L0_attn_in['b_qkv'], 'L0_attn_W_out': _L0_attn_in['W_out'], 'L0_attn_b_out': _L0_attn_in['b_out'], 'L0_ffn_switch_w': _L0_ffn_in['switch_w'], 'L0_ffn_switch_b': _L0_ffn_in['switch_b'], 'L0_ffn_w1': _L0_ffn_in['w1'], 'L0_ffn_b1': _L0_ffn_in['b1'], 'L0_ffn_w2': _L0_ffn_in['w2'], 'L0_ffn_b2': _L0_ffn_in['b2']}

def reference(x, cls_tok, L0_tok_ln_gamma, L0_tok_ln_beta, L0_tok_W, L0_tok_b, L0_attn_W_qkv, L0_attn_b_qkv, L0_attn_W_out, L0_attn_b_out, L0_ffn_switch_w, L0_ffn_switch_b, L0_ffn_w1, L0_ffn_b1, L0_ffn_w2, L0_ffn_b2):
    import jax
    import jax.numpy as jnp

    def _L0_tok_ref(x, ln_gamma, ln_beta, W, b):
        import jax, jax.numpy as jnp
        import numpy as np
        PATCH = 16
        EPS = 1e-05

        def _shift(x, pad_spec):
            l, r, t, b = pad_spec
            H, W = (x.shape[2], x.shape[3])
            xp = jnp.pad(x, ((0, 0), (0, 0), (max(t, 0), max(b, 0)), (max(l, 0), max(r, 0))))
            h0 = -t if t < 0 else 0
            w0 = -l if l < 0 else 0
            return xp[:, :, h0:h0 + H, w0:w0 + W]
        shifts = [(1, -1, 0, 0), (-1, 1, 0, 0), (0, 0, 1, -1), (0, 0, -1, 1)]
        xs = jnp.concatenate([x] + [_shift(x, s) for s in shifts], axis=1)
        B, C5, H, Wd = xs.shape
        h, w = (H // PATCH, Wd // PATCH)
        t = xs.reshape(B, C5, h, PATCH, w, PATCH)
        t = t.transpose(0, 2, 4, 3, 5, 1)
        t = t.reshape(B, h * w, PATCH * PATCH * C5)
        mu = jnp.mean(t, axis=-1, keepdims=True)
        var = jnp.var(t, axis=-1, keepdims=True)
        tn = (t - mu) * jax.lax.rsqrt(var + EPS) * ln_gamma + ln_beta
        return jnp.einsum('bnp,pd->bnd', tn, W) + b

    def _L0_attn_ref(x, W_qkv, b_qkv, W_out, b_out):
        import jax, jax.numpy as jnp
        import numpy as np
        NUM_HEADS = 12

        def rotate_every_two(x):
            x1 = x[..., ::2]
            x2 = x[..., 1::2]
            return jnp.stack((-x2, x1), axis=-1).reshape(x.shape)

        def rope_cos_sin(seq_len, dim):
            inv_freq = 1.0 / 10000.0 ** (jnp.arange(0, dim, 2, dtype=jnp.float32) / dim)
            t = jnp.arange(seq_len, dtype=jnp.float32)
            freqs = t[:, None] * inv_freq[None, :]
            emb = jnp.concatenate([freqs, freqs], axis=-1)
            return (jnp.cos(emb)[None, None], jnp.sin(emb)[None, None])
        B, S, D = x.shape
        H = NUM_HEADS
        hd = D // H
        qkv = x @ W_qkv + b_qkv
        qkv = qkv.reshape(B, S, 3, H, hd).transpose(2, 0, 3, 1, 4)
        q, k, v = (qkv[0], qkv[1], qkv[2])
        cos, sin = rope_cos_sin(S, hd)
        q = q * cos + rotate_every_two(q) * sin
        k = k * cos + rotate_every_two(k) * sin
        scores = jnp.einsum('bhqd,bhkd->bhqk', q, k) / np.float32(np.sqrt(hd))
        probs = jax.nn.softmax(scores, axis=-1)
        ctx = jnp.einsum('bhqk,bhkd->bhqd', probs, v)
        ctx = ctx.transpose(0, 2, 1, 3).reshape(B, S, D)
        return ctx @ W_out + b_out

    def _L0_ffn_ref(x, switch_w, switch_b, w1, b1, w2, b2):
        import jax, jax.numpy as jnp
        import numpy as np
        CAPACITY_FACTOR = 1.25
        B, S, D = x.shape
        E = w1.shape[0]
        xf = x.reshape(-1, D)
        N = xf.shape[0]
        capacity = int(CAPACITY_FACTOR * N / E)
        probs = jax.nn.softmax(xf @ switch_w + switch_b, axis=-1)
        prob_max = jnp.max(probs, axis=-1)
        routes = jnp.argmax(probs, axis=-1)
        sort_idx = jnp.lexsort((-prob_max, routes))
        counts = jnp.bincount(routes, length=E)
        starts = jnp.concatenate([jnp.zeros((1,), counts.dtype), jnp.cumsum(counts)[:-1]])
        rank_sorted = jnp.arange(N) - starts[routes[sort_idx]]
        rank = jnp.zeros((N,), jnp.int32).at[sort_idx].set(rank_sorted.astype(jnp.int32))
        keep = rank < capacity
        dest_e = jnp.where(keep, routes, E)
        dest_c = jnp.where(keep, rank, 0)
        buf = jnp.zeros((E + 1, capacity, D), xf.dtype).at[dest_e, dest_c].set(xf)
        h = jax.nn.gelu(jnp.einsum('ecd,edf->ecf', buf[:E], w1) + b1[:, None, :], approximate=False)
        o = jnp.einsum('ecf,efd->ecd', h, w2) + b2[:, None, :]
        y_exp = o[routes, dest_c]
        y = jnp.where(keep[:, None], y_exp, xf)
        out = y * prob_max[:, None]
        return out.reshape(B, S, D)
    h = _L0_tok_ref(x, L0_tok_ln_gamma, L0_tok_ln_beta, L0_tok_W, L0_tok_b)
    h = jnp.concatenate([jnp.broadcast_to(cls_tok, (h.shape[0], 1, h.shape[2])), h], axis=1)
    h = h + _L0_attn_ref(_layernorm(h, axis=-1), L0_attn_W_qkv, L0_attn_b_qkv, L0_attn_W_out, L0_attn_b_out)
    h = h + _L0_ffn_ref(_layernorm(h, axis=-1), L0_ffn_switch_w, L0_ffn_switch_b, L0_ffn_w1, L0_ffn_b1, L0_ffn_w2, L0_ffn_b2)
    return h

_drawn_inputs = setup_inputs


def setup_inputs(seed=0):
    import zlib

    import numpy as np

    out = dict(_drawn_inputs(seed))
    spreads = {'L0_tok_ln_gamma': (1.0, 0.2),
     'L0_tok_ln_beta': (0.0, 0.1),
     'L0_tok_b': (0.0, 0.1),
     'L0_ffn_switch_b': (0.0, 0.1),
     'L0_ffn_b1': (0.0, 0.8),
     'L0_ffn_b2': (0.0, 0.475)}
    factors = {'cls_tok': 4.03,
     'L0_attn_b_qkv': 3.913,
     'L0_attn_b_out': 4.133,
     'L0_ffn_w1': 4.139,
     'L0_ffn_w2': 3.851}
    for name, (base, spread) in spreads.items():
        noise = np.random.default_rng([zlib.crc32(name.encode()), seed]).standard_normal(out[name].shape)
        drawn = base * np.exp(spread * noise) if base else spread * noise
        out[name] = jnp.asarray(drawn.astype(out[name].dtype))
    for name, factor in factors.items():
        out[name] = (out[name] * factor).astype(out[name].dtype)
    return out
```

```python
from contextlib import ExitStack

import concourse.bass as bass
from concourse import mybir

F32, F16, U32 = mybir.dt.float32, mybir.dt.float16, mybir.dt.uint32
ALU, ACT, AX = mybir.AluOpType, mybir.ActivationFunctionType, mybir.AxisListType

P = 128
IMAGES, SIDE, PATCH, CH = 64, 14, 16, 3
PATCHES = SIDE * SIDE
TOK = PATCHES + 1
REST = PATCHES - P
D, HEADS, HD = 192, 12, 16
TERMS = PATCH * PATCH * CH * 5
KP, KT, SHIFTS = 121, 8, 5
GT = 256
GROUPS = IMAGES * PATCHES // GT
EXPERTS, FF = 8, 768
NTOK = IMAGES * TOK
CAP = int(1.25 * NTOK / EXPERTS)
REC = 196
EPS = 1e-5
NW = 3 * D + D + EXPERTS
W_OUT, W_SW = 3 * D, 4 * D
FAR = float(1 << 22)
TILES = (NTOK + EXPERTS * (P - 1)) // P
REGION = (NTOK // P + 3) * P
DUMMY = EXPERTS * REGION
CHUNK = NTOK // 16
FT = FF // P
STEPS = 29

C_ID, C_TRI, C_COS, C_SIN, C_MULT, C_TOKN, C_VALID, C_FAR, C_SLOT, C_IOTA = 0, 128, 256, 1024, 1792, 1793, 1795, 1797, 1799, 1807
N_CONST = 1816
K_BLOCK, K_BEFORE, K_UPTO, K_IOTA, K_IOTA128, K_SEL, K_TAIL = 0, 128, 256, 384, 512, 640, 648
K_FIRST, K_CODE, K_REGION, K_EXPERT, K_PAD, N_CONST3 = 656, 657, 658, 659, 660, 661


def after(*steps):
    done, total = {}, 0
    for s in steps:
        name, n = s if isinstance(s, tuple) else (s, 1)
        total += n
        done[name] = total
    return done


PLAN = after("onef", "one788", ("prow", 6), "pe_e", "n_cnt", "n_e", "ntile", "dn", "end", "tails", "start", "g_cnt", "tie", "tied",
             "room", "lim", "cut_cnt", "sel_a", "vrow", "sel", ("vals", 3), "cut", "vals_all", ("tables", 3))
SUMS = after("n", "end", "tail", "g", "before", "cut", "table")


class Sems:

    def __init__(self, nc, ctx):
        self._made, self._nc, self._ctx = {}, nc, ctx

    def __getitem__(self, name):
        if name not in self._made:
            self._made[name] = self._ctx.enter_context(self._nc.semaphore(name))
        return self._made[name]


def wait(eng, sem, value):
    if not (isinstance(value, int) and value <= 0):
        eng.wait_ge(sem, value)


def build(nc, xt, wraw, graw, braw, tokb, cls, wqkv, bqkv, wout, bout, wsw, bsw, w1, b1, w2, b2, consts, consts3, out):
    ctx = ExitStack()
    with ctx:
        sb = lambda name, shape, dt=F32: area.enter_context(nc.sbuf_tensor(name, shape, dt))
        area = ctx
        S = Sems(nc, ctx)
        hp = nc.dram_tensor("hp", (IMAGES * PATCHES, D), F32).ap()

        cst = sb("cst", [P, N_CONST])
        ident = cst[:, C_ID:C_ID + P]
        idh = sb("idh", [P, P], F16)
        oneh = sb("oneh", [P, P], F16)
        pall = sb("pall", [P, 2, 2, IMAGES])
        ps = ctx.enter_context(nc.psum_tensor("ps", [P, 8, 512], F32))
        area = early = ctx.enter_context(ExitStack())
        xb = sb("xb", [KP, 2, KT, GT])
        xsq = sb("xsq", [KP, KT, GT])
        xss = sb("xss", [KP, GT])
        wr = sb("wr", [KP, KT, SHIFTS, D])
        gb = sb("gb", [KP, 2, KT, SHIFTS])
        wg = sb("wg", [KP, 2, SHIFTS, D])
        wf = sb("wf", [KP, KT, D + 1])
        ones = sb("ones", [P, P])
        gsum = sb("gsum", [P, D])
        brow = sb("brow", [P, D])
        brow0 = sb("brow0", [P, D])
        xst = sb("xst", [P, 2, 4, 2])
        hm = sb("hm", [P, 2, D])
        ho = sb("ho", [P, 2, 2, D])
        mhalf = sb("mhalf", [P, 2])

        hx = sb("hx", [P, 2, 2, D])
        rec = sb("rec", [P, 2, 2, REC])
        wstage = sb("wstage", [P, 3, NW])
        wst = sb("wst", [P, 4, NW], F16)
        st = {n: sb(n, [P, 2, 2, 256], F16) for n in ("s1", "s2", "s3")}
        tt = {n: sb(n, [P, 4, 256], F16) for n in ("t1", "t2", "t3")}
        trih = sb("trih", [P, P], F16)
        mvs = sb("mvs", [P, 2, 2, 6])
        mv = sb("mv", [P, 2, 2, 2])
        mve = sb("mve", [P, 2, 2])
        rstd1 = sb("rstd1", [P, 2])
        hn = sb("hn", [P, 2, D])
        xn = sb("xn", [P, 2, D])
        cn = sb("cn", [P, 2, D])
        rc = sb("rc", [P, 2, HEADS])
        ra = sb("ra", [P, 2, 2 * D])
        rb = sb("rb", [P, 2, 2 * D])
        qk = sb("qk", [P, 2, 2 * D])
        qks = sb("qks", [P, 2, 2, 2 * HEADS, 4, HD], F16)
        kms = sb("kms", [P, 2, 6, 2, 256], F16)
        qt = sb("qt", [P, 6, 256], F16)
        q2t = sb("q2t", [P, 6, 256], F16)
        va = sb("va", [P, 2, 2, HEADS, 32])
        pt = sb("pt", [P, 2, HEADS, TOK])
        ctxt = sb("ctxt", [P, 3, 256])
        mx = sb("mx", [P, 2, HEADS])
        lmx = sb("lmx", [P, 2])
        ld = sb("ld", [P, 2, EXPERTS])
        le = sb("le", [P, 2, EXPERTS])
        lsum = sb("lsum", [P, 2])
        c8 = sb("c8", [P, 2, EXPERTS])
        code = sb("code", [P, 2, 2])
        oh = sb("oh", [P, 2, 2, EXPERTS], F16)
        cum = sb("cum", [P, 2, 2, EXPERTS], F16)
        sl = sb("sl", [P, 2, EXPERTS])
        sl2 = sb("sl2", [P, 2, EXPERTS])
        slot = sb("slot", [P, 2])
        idx = sb("idx", [P, 2, 2], U32)
        tokn = sb("tokn", [P, 2])
        records = nc.dram_tensor("records", (DUMMY + P, REC), F32).ap()
        pflat = nc.dram_tensor("pflat", (2, IMAGES, TOK), F32).ap()
        half6 = ps[:, 6, :].bitcast(F16).rearrange("p (s c) -> p s c", c=256)
        half7 = ps[:, 7, :].bitcast(F16).rearrange("p (s c) -> p s c", c=256)

        early.close()
        area = ctx

        c3 = sb("c3", [P, N_CONST3])
        onef = sb("onef", [P, P])
        prow = sb("prow", [IMAGES, 2, TOK])
        eb = sb("eb", [P, 2, CHUNK])
        pe_e = sb("pe_e", [P, CHUNK])
        scr = sb("scr", [P, CHUNK])
        tie = sb("tie", [P, CHUNK])
        tied = sb("tied", [P, CHUNK])
        one788 = sb("one788", [P, CHUNK])
        cols = {n: sb(n, [P, 1]) for n in ("cnt", "n_e", "ntile", "end", "start", "vrow", "lo", "stepc", "cand", "took", "room", "lim", "cutc")}
        dn = sb("dn", [P, EXPERTS])
        tails = sb("tails", [P, EXPERTS], U32)
        padrec = sb("padrec", [P, REC])
        ended = sb("ended", [P, P])
        sel = sb("sel", [P, P])
        vals = sb("vals", [P, 4, TILES])
        rowt = sb("rowt", [P, TILES], U32)
        expt = sb("expt", [P, TILES], U32)
        tct = sb("tct", [P, 2, TILES])
        f1 = sb("f1", [P, 2, 3, FF])
        f2 = sb("f2", [P, 2, FT, D])
        fb2 = sb("fb2", [P, EXPERTS, D])
        w1s = sb("w1s", [P, EXPERTS, 4 * FF], F16)
        w2s = sb("w2s", [P, EXPERTS, FT * 2 * D], F16)
        b2s = sb("b2s", [P, EXPERTS, D], F16)
        xr = sb("xr", [P, 4, REC])
        xn4 = sb("xn4", [P, 2, D])
        st4 = sb("st4", [P, 2, 2, 256], F16)
        xt4 = sb("xt4", [P, 2, 4, P], F16)
        hf = sb("hf", [P, 2, FF])
        hh = sb("hh", [P, 2, FF], F16)
        hl = sb("hl", [P, 2, FF], F16)
        small = sb("small", [P, 2, 8])
        keepp = sb("keepp", [P, 4, 2])
        base = sb("base", [P, 4, D])
        orow = sb("orow", [P, 2, D])

        block = ctx.enter_context(nc.Block())

        def run_images(eng, step):
            for s in range(3):
                step(s, s % 2, s // 2)
            with eng.Fori(0, (IMAGES - 4) // 2) as i:
                step(2 * i + 3, 1, i + 1)
                step(2 * i + 4, 0, i + 2)
            for s in range(IMAGES - 1, IMAGES + 1):
                step(s, s % 2, s // 2)

        def carried(eng):
            eng.sem_inc(S["carried"], 1)

        def front(s):
            return not isinstance(s, int) or s < IMAGES

        def back(s):
            return not isinstance(s, int) or s > 0

        def groups(eng, body):
            for g in range(3):
                body(g, g % 2, g // 2)
            with eng.Fori(0, (GROUPS - 3) // 2) as i:
                body(2 * i + 3, 1, i + 1)
                body(2 * i + 4, 0, i + 2)

        @block.sync
        def _(sp):
            sp.dma_start(wr[:, :, :, :], wraw).then_inc(S["w_in"], 16)
            sp.dma_start(gb[:, 0, :, :], graw).then_inc(S["g_in"], 16)
            sp.dma_start(gb[:, 1, :, :], braw).then_inc(S["b_in"], 16)
            sp.dma_start(cst[:, :], consts).then_inc(S["c_in"], 16)
            sp.dma_start(brow0[:, :], tokb.partition_broadcast(P)).then_inc(S["tb_in"], 16)

            def load(g, p, half):
                wait(sp, S["acc"], 2 * (g - 1))
                wait(sp, S["sq"], g - 1)
                sp.dma_start(xb[:, p, :, :], xt[bass.ds(g, 1), :, :, :].rearrange("g p k t -> (g p) k t")).then_inc(S[f"x_in{p}"], 16)
            groups(sp, load)
            sp.wait_ge(S["wz"], 1)
            for c, n, w, b in ((0, 3 * D, wqkv, bqkv), (W_OUT, D, wout, bout), (W_SW, EXPERTS, wsw, bsw)):
                sp.dma_start(wstage[:, 0, c:c + n], w[0:P, :]).then_inc(S["ws_in"], 16)
                for r in (0, 64):
                    sp.dma_start(wstage[r:r + 64, 1, c:c + n], w[P:D, :]).then_inc(S["ws_in"], 16)
                for r in (64, 96):
                    sp.dma_start(wstage[r:r + 1, 2, c:c + n], b.rearrange("(a n) -> a n", a=1)).then_inc(S["ws_in"], 16)
            sp.wait_ge(S["mem"], 1)
            for q in range(2):
                sp.dma_start(hx[REST:REST + 1, q, 1, :], cls).then_inc(S["cls_in"], 16)
            sp.wait_ge(S["hp_out0"], 16 * ((GROUPS + 1) // 2))
            sp.wait_ge(S["hp_out1"], 16 * (GROUPS // 2))

            def image_in(s, p, half):
                if front(s):
                    wait(sp, S["h2"], s - 1)
                    sp.dma_start(hx[:, p, 0, :], hp[bass.ds(PATCHES * s, P), :]).then_inc(S[f"h_in{p}"], 16)
                    sp.dma_start(hx[0:REST, p, 1, :], hp[bass.ds(PATCHES * s + P, REST), :]).then_inc(S[f"h_in{p}"], 16)
            run_images(sp, image_in)

        @block.gpsimd
        def _(pool):
            pool.memset(mhalf[:, :], -0.5).then_inc(S["mhalf"], 1)
            pool.wait_ge(S["mhalf"], 1)

            def power(g, p, half):
                pool.wait_ge(S["var"], g + 1)
                pool.tensor_tensor(xst[:, p, 3, :], xst[:, p, 2, :], mhalf[:, :], ALU.pow).then_inc(S["rstd"], 1)
            for a in (hx, qks, kms, qt, va, *st.values(), *tt.values(), cum):
                pool.memset(a.ap() if hasattr(a, "ap") and callable(a.ap) else a, 0.0).then_inc(S["zero"], 1)
            pool.wait_ge(S["zero"], 12)
            for a in st.values():
                pool.memset(a[:, :, 0, D:256:32], 1.0).then_inc(S["one"], 1)
            pool.memset(qks[:, :, :, HEADS:, 3, 0:2].rearrange("p a t h r -> p (a t) h r"), 1.0).then_inc(S["one"], 1)
            pool.memset(va[:, :, :, :, HD:HD + 1].rearrange("p a t h r -> p (a t) h r"), 1.0).then_inc(S["one"], 1)
            pool.memset(ctxt[:, :, :], 1.0).then_inc(S["one"], 1)
            pool.memset(oneh[:, :], 1.0).then_inc(S["one"], 1)
            pool.wait_ge(S["c_in"], 16)
            pool.tensor_copy(tokn[:, :], cst[:, C_TOKN:C_TOKN + 2]).then_inc(S["one"], 1)
            pool.wait_ge(S["one"], 8)
            pool.drain().then_inc(S["mem"], 1)
            groups(pool, power)
            pool.wait_ge(S["wst"], 6)

            def step(s, p, half):
                k, kp, kh = s - 1, 1 - p, (half if p else half - 1)
                if front(s):
                    pool.wait_ge(S["ln1_var"], s + 1)
                    pool.tensor_tensor(rstd1[:, :], mve[:, 0, :], mhalf[:, :], ALU.pow).then_inc(S["ln1_rstd"], 1)
                    wait(pool, S["q2_ps"], 2 * (s - 1))
                    carried(pool)
                    pool.memset(qks[:, p, :, 0:HEADS, 3, 0:2], 0.0).then_inc(S["m_zero"], 1)
                    for t in range(2):
                        pool.wait_ge(S["qk_hi"], 2 * s + t + 1)
                        src = qk[:, t, :].rearrange("p (w h r) -> p w h r", w=2, r=HD)
                        both = qks[:, p, t, :, :, :].rearrange("p (w h) s r -> p w (h s r)", w=2)
                        hi = qks[:, p, t, :, 0, :].rearrange("p (w h) r -> p w h r", w=2)
                        for w in range(2):
                            pool.tensor_tensor(qks[:, p, t, HEADS * w:HEADS * (w + 1), 1 + w, :], src[:, w, :, :], hi[:, w, :, :],
                                               ALU.subtract).then_inc(S["qk_lo"], 1)
                if back(s):
                    wait(pool, S[f"sc_done{kp}"], 32 * kh)
                    carried(pool)
                    pool.tensor_copy(rec[:, kp, :, REC - 1].bitcast(U32), tokn[:, :]).then_inc(S["tok"], 1)
                    pool.wait_ge(S["tok"], 2 * k + 1)
                    carried(pool)
                    pool.tensor_scalar(tokn[:, :], tokn[:, :], float(TOK), None, ALU.add).then_inc(S["tok"], 1)
                    pool.wait_ge(S["ln2_var"], s)
                    pool.tensor_tensor(rec[:, kp, :, D + 1], mve[:, 1, :], mhalf[:, :], ALU.pow).then_inc(S["ln2_rstd"], 1)
                    pool.tensor_copy(rec[:, kp, :, D], mv[:, 1, :, 0]).then_inc(S["rec_m"], 1)
                    pool.wait_ge(S["prob"], s)
                    carried(pool)
                    pool.tensor_copy(pall[:, 0, :, bass.ds(k, 1)], rec[:, kp, :, D + 2:D + 3]).then_inc(S["pall"], 1)
                    pool.wait_ge(S["onehot"], s)
                    carried(pool)
                    pool.tensor_copy(pall[:, 1, :, bass.ds(k, 1)], code[:, 1, :].unsqueeze(2)).then_inc(S["pall"], 1)
                    wait(pool, S["prefix"], k)
                    pool.tensor_tensor(cum[:, kp, 1, :], cum[:, kp, 0, :], oh[:, kp, 0, :], ALU.add).then_inc(S["cum"], 1)
                    pool.wait_ge(S["cum"], 2 * k + 1)
                    pool.tensor_tensor(cum[:, 1 - kp, 0, :], cum[:, kp, 1, :], oh[:, kp, 1, :], ALU.add).then_inc(S["cum"], 1)
                    pool.wait_ge(S["slot"], s)
                    pool.wait_ge(S["tok"], 2 * k + 1)
                    pool.wait_ge(S["rec_m"], s)
                    pool.wait_ge(S["ln2_rstd"], s)
                    carried(pool)
                    for t in range(2):
                        pool.indirect_dma_start(records, bass.IndirectOffsetOnAxis(ap=idx[:, kp, t:t + 1], axis=0), rec[:, kp, t, :],
                                                None, bounds_check=EXPERTS * REGION - 1, oob_is_err=False).then_inc(S[f"sc_done{kp}"], 16)
            run_images(pool, step)

        @block.scalar
        def _(act):
            def store(g, p, half):
                act.wait_ge(S["ho"], 2 * (g + 1))
                act.dma_start(hp[bass.ds(GT * g, GT), :].rearrange("(t p) d -> p t d", p=P), ho[:, p, :, :]).then_inc(S[f"hp_out{p}"], 16)

            def square(g, p, half):
                act.wait_ge(S[f"x_in{p}"], 16 * (half + 1))
                wait(act, S["sqs"], g)
                act.activation(xsq[:, :, :], xb[:, p, :, :], ACT.Square).then_inc(S["sq"], 1)
                if not (isinstance(g, int) and g == 0):
                    store(g - 1, 1 - p, None)
            groups(act, square)
            store(GROUPS - 1, (GROUPS - 1) % 2, None)
            act.wait_ge(S["mem"], 1)

            def high(name, src):
                act.activation(st[name][:, :, 0, 0:D], src[:, :, :], ACT.Copy).then_inc(S[name + "_hi"], 1)
                act.activation(st[name][:, :, 1, D:256], src[:, :, P:D], ACT.Copy).then_inc(S[name + "_hi"], 1)

            def turned(name, half):
                act.activation(tt[name][:, :, 0:TOK], half[:, :, 0:TOK], ACT.Copy).then_inc(S[name + "_cp"], 1)

            def step(s, p, half):
                k, kp = s - 1, 1 - p
                f, b = front(s), back(s)

                def exps(u):
                    act.wait_ge(S["st_ps"], 6 * k + u + 1)
                    wait(act, S["ctx_ps"], 3 * (k - 1) + u // 2 + 1)
                    g, kt = u // 2, u % 2
                    act.activation(pt[:, kt, 4 * g:4 * g + 4, :].rearrange("p (a c) n -> p a (c n)", a=2),
                                   ps[:, 2:4, 0:2 * TOK], ACT.Exp, scale=HD ** -0.5).then_inc(S["exp"], 1)

                def context(g):
                    act.wait_ge(S["ctx_ps"], 3 * k + g + 1)
                    wait(act, S["ct_ps"], 2 * k)
                    act.activation(ctxt[:, g, 0:TOK], ps[:, 5, 0:TOK], ACT.Copy).then_inc(S["ctx_cp"], 1)

                def keys(u):
                    act.wait_ge(S["k_ps"], 2 * s + u + 1)
                    wait(act, S["st_ps"], 6 * (s - 1))
                    act.activation(kms[0:64, p, 3 * u:3 * u + 3, 0, 0:TOK], half6[0:64, 0:3, 0:TOK], ACT.Copy).then_inc(S["k_cpa"], 1)

                if f:
                    act.wait_ge(S["ln1_hn"], 2 * (s + 1))
                    wait(act, S["t1_ps"], s)
                    high("s1", hn)
                    act.wait_ge(S["t1_ps"], s + 1)
                    wait(act, S["v_ps"], s)
                    turned("t1", half6)
                if b:
                    exps(0)
                if f:
                    act.wait_ge(S["v_ps"], s + 1)
                    wait(act, S["ctx_ps"], 3 * (s - 1))
                    act.activation(va[:, p, :, :, 0:HD], ps[:, 5, 0:2 * D].rearrange("p (t h r) -> p t h r", t=2, r=HD),
                                   ACT.Copy).then_inc(S["v_cp"], 1)
                if b:
                    exps(1)
                if f:
                    wait(act, S["q2_ps"], 2 * (s - 1))
                    for t in range(2):
                        act.wait_ge(S["rope"], 2 * s + t + 1)
                        act.activation(qks[:, p, t, :, 0, :], qk[:, t, :].rearrange("p (h r) -> p h r", r=HD), ACT.Copy).then_inc(S["qk_hi"], 1)
                    for t in range(2):
                        for w in range(2):
                            act.activation(qks[:, p, t, HEADS * w:HEADS * (w + 1), 2 - w, :],
                                           qk[:, t, D * w:D * (w + 1)].rearrange("p (h r) -> p h r", r=HD), ACT.Copy).then_inc(S["qk_hi2"], 1)
                if b:
                    context(0)
                if f:
                    keys(0)
                if b:
                    exps(2)
                if f:
                    keys(1)
                if b:
                    exps(3)
                    context(1)
                    exps(4)
                    exps(5)
                    context(2)
                    act.wait_ge(S["cn"], 2 * s)
                    wait(act, S["t2_ps"], k)
                    high("s2", cn)
                    act.wait_ge(S["t2_ps"], s)
                    wait(act, S["wo_ps"], k)
                    turned("t2", half7)
                    act.wait_ge(S["xn"], 2 * s)
                    wait(act, S["t3_ps"], k)
                    high("s3", xn)
                    act.wait_ge(S["t3_ps"], s)
                    wait(act, S["lg_ps"], k)
                    turned("t3", half7)
                    act.wait_ge(S["ld"], s)
                    act.activation(le[:, :, :], ld[:, :, :], ACT.Exp).then_inc(S["le"], 1)
            run_images(act, step)

        @block.tensor
        def _(pe):
            pe.wait_ge(S["w_in"], 16)
            pe.wait_ge(S["b_in"], 16)
            n = KT * SHIFTS
            for k in range(n):
                last = pe.matmul(ps[:, 6, 0:D], gb[:, 1, k // SHIFTS, k % SHIFTS:k % SHIFTS + 1].broadcast_to([KP, P]),
                                 wr[:, k // SHIFTS, k % SHIFTS, :], start=(k == 0), stop=(k == n - 1))
            last.then_inc(S["bw"], 1)
            pe.wait_ge(S["wf"], KT)
            pe.wait_ge(S["ones"], 2)
            pe.wait_ge(S["c_in"], 16)
            for k in range(KT):
                last = pe.matmul(ps[:, 7, 0:D], ones[0:KP, :], wf[:, k, 0:D], start=(k == 0), stop=(k == KT - 1))
            last.then_inc(S["gs"], 1)

            def product(g, p, half):
                pe.wait_ge(S[f"x_in{p}"], 16 * (half + 1))
                wait(pe, S["ho"], 2 * (g - 1))
                for t in range(2):
                    for k in range(KT):
                        pe.matmul(ps[:, 2 * p + t, 0:D + 1], xb[:, p, k, t * P:(t + 1) * P], wf[:, k, :],
                                  start=(k == 0), stop=(k == KT - 1))
                    if t == 0:
                        pe.wait_ge(S["sqs"], g + 1)
                    pe.matmul(ps[:, 2 * p + t, D + 1:D + 2], xss[:, t * P:(t + 1) * P], cst[0:KP, C_MULT:C_MULT + 1],
                              start=True, stop=True).then_inc(S["acc"], 1)
            groups(pe, product)
            pe.wait_ge(S["mem"], 1)
            pe.wait_ge(S["wst"], 9)
            pe.wait_ge(S["ho"], 2 * GROUPS)

            def turn(name, half):
                a = st[name]
                for t in range(2):
                    for c, src in enumerate((a[:, t, 0, 0:P], a[:, t, 1, 0:P], a[:, t, 1, P:256], a[:, t, 0, P:256])):
                        last = pe.transpose(half[:, c, t * P:(t + 1) * P], src, idh[:, :])
                return last

            def stacked(o, x, t, c, n):
                for i, (a, w) in enumerate(((0, 0), (0, 1), (1, 0), (2, 2), (3, 3))):
                    last = pe.matmul(o, tt[x][:, a, t * P:(t + 1) * P], wst[:, w, c:c + n], start=(i == 0), stop=(i == 4))
                return last

            def pairs(s, p, w, u, half):
                for i in range(3):
                    h = HEADS * w + 2 * (3 * u + i)
                    for t in range(2):
                        last = pe.transpose(half[:, i, t * P:(t + 1) * P], qks[:, p, t, h:h + 2, :, :].rearrange("p h s r -> p (h s r)"), idh[:, :])
                return last

            def step(s, p, half):
                k, kp = s - 1, 1 - p
                f, b = front(s), back(s)

                def queries2(u):
                    pe.wait_ge(S["m_lo"], s)
                    if u == 0:
                        wait(pe, S["t3_cp"], k)
                    else:
                        pe.wait_ge(S["q2_cp"], 2 * k + 1)
                    pairs(k, kp, 0, u, half7).then_inc(S["q2_ps"], 1)

                def scores_t(u):
                    g, kt = u // 2, u % 2
                    pe.wait_ge(S["q2_cp"], 2 * k + (1 if g < 1 else 2))
                    wait(pe, S["exp"], 6 * k + u)
                    for c in range(4):
                        h = 4 * g + c
                        last = pe.matmul(ps[:, 2 + c // 2, (c % 2) * TOK:(c % 2 + 1) * TOK], kms[:, kp, h // 2, h % 2, kt * P:(kt + 1) * P],
                                         q2t[:, h // 2, 0:TOK], start=True, stop=True)
                    last.then_inc(S["st_ps"], 1)

                def weighted(g):
                    pe.wait_ge(S["exp"], 6 * k + 2 * g + 2)
                    if g == 0:
                        pe.wait_ge(S["v_cp"], s + 1 if f else s)
                    else:
                        pe.wait_ge(S["ctx_cp"], 3 * k + g)
                    for kt in range(2):
                        n = P if kt == 0 else TOK - P
                        for c in range(4):
                            last = pe.matmul(ps[32 * c:32 * c + 32, 5, 0:TOK], va[0:n, kp, kt, 4 * g + c, :], pt[0:n, kt, 4 * g + c, :],
                                             start=(kt == 0), stop=(kt == 1), tile_position=(0, 32 * c))
                    last.then_inc(S["ctx_ps"], 1)

                def project(t):
                    pe.wait_ge(S["t1_cp"], s + 1)
                    wait(pe, S["rope_b"], 2 * s + t)
                    stacked(ps[:, 4, 0:2 * D], "t1", t, 0, 2 * D).then_inc(S["qk_ps"], 1)

                def maxima(u):
                    q, g = u // 3, u % 3
                    pe.wait_ge(S["q_cp"], 2 * (s + 1))
                    pe.wait_ge(S["k_cpa"], 2 * (s + 1))
                    pe.wait_ge(S["k_cpd"], 2 * (s + 1))
                    wait(pe, S["s_max"], 6 * s + u)
                    for c in range(2):
                        last = pe.matmul(ps[:, c, 0:2 * TOK], qt[:, 2 * g + c, q * P:(q + 1) * P], kms[:, p, 2 * g + c, :, 0:TOK], start=True, stop=True)
                    last.then_inc(S["s_ps"], 1)

                if b:
                    queries2(0)
                if f:
                    pe.wait_ge(S["s1_lo"], s + 1)
                    wait(pe, S["q_cp"], 2 * s)
                    turn("s1", half6).then_inc(S["t1_ps"], 1)
                if b:
                    queries2(1)
                if f:
                    project(0)
                if b:
                    scores_t(0)
                if f:
                    project(1)
                    wait(pe, S["v_cp"], s)
                    wait(pe, S["slot_a"], s - 1)
                    for t in range(2):
                        last = stacked(ps[:, 5, t * D:(t + 1) * D], "t1", t, 2 * D, D)
                    last.then_inc(S["v_ps"], 1)
                if b:
                    scores_t(1)
                    if not f:
                        pe.wait_ge(S["slot_a"], s - 1)
                    weighted(0)
                if f:
                    pe.wait_ge(S["qk_lo"], 4 * (s + 1))
                    pe.wait_ge(S["qk_hi2"], 4 * (s + 1))
                    pe.wait_ge(S["m_zero"], s + 1)
                    pe.wait_ge(S["t1_cp"], s + 1)
                    pairs(s, p, 1, 0, half6).then_inc(S["k_ps"], 1)
                if b:
                    scores_t(2)
                if f:
                    pe.wait_ge(S["k_cpa"], 2 * s + 1)
                    pe.wait_ge(S["k_cpd"], 2 * s + 1)
                    pairs(s, p, 1, 1, half6).then_inc(S["k_ps"], 1)
                if b:
                    scores_t(3)
                    weighted(1)
                if f:
                    pe.wait_ge(S["k_cpa"], 2 * s + 2)
                    pe.wait_ge(S["k_cpd"], 2 * s + 2)
                    pairs(s, p, 0, 0, half6).then_inc(S["q_ps"], 1)
                if b:
                    scores_t(4)
                if f:
                    pe.wait_ge(S["q_cp"], 2 * s + 1)
                    pairs(s, p, 0, 1, half6).then_inc(S["q_ps"], 1)
                if b:
                    scores_t(5)
                    weighted(2)
                for u in range(6):
                    if b and u < 2:
                        pe.wait_ge(S["ctx_cp"], 3 * s)
                        if u == 1:
                            pe.wait_ge(S["cn"], 2 * k + 1)
                        for g in range(3):
                            last = pe.transpose(ps[:, 5, g * P:(g + 1) * P], ctxt[:, g, u * P:(u + 1) * P], ident)
                        last.then_inc(S["ct_ps"], 1)
                    if f:
                        maxima(u)
                    if b and u == 2:
                        pe.wait_ge(S["s2_lo"], s)
                        pe.wait_ge(S["q2_cp"], 2 * s)
                        turn("s2", half7).then_inc(S["t2_ps"], 1)
                    if b and u == 3:
                        pe.wait_ge(S["t2_cp"], s)
                        pe.wait_ge(S["cn"], 2 * s)
                        for t in range(2):
                            last = stacked(ps[:, 5, t * D:(t + 1) * D], "t2", t, W_OUT, D)
                        last.then_inc(S["wo_ps"], 1)
                if b:
                    pe.wait_ge(S["s3_lo"], s)
                    pe.wait_ge(S["t2_cp"], s)
                    turn("s3", half7).then_inc(S["t3_ps"], 1)
                    pe.wait_ge(S["t3_cp"], s)
                    pe.wait_ge(S["h2"], s)
                    for t in range(2):
                        last = stacked(ps[:, 5, t * EXPERTS:(t + 1) * EXPERTS], "t3", t, W_SW, EXPERTS)
                    last.then_inc(S["lg_ps"], 1)
                    pe.wait_ge(S["onehot"], s)
                    pe.wait_ge(S["ld"], s)
                    pe.wait_ge(S["cum"], 2 * k + 1)
                    for t in range(2):
                        pe.matmul(ps[:, 5, 256 + t * EXPERTS:256 + (t + 1) * EXPERTS], trih[:, :], oh[:, kp, t, :], start=True, stop=False)
                        last = pe.matmul(ps[:, 5, 256 + t * EXPERTS:256 + (t + 1) * EXPERTS], oneh[:, :], cum[:, kp, t, :], start=False, stop=True)
                    last.then_inc(S["prefix"], 1)
            run_images(pe, step)

        @block.vector
        def _(dve):
            dve.memset(ones[:, :], 1.0).then_inc(S["ones"], 1)
            dve.wait_ge(S["w_in"], 16)
            dve.wait_ge(S["g_in"], 16)
            for k in range(KT):
                wait(dve, S["wf"], k - 1)
                dve.tensor_tensor(wg[:, k % 2, :, :], wr[:, k, :, :], gb[:, 0, k, :].unsqueeze(2).broadcast_to([KP, SHIFTS, D]),
                                  ALU.mult).then_inc(S["wg"], 1)
                dve.wait_ge(S["wg"], k + 1)
                dve.tensor_reduce(wf[:, k, 0:D], wg[:, k % 2, :, :].rearrange("p s d -> p d s"), AX.X, ALU.add).then_inc(S["wf"], 1)
            dve.wait_ge(S["c_in"], 16)
            dve.tensor_copy(wf[:, :, D], cst[0:KP, C_MULT:C_MULT + 1].broadcast_to([KP, KT])).then_inc(S["ones"], 1)
            dve.wait_ge(S["bw"], 1)
            dve.wait_ge(S["tb_in"], 16)
            dve.tensor_tensor(brow[:, :], ps[:, 6, 0:D], brow0[:, :], ALU.add).then_inc(S["rows"], 1)
            dve.wait_ge(S["gs"], 1)
            dve.tensor_copy(gsum[:, :], ps[:, 7, 0:D]).then_inc(S["rows"], 1)
            dve.wait_ge(S["rows"], 2)

            def sums(g, p, half):
                dve.wait_ge(S["sq"], g + 1)
                wait(dve, S["acc"], 2 * g)
                dve.tensor_reduce(xss[:, :], xsq[:, :, :].rearrange("p k t -> p t k"), AX.X, ALU.add).then_inc(S["sqs"], 1)

            def finish(g, p, half):
                acc = ps[:, 2 * p:2 * p + 2, :]
                dve.wait_ge(S["acc"], 2 * (g + 1))
                dve.tensor_scalar(xst[:, p, 0, :], acc[:, :, D], -1.0 / TERMS, None, ALU.mult).then_inc(S["stat"], 1)
                dve.tensor_scalar(xst[:, p, 1, :], acc[:, :, D + 1], 1.0 / TERMS, None, ALU.mult).then_inc(S["stat"], 1)
                dve.wait_ge(S["stat"], 3 * g + 2)
                dve.tensor_tensor(xst[:, p, 2, :], xst[:, p, 0, :], xst[:, p, 0, :], ALU.mult).then_inc(S["stat"], 1)
                dve.wait_ge(S["stat"], 3 * g + 3)
                dve.scalar_tensor_tensor(out=xst[:, p, 2, :], in0=xst[:, p, 1, :], scalar=EPS, in1=xst[:, p, 2, :],
                                         op0=ALU.add, op1=ALU.subtract).then_inc(S["var"], 1)
                for t in range(2):
                    dve.scalar_tensor_tensor(out=hm[:, t, :], in0=gsum[:, :], scalar=xst[:, p, 0, t:t + 1], in1=acc[:, t, 0:D],
                                             op0=ALU.mult, op1=ALU.add).then_inc(S["hm"], 1)
                dve.wait_ge(S["rstd"], g + 1)
                wait(dve, S[f"hp_out{p}"], 16 * half)
                for t in range(2):
                    dve.wait_ge(S["hm"], 2 * g + t + 1)
                    dve.scalar_tensor_tensor(out=ho[:, p, t, :], in0=hm[:, t, :], scalar=xst[:, p, 3, t:t + 1], in1=brow[:, :],
                                             op0=ALU.mult, op1=ALU.add).then_inc(S["ho"], 1)

            def step(g, p, half):
                sums(g, p, half)
                if not (isinstance(g, int) and g == 0):
                    finish(g - 1, 1 - p, half - 1 if p == 0 else half)
            groups(dve, step)
            finish(GROUPS - 1, 0, GROUPS // 2)

            dve.memset(wstage[:, 2, :], 0.0).then_inc(S["wz"], 1)
            dve.tensor_copy(idh[:, :], ident).then_inc(S["wst"], 1)
            dve.tensor_copy(trih[:, :], cst[:, C_TRI:C_TRI + P]).then_inc(S["wst"], 1)
            dve.wait_ge(S["ws_in"], 16 * 15)
            dve.tensor_copy(wst[:, 0, :], wstage[:, 0, :]).then_inc(S["wst"], 1)
            dve.tensor_copy(wst[:, 2, :], wstage[:, 1, :]).then_inc(S["wst"], 1)
            dve.tensor_copy(wst[64:P, 3, :], wstage[64:P, 2, :]).then_inc(S["wst"], 1)
            dve.wait_ge(S["wst"], 5)
            dve.tensor_tensor(wst[:, 1, :], wstage[:, 0, :], wst[:, 0, :], ALU.subtract).then_inc(S["wst"], 1)
            dve.tensor_tensor(wst[0:64, 3, :], wstage[0:64, 1, :], wst[0:64, 2, :], ALU.subtract).then_inc(S["wst"], 1)
            dve.tensor_tensor(wst[96:P, 3, :], wstage[96:P, 2, :], wst[96:P, 3, :], ALU.subtract).then_inc(S["wst"], 1)
            dve.wait_ge(S["mem"], 1)
            dve.wait_ge(S["cls_in"], 32)
            dve.wait_ge(S["wst"], 8)
            dve.tensor_copy(code[:, 0, :], cst[:, C_VALID:C_VALID + 2]).then_inc(S["wst"], 1)

            def low(name, src):
                dve.tensor_tensor(st[name][:, :, 1, 0:D], src[:, :, :], st[name][:, :, 0, 0:D], ALU.subtract).then_inc(S[name + "_lo"], 1)

            def stats(x, i, n, name):
                for t in range(2):
                    dve.bn_stats(mvs[:, i, t, :], x(t)).then_inc(S[name + "_st"], 1)
                dve.wait_ge(S[name + "_st"], 2 * n)
                carried(dve)
                for t in range(2):
                    dve.bn_aggr(mv[:, i, t, :], mvs[:, i, t, :]).then_inc(S[name + "_mv"], 1)
                dve.wait_ge(S[name + "_mv"], 2 * n)
                dve.tensor_scalar(mve[:, i, :], mv[:, i, :, 1], EPS, None, ALU.add).then_inc(S[name + "_var"], 1)

            def step(s, p, half):
                k, kp, kh = s - 1, 1 - p, (half if p else half - 1)
                f, b = front(s), back(s)

                def queries(u, second):
                    n, sem, dst = (k, "q2", q2t) if second else (s, "q", qt)
                    dve.wait_ge(S[sem + "_ps"], 2 * n + u + 1)
                    wait(dve, S["st_ps" if second else "s_ps"], 6 * n)
                    dve.tensor_copy(dst[:, 3 * u:3 * u + 3, 0:TOK], (half7 if second else half6)[:, 0:3, 0:TOK]).then_inc(S[sem + "_cp"], 1)

                def largest(u):
                    q, g = u // 3, u % 3
                    dve.wait_ge(S["s_ps"], 6 * s + u + 1)
                    dve.tensor_reduce(mx[:, q, 4 * g:4 * g + 4].rearrange("p (a b) -> p a b", a=2),
                                      ps[:, 0:2, 0:2 * TOK].rearrange("p a (b n) -> p a b n", b=2), AX.X, ALU.max).then_inc(S["s_max"], 1)

                if f:
                    dve.wait_ge(S[f"h_in{p}"], 32 * (half + 1))
                    stats(lambda t: hx[:, p, t, :], 0, s + 1, "ln1")
                if b:
                    queries(0, True)
                if f:
                    dve.wait_ge(S["ln1_rstd"], s + 1)
                    for t in range(2):
                        dve.tensor_scalar(hn[:, t, :], hx[:, p, t, :], mv[:, 0, t, 0:1], rstd1[:, t:t + 1], ALU.subtract, ALU.mult).then_inc(S["ln1_hn"], 1)
                    dve.wait_ge(S["ln1_hn"], 2 * (s + 1))
                    dve.wait_ge(S["s1_hi"], 2 * (s + 1))
                    low("s1", hn)
                if b:
                    queries(1, True)
                if f:
                    for t in range(2):
                        dve.wait_ge(S["qk_ps"], 2 * s + t + 1)
                        dve.tensor_tensor(ra[:, t, :], ps[:, 4, 0:2 * D], cst[:, C_COS + t * 2 * D:C_COS + (t + 1) * 2 * D], ALU.mult).then_inc(S["rope_a"], 1)
                        dve.tensor_tensor(rb[:, t, :].rearrange("p (a b) -> p a b", b=2),
                                          ps[:, 4, 0:2 * D].rearrange("p (a b) -> p a b", b=2)[:, :, ::-1],
                                          cst[:, C_SIN + t * 2 * D:C_SIN + (t + 1) * 2 * D].rearrange("p (a b) -> p a b", b=2), ALU.mult).then_inc(S["rope_b"], 1)
                        dve.wait_ge(S["rope_a"], 2 * s + t + 1)
                        dve.wait_ge(S["rope_b"], 2 * s + t + 1)
                        wait(dve, S["qk_lo"], 4 * s)
                        wait(dve, S["qk_hi2"], 4 * s)
                        dve.tensor_tensor(qk[:, t, :], ra[:, t, :], rb[:, t, :], ALU.add).then_inc(S["rope"], 1)
                    for u in range(2):
                        dve.wait_ge(S["k_ps"], 2 * s + u + 1)
                        wait(dve, S["st_ps"], 6 * (s - 1))
                        dve.tensor_copy(kms[64:P, p, 3 * u:3 * u + 3, 1, 0:TOK], half6[64:P, 0:3, 0:TOK]).then_inc(S["k_cpd"], 1)
                    for u in range(2):
                        queries(u, False)
                for u in range(6):
                    if b and u < 2:
                        tok = ps[:, 5, 0:3 * P].rearrange("p (h r) -> p h r", r=32)
                        dve.wait_ge(S["ct_ps"], 2 * k + u + 1)
                        dve.reciprocal(rc[:, u, :], tok[:, :, HD]).then_inc(S["den"], 1)
                        dve.wait_ge(S["den"], 2 * k + u + 1)
                        wait(dve, S["s2_hi"], 2 * k)
                        wait(dve, S["s2_lo"], k)
                        dve.tensor_tensor(cn[:, u, :].rearrange("p (h r) -> p h r", r=HD), tok[:, :, 0:HD],
                                          rc[:, u, :].unsqueeze(2).broadcast_to([P, HEADS, HD]), ALU.mult).then_inc(S["cn"], 1)
                    if b and u == 2:
                        dve.wait_ge(S["s2_hi"], 2 * s)
                        dve.wait_ge(S["cn"], 2 * s)
                        low("s2", cn)
                    if b and u == 4:
                        dve.wait_ge(S["wo_ps"], s)
                        wait(dve, S[f"sc_done{kp}"], 32 * kh)
                        dve.tensor_tensor(rec[:, kp, :, 0:D], ps[:, 5, 0:2 * D].rearrange("p (t d) -> p t d", t=2), hx[:, kp, :, :], ALU.add).then_inc(S["h2"], 1)
                        dve.wait_ge(S["h2"], s)
                        wait(dve, S["rec_m"], k)
                        stats(lambda t: rec[:, kp, t, 0:D], 1, s, "ln2")
                    if b and u == 5:
                        dve.wait_ge(S["ln2_rstd"], s)
                        for t in range(2):
                            dve.tensor_scalar(xn[:, t, :], rec[:, kp, t, 0:D], mv[:, 1, t, 0:1], rec[:, kp, t, D + 1:D + 2], ALU.subtract, ALU.mult).then_inc(S["xn"], 1)
                        dve.wait_ge(S["xn"], 2 * s)
                        dve.wait_ge(S["s3_hi"], 2 * s)
                        low("s3", xn)
                    if f:
                        largest(u)
                if f:
                    dve.wait_ge(S["s_max"], 6 * (s + 1))
                    dve.wait_ge(S["q_ps"], 2 * (s + 1))
                    dve.tensor_scalar(qks[:, p, :, 0:HEADS, 3, 0], mx[:, :, :], -1.0, None, ALU.mult).then_inc(S["m_hi"], 1)
                    dve.wait_ge(S["m_hi"], s + 1)
                    dve.scalar_tensor_tensor(out=qks[:, p, :, 0:HEADS, 3, 1], in0=mx[:, :, :], scalar=-1.0, in1=qks[:, p, :, 0:HEADS, 3, 0],
                                             op0=ALU.mult, op1=ALU.subtract).then_inc(S["m_lo"], 1)
                if b:
                    lg = ps[:, 5, 0:2 * EXPERTS].rearrange("p (t e) -> p t e", t=2)
                    iota = cst[:, C_IOTA:C_IOTA + EXPERTS].unsqueeze(1).broadcast_to([P, 2, EXPERTS])
                    dve.wait_ge(S["lg_ps"], s)
                    dve.tensor_reduce(lmx[:, :], lg, AX.X, ALU.max).then_inc(S["lmx"], 1)
                    dve.wait_ge(S["lmx"], s)
                    wait(dve, S["le"], k)
                    dve.tensor_tensor(ld[:, :, :], lg, lmx[:, :].unsqueeze(2).broadcast_to([P, 2, EXPERTS]), ALU.subtract).then_inc(S["ld"], 1)
                    dve.wait_ge(S["ld"], s)
                    dve.scalar_tensor_tensor(out=c8[:, :, :], in0=ld[:, :, :], scalar=0.0, in1=iota, op0=ALU.is_equal, op1=ALU.mult).then_inc(S["c8"], 1)
                    dve.wait_ge(S["c8"], s)
                    dve.tensor_reduce(lsum[:, :], c8[:, :, :], AX.X, ALU.max).then_inc(S["cm"], 1)
                    dve.wait_ge(S["cm"], s)
                    wait(dve, S["pall"], 2 * k)
                    dve.tensor_tensor(code[:, 1, :], lsum[:, :], code[:, 0, :], ALU.mult).then_inc(S["code"], 1)
                    dve.wait_ge(S["code"], s)
                    wait(dve, S["cum"], 2 * (k - 1))
                    dve.tensor_tensor(oh[:, kp, :, :], iota, code[:, 1, :].unsqueeze(2).broadcast_to([P, 2, EXPERTS]), ALU.is_equal).then_inc(S["onehot"], 1)
                    dve.wait_ge(S["le"], s)
                    dve.tensor_reduce(lmx[:, :], le[:, :, :], AX.X, ALU.add).then_inc(S["lsum"], 1)
                    dve.wait_ge(S["lsum"], s)
                    dve.reciprocal(rec[:, kp, :, D + 2], lmx[:, :]).then_inc(S["prob"], 1)
                    dve.wait_ge(S["prefix"], s)
                    dve.tensor_tensor(sl[:, :, :], ps[:, 5, 256:256 + 2 * EXPERTS].rearrange("p (t e) -> p t e", t=2),
                                      cst[:, C_SLOT:C_SLOT + EXPERTS].unsqueeze(1).broadcast_to([P, 2, EXPERTS]), ALU.add).then_inc(S["slot_a"], 1)
                    dve.wait_ge(S["slot_a"], s)
                    dve.tensor_tensor(sl2[:, :, :], sl[:, :, :], oh[:, kp, :, :], ALU.mult).then_inc(S["slot_b"], 1)
                    dve.wait_ge(S["slot_b"], s)
                    dve.tensor_reduce(slot[:, :], sl2[:, :, :], AX.X, ALU.add).then_inc(S["slot_c"], 1)
                    dve.wait_ge(S["slot_c"], s)
                    dve.tensor_tensor(idx[:, kp, :], slot[:, :], cst[:, C_FAR:C_FAR + 2], ALU.add).then_inc(S["slot"], 1)
            run_images(dve, step)

        def early_done(eng):
            eng.wait_ge(S["early"], 4)

        def run_tiles(eng, step):
            for s in range(8):
                step(s, s % 2, s % 4, s // 4)
            whole = (TILES - 8) // 4
            with eng.Fori(0, whole) as i:
                for r in range(4):
                    step(4 * i + (8 + r), r % 2, r, i + 2)
            for s in range(8 + 4 * whole, TILES + 3):
                step(s, s % 2, s % 4, s // 4)

        def within(s, back):
            return not isinstance(s, int) or 0 <= s - back < TILES

        @block.sync
        def _(sp):
            early_done(sp)
            sp.dma_start(c3[:, :], consts3).then_inc(S["c3_in"], 16)
            sp.wait_ge(S["f_zero"], 2)
            for r in (0, 32):
                sp.dma_start(fb2[r:r + 1, :, :], b2.rearrange("(a e) d -> a e d", a=1)).then_inc(S["b2_in"], 16)

            def weights(e):
                q = e % 2
                wait(sp, S["f_hi"], 4 * (e - 1))
                wait(sp, S["f_lo"], 4 * (e - 1))
                sp.dma_start(f1[:, q, 0, :], w1[e, 0:P, :]).then_inc(S[f"f_in{q}"], 16)
                for r in (0, 64):
                    sp.dma_start(f1[r:r + 64, q, 1, :], w1[e, P:D, :]).then_inc(S[f"f_in{q}"], 16)
                for r in (64, 96):
                    sp.dma_start(f1[r:r + 1, q, 2, :], b1[e:e + 1, :]).then_inc(S[f"f_in{q}"], 16)
                sp.dma_start(f2[:, q, :, :], w2[e].rearrange("(f p) d -> p f d", p=P)).then_inc(S[f"f_in{q}"], 16)
            weights(0)
            weights(1)
            sp.wait_ge(S["plan"], PLAN["prow"])
            sp.dma_start(pflat.rearrange("a i n -> i a n"), prow[:, :, :]).then_inc(S["pf_out"], 16)
            sp.wait_ge(S["pf_out"], 16)
            for e in range(EXPERTS):
                sp.dma_start(eb[16 * e:16 * e + 16, :, :], pflat.rearrange("a i n -> a (i n)").rearrange("a (c n) -> c a n", c=16)).then_inc(S["eb_in"], 16)
            for e in range(2, EXPERTS):
                weights(e)
            sp.wait_ge(S["padrec"], 1)
            sp.dma_start(records[DUMMY:DUMMY + P, :], padrec[:, :]).then_inc(S["pad_out"], 16)
            for q in range(2):
                sp.wait_ge(S[f"sc_done{q}"], 16 * IMAGES)
            sp.wait_ge(S["tail_out"], 16 * EXPERTS)
            sp.wait_ge(S["pad_out"], 16)
            sp.wait_ge(S["plan"], PLAN["tables"])

            def step(s, p, r, q):
                if within(s, 0):
                    row = sp.value_load(rowt[0:1, bass.ds(s, 1)], min_val=0, max_val=DUMMY)
                    wait(sp, S[f"y_out{r}"], 16 * q)
                    sp.dma_start(xr[:, r, :], records[bass.ds(row, P), :]).then_inc(S[f"x4_in{r}"], 16)
            run_tiles(sp, step)
            for r in range(4):
                sp.wait_ge(S[f"y_out{r}"], 16 * len(range(r, TILES, 4)))

        @block.gpsimd
        def _(pool):
            for q in range(2):
                pool.wait_ge(S[f"sc_done{q}"], 16 * IMAGES)
            pool.drain().then_inc(S["early"], 1)
            early_done(pool)
            for a in (f1[:, 0, 2, :], f1[:, 1, 2, :]):
                pool.memset(a, 0.0).then_inc(S["f_zero1"], 1)
            pool.memset(fb2[:, :, :], 0.0).then_inc(S["f_zero"], 1)
            pool.wait_ge(S["f_zero1"], 2)
            pool.wait_ge(S["f_zero"], 1)
            pool.memset(padrec[:, :], 0.0).then_inc(S["f_zero"], 1)
            pool.memset(st4[:, :, :, :], 0.0).then_inc(S["st4_zero"], 1)
            pool.wait_ge(S["f_zero"], 2)
            pool.wait_ge(S["st4_zero"], 1)
            pool.memset(st4[:, :, 0, D:256:32], 1.0).then_inc(S["st4"], 1)
            pool.wait_ge(S["c3_in"], 16)
            pool.tensor_copy(padrec[:, REC - 1:REC].bitcast(U32), c3[:, K_PAD:K_PAD + 1]).then_inc(S["padrec"], 1)

            def lows(e):
                q = e % 2
                pool.wait_ge(S["f_hi"], 4 * (e + 1))
                hi1, hi2 = w1s[:, e, :], w2s[:, e, :].rearrange("p (f s d) -> p f s d", f=FT, s=2)
                pool.tensor_tensor(hi1[:, FF:2 * FF], f1[:, q, 0, :], hi1[:, 0:FF], ALU.subtract).then_inc(S["f_lo"], 1)
                pool.wait_ge(S["f_lo"], 4 * e + 1)
                pool.tensor_tensor(hi1[0:64, 3 * FF:4 * FF], f1[0:64, q, 1, :], hi1[0:64, 2 * FF:3 * FF], ALU.subtract).then_inc(S["f_lo"], 1)
                pool.wait_ge(S["f_lo"], 4 * e + 2)
                pool.tensor_tensor(hi1[96:P, 3 * FF:4 * FF], f1[96:P, q, 2, :], hi1[96:P, 3 * FF:4 * FF], ALU.subtract).then_inc(S["f_lo"], 1)
                pool.wait_ge(S["f_lo"], 4 * e + 3)
                pool.tensor_tensor(hi2[:, :, 1, :], f2[:, q, :, :], hi2[:, :, 0, :], ALU.subtract).then_inc(S["f_lo"], 1)
            pool.wait_ge(S["b2_hi"], 1)
            pool.wait_ge(S["padrec"], 1)
            pool.tensor_tensor(b2s[32:64, :, :], fb2[32:64, :, :], b2s[32:64, :, :], ALU.subtract).then_inc(S["b2_lo"], 1)
            pool.wait_ge(S["b2_lo"], 1)
            lows(0)
            pool.wait_ge(S["plan"], PLAN["tails"])
            pool.wait_ge(S["padrec"], 1)
            for e in range(EXPERTS):
                pool.indirect_dma_start(records, bass.IndirectOffsetOnAxis(ap=tails[:, e:e + 1], axis=0), padrec[:, :],
                                        None, bounds_check=DUMMY - 1, oob_is_err=False).then_inc(S["tail_out"], 16)
            pool.wait_ge(S["tail_out"], 16 * EXPERTS)
            for e in range(1, EXPERTS):
                lows(e)
            pool.wait_ge(S["plan"], PLAN["tables"])

            def step(s, p, r, q):
                if within(s, 0):
                    x, v = xr[:, r, :], small[:, p, :]
                    prob, n = x[:, D + 2:D + 3], bass.ds(s, 1)
                    col = lambda i: v[:, i:i + 1]
                    pool.wait_ge(S[f"x4_in{r}"], 16 * (q + 1))
                    carried(pool)
                    pool.tensor_copy(small[:, p, 4:6], tct[:, :, n].rearrange("p a n -> p (a n)")).then_inc(S["kept"], 1)
                    pool.tensor_copy(col(0), x[:, REC - 1:REC].bitcast(U32)).then_inc(S["kept"], 1)
                    pool.wait_ge(S["kept"], 7 * s + 1)
                    carried(pool)
                    pool.tensor_scalar(col(1), col(4), prob, None, ALU.is_equal).then_inc(S["kept"], 1)
                    pool.wait_ge(S["kept"], 7 * s + 2)
                    pool.wait_ge(S["kept"], 7 * s + 3)
                    carried(pool)
                    pool.tensor_scalar(col(2), col(5), col(0), col(1), ALU.is_ge, ALU.mult).then_inc(S["kept"], 1)
                    pool.wait_ge(S["kept"], 7 * s + 4)
                    carried(pool)
                    pool.tensor_scalar(col(3), col(4), prob, col(2), ALU.is_lt, ALU.add).then_inc(S["kept"], 1)
                    pool.wait_ge(S["kept"], 7 * s + 5)
                    wait(pool, S["fin"], s - 3)
                    pool.tensor_tensor(keepp[:, r, 0:1], col(3), prob, ALU.mult).then_inc(S["kept"], 1)
                    pool.wait_ge(S["kept"], 7 * s + 6)
                    pool.tensor_tensor(keepp[:, r, 1:2], prob, keepp[:, r, 0:1], ALU.subtract).then_inc(S["kept"], 1)
                if within(s, 3):
                    o = (r + 1) % 4
                    pool.wait_ge(S["fin"], s - 2)
                    carried(pool)
                    pool.indirect_dma_start(out, bass.IndirectOffsetOnAxis(ap=xr[:, o, REC - 1:REC].bitcast(U32), axis=0), orow[:, 1 - p, :],
                                            None, bounds_check=NTOK - 1, oob_is_err=False).then_inc(S[f"y_out{o}"], 16)
            run_tiles(pool, step)

        @block.scalar
        def _(act):
            act.drain().then_inc(S["early"], 1)
            early_done(act)
            act.wait_ge(S["b2_in"], 32)
            act.activation(b2s[:, :, :], fb2[:, :, :], ACT.Copy).then_inc(S["b2_hi"], 1)
            for e in range(EXPERTS):
                q = e % 2
                act.wait_ge(S[f"f_in{q}"], 96 * (e // 2 + 1))
                hi1, hi2 = w1s[:, e, :], w2s[:, e, :].rearrange("p (f s d) -> p f s d", f=FT, s=2)
                act.activation(hi1[:, 0:FF], f1[:, q, 0, :], ACT.Copy).then_inc(S["f_hi"], 1)
                act.activation(hi1[:, 2 * FF:3 * FF], f1[:, q, 1, :], ACT.Copy).then_inc(S["f_hi"], 1)
                act.activation(hi1[64:P, 3 * FF:4 * FF], f1[64:P, q, 2, :], ACT.Copy).then_inc(S["f_hi"], 1)
                act.activation(hi2[:, :, 0, :], f2[:, q, :, :], ACT.Copy).then_inc(S["f_hi"], 1)
            act.wait_ge(S["st4"], 1)

            def step(s, p, r, q):
                def gelu(half):
                    act.wait_ge(S["h_ps"], 2 * s - 1 + half)
                    wait(act, S["hl"], 2 * (s - 3) + 2)
                    act.activation(hf[:, 1 - p, 3 * P * half:3 * P * (half + 1)], ps[:, 2 + 2 * (1 - p) + half, 0:3 * P], ACT.Gelu).then_inc(S["hf"], 1)

                def high(half):
                    act.wait_ge(S["hf"], 2 * s - 1 + half)
                    wait(act, S["y_ps"], s - 2)
                    act.activation(hh[:, 1 - p, 3 * P * half:3 * P * (half + 1)], hf[:, 1 - p, 3 * P * half:3 * P * (half + 1)], ACT.Copy).then_inc(S["hh"], 1)

                if within(s, 1):
                    gelu(0)
                if within(s, 0):
                    act.wait_ge(S["xn4"], s + 1)
                    wait(act, S["t4_ps"], s - 1)
                    act.activation(st4[:, p, 0, 0:D], xn4[:, p, :], ACT.Copy).then_inc(S["x_hi"], 1)
                    act.activation(st4[:, p, 1, D:256], xn4[:, p, P:D], ACT.Copy).then_inc(S["x_hi"], 1)
                if within(s, 1):
                    high(0)
                    gelu(1)
                    high(1)
                if within(s, 0):
                    act.wait_ge(S["t4_ps"], s + 1)
                    wait(act, S["h_ps"], 2 * (s - 1))
                    act.activation(xt4[:, p, :, :], ps[:, p, 0:256].bitcast(F16).rearrange("p (c n) -> p c n", c=4), ACT.Copy).then_inc(S["xt4"], 1)
            run_tiles(act, step)

        @block.tensor
        def _(pe):
            pe.drain().then_inc(S["early"], 1)
            early_done(pe)
            pe.wait_ge(S["pall"], 2 * IMAGES)
            for a in range(2):
                for t in range(2):
                    pe.transpose(ps[0:IMAGES, a, t * P:(t + 1) * P], pall[:, a, t, :], ident).then_inc(S["pt_ps"], 1)
            pe.wait_ge(S["c3_in"], 16)
            total = lambda o, w, x, name: pe.matmul(o, w, x, start=True, stop=True).then_inc(S[name], 1)
            block_sum = c3[:, K_BLOCK:K_BLOCK + P]
            pe.wait_ge(S["plan"], PLAN["n_cnt"])
            total(ps[:, 3, 0:1], block_sum, cols["cnt"][:, :], "sums")
            pe.wait_ge(S["plan"], PLAN["ntile"])
            total(ps[:, 3, 1:2], c3[:, K_UPTO:K_UPTO + P], cols["ntile"][:, :], "sums")
            pe.wait_ge(S["plan"], PLAN["onef"])
            pe.wait_ge(S["plan"], PLAN["dn"])
            total(ps[:, 4, 0:EXPERTS], onef[:, :], dn[:, :], "sums")
            with pe.Fori(0, STEPS) as i:
                pe.wait_ge(S["count"], i + 1)
                total(ps[:, 2, 0:1], block_sum, cols["cnt"][:, :], "sum_ps")
            pe.wait_ge(S["plan"], PLAN["g_cnt"])
            total(ps[:, 3, 2:3], block_sum, cols["cnt"][:, :], "sums")
            pe.wait_ge(S["plan"], PLAN["tied"])
            total(ps[:, 4, 8:9], c3[:, K_BEFORE:K_BEFORE + P], tied[:, CHUNK - 1:CHUNK], "sums")
            pe.wait_ge(S["plan"], PLAN["cut_cnt"])
            total(ps[:, 3, 3:4], block_sum, cols["cutc"][:, :], "sums")
            pe.wait_ge(S["plan"], PLAN["vals_all"])
            total(ps[:, 5, 0:4 * TILES], onef[:, :], vals[:, :, :].rearrange("p a n -> p (a n)"), "sums")
            pe.wait_ge(S["plan"], PLAN["tables"])
            pe.wait_ge(S["f_hi"], 4 * EXPERTS)
            pe.wait_ge(S["f_lo"], 4 * EXPERTS)
            pe.wait_ge(S["b2_lo"], 1)

            def step(s, p, r, q):
                if within(s, 1):
                    e = pe.value_load(expt[0:1, bass.ds(s - 1, 1)], min_val=0, max_val=EXPERTS - 1)
                    pe.wait_ge(S["xt4"], s)
                    wait(pe, S["hf"], 2 * (s - 3) + 2)
                    for f in range(FT):
                        for i, (a, w) in enumerate(((0, 0), (0, 1), (1, 0), (2, 2), (3, 3))):
                            last = pe.matmul(ps[:, 2 + 2 * (1 - p) + f // 3, (f % 3) * P:(f % 3 + 1) * P],
                                             w1s[:, bass.ds(e, 1), w * FF + f * P:w * FF + (f + 1) * P], xt4[:, 1 - p, a, :],
                                             start=(i == 0), stop=(i == 4))
                        if f % 3 == 2:
                            last.then_inc(S["h_ps"], 1)
                if within(s, 0):
                    pe.wait_ge(S["x_lo"], s + 1)
                    pe.wait_ge(S["x_hi"], 2 * (s + 1))
                    wait(pe, S["xt4"], s - 1)
                    o = ps[:, p, 0:256].bitcast(F16)
                    for c, src in enumerate((st4[:, p, 0, 0:P], st4[:, p, 1, 0:P], st4[:, p, 1, P:256], st4[:, p, 0, P:256])):
                        last = pe.transpose(o[:, c * P:(c + 1) * P], src, idh[:, :])
                    last.then_inc(S["t4_ps"], 1)
                if within(s, 2):
                    e = pe.value_load(expt[0:1, bass.ds(s - 2, 1)], min_val=0, max_val=EXPERTS - 1)
                    pe.wait_ge(S["hh"], 2 * (s - 1))
                    pe.wait_ge(S["hl"], 2 * (s - 1))
                    wait(pe, S["fin"], s - 3)
                    y = ps[:, 6 + p, 0:D]
                    pe.matmul(y, oneh[:, :], b2s[:, bass.ds(e, 1), :], start=True, stop=False)
                    for f in range(FT):
                        for i, (a, w) in enumerate(((hh, 0), (hh, 1), (hl, 0))):
                            last = pe.matmul(y, a[:, p, f * P:(f + 1) * P], w2s[:, bass.ds(e, 1), (2 * f + w) * D:(2 * f + w + 1) * D],
                                             start=False, stop=(f == FT - 1 and i == 2))
                    last.then_inc(S["y_ps"], 1)
            run_tiles(pe, step)

        @block.vector
        def _(dve):
            dve.drain().then_inc(S["early"], 1)
            early_done(dve)
            dve.memset(onef[:, :], 1.0).then_inc(S["plan"], 1)
            dve.memset(one788[:, :], 1.0).then_inc(S["plan"], 1)
            dve.memset(cols["lo"][:, :], 0.0).then_inc(S["lo"], 1)
            dve.memset(cols["stepc"][:, :], 1.0).then_inc(S["halved"], 1)
            dve.memset(cols["cand"][:, :], 1.0).then_inc(S["cand"], 1)
            for a in range(2):
                for n, (to, at, length) in enumerate(((1, 0, P), (1 + P, P, REST), (0, P + REST, 1))):
                    dve.wait_ge(S["pt_ps"], 2 * a + 2)
                    dve.tensor_copy(prow[:, a, to:to + length], ps[0:IMAGES, a, at:at + length]).then_inc(S["plan"], 1)
            C = {n: c[:, :] for n, c in cols.items()}
            first = c3[:, K_FIRST:K_FIRST + 1]
            iota, iota128 = c3[:, K_IOTA:K_IOTA + P], c3[:, K_IOTA128:K_IOTA128 + P]
            dve.wait_ge(S["c3_in"], 16)
            dve.wait_ge(S["eb_in"], 16 * EXPERTS)
            dve.scalar_tensor_tensor(out=pe_e[:, :], in0=eb[:, 1, :], scalar=c3[:, K_CODE:K_CODE + 1], in1=eb[:, 0, :],
                                     op0=ALU.is_equal, op1=ALU.mult).then_inc(S["plan"], 1)
            dve.wait_ge(S["plan"], PLAN["pe_e"])

            def count(src, bound, op, acc, name, n=CHUNK):
                dve.tensor_scalar(scr[:, 0:n], src, bound, None, op, ALU.add, accum_out=C[acc]).then_inc(S[name], 1)
            count(pe_e[:, :], 0.0, ALU.is_gt, "cnt", "plan")
            dve.wait_ge(S["sums"], SUMS["n"])
            dve.tensor_copy(C["n_e"], ps[:, 3, 0:1]).then_inc(S["plan"], 1)
            dve.wait_ge(S["plan"], PLAN["n_e"])
            dve.wait_ge(S["plan"], PLAN["n_cnt"])
            count(iota128, C["n_e"], ALU.is_lt, "ntile", "plan", P)
            dve.tensor_scalar(dn[:, :], c3[:, K_SEL:K_SEL + EXPERTS], C["n_e"], None, ALU.mult).then_inc(S["plan"], 1)
            dve.wait_ge(S["sums"], SUMS["end"])
            dve.wait_ge(S["plan"], PLAN["ntile"])
            dve.tensor_copy(C["end"], ps[:, 3, 1:2]).then_inc(S["plan"], 1)
            dve.wait_ge(S["sums"], SUMS["tail"])
            dve.tensor_tensor(tails[:, :], ps[:, 4, 0:EXPERTS], c3[:, K_TAIL:K_TAIL + EXPERTS], ALU.add).then_inc(S["plan"], 1)
            dve.wait_ge(S["plan"], PLAN["end"])
            dve.tensor_tensor(C["start"], C["end"], C["ntile"], ALU.subtract).then_inc(S["plan"], 1)
            with dve.Fori(0, STEPS) as i:
                dve.wait_ge(S["cand"], i + 1)
                dve.wait_ge(S["halved"], i + 1)
                count(pe_e[:, :], C["cand"], ALU.is_ge, "cnt", "count")
                dve.wait_ge(S["sum_ps"], i + 1)
                dve.scalar_tensor_tensor(out=C["took"], in0=ps[:, 2, 0:1], scalar=float(CAP), in1=C["stepc"], op0=ALU.is_ge, op1=ALU.mult).then_inc(S["took"], 1)
                dve.wait_ge(S["took"], i + 1)
                dve.tensor_scalar(C["stepc"], C["stepc"], 0.5, None, ALU.mult).then_inc(S["halved"], 1)
                dve.wait_ge(S["lo"], i + 1)
                dve.tensor_tensor(C["lo"], C["took"], C["lo"], ALU.add).then_inc(S["lo"], 1)
                dve.wait_ge(S["lo"], i + 2)
                dve.wait_ge(S["halved"], i + 2)
                dve.tensor_tensor(C["cand"], C["lo"], C["stepc"], ALU.add).then_inc(S["cand"], 1)
            dve.wait_ge(S["count"], STEPS)
            count(pe_e[:, :], C["lo"], ALU.is_gt, "cnt", "plan")
            dve.tensor_scalar(tie[:, :], pe_e[:, :], C["lo"], None, ALU.is_equal).then_inc(S["plan"], 1)
            dve.wait_ge(S["plan"], PLAN["tie"])
            dve.wait_ge(S["plan"], PLAN["one788"])
            dve.tensor_tensor_scan(tied[:, :], one788[:, :], tie[:, :], 0.0, ALU.mult, ALU.add).then_inc(S["plan"], 1)
            dve.wait_ge(S["sums"], SUMS["g"])
            dve.tensor_scalar(C["room"], ps[:, 3, 2:3], -1.0, float(CAP), ALU.mult, ALU.add).then_inc(S["plan"], 1)
            dve.wait_ge(S["sums"], SUMS["before"])
            dve.wait_ge(S["plan"], PLAN["room"])
            dve.tensor_tensor(C["lim"], C["room"], ps[:, 4, 8:9], ALU.subtract).then_inc(S["plan"], 1)
            dve.wait_ge(S["plan"], PLAN["lim"])
            dve.wait_ge(S["plan"], PLAN["tied"])
            dve.wait_ge(S["plan"], PLAN["g_cnt"])
            count(tied[:, :], C["lim"], ALU.is_lt, "cutc", "plan")
            dve.wait_ge(S["plan"], PLAN["start"])
            dve.tensor_scalar(ended[:, :], iota, C["end"], first, ALU.is_lt, ALU.mult).then_inc(S["plan"], 1)
            dve.scalar_tensor_tensor(out=C["vrow"], in0=C["start"], scalar=-float(P), in1=c3[:, K_REGION:K_REGION + 1],
                                     op0=ALU.mult, op1=ALU.add).then_inc(S["plan"], 1)
            dve.wait_ge(S["plan"], PLAN["sel_a"])
            dve.scalar_tensor_tensor(out=sel[:, :], in0=iota, scalar=C["start"], in1=ended[:, :], op0=ALU.is_ge, op1=ALU.mult).then_inc(S["plan"], 1)
            dve.wait_ge(S["plan"], PLAN["sel"])
            dve.wait_ge(S["plan"], PLAN["vrow"])
            dve.scalar_tensor_tensor(out=vals[:, 0, :], in0=iota128[:, 0:TILES], scalar=C["vrow"], in1=sel[:, 0:TILES],
                                     op0=ALU.add, op1=ALU.mult).then_inc(S["plan"], 1)
            dve.tensor_scalar(vals[:, 1, :], sel[:, 0:TILES], c3[:, K_EXPERT:K_EXPERT + 1], None, ALU.mult).then_inc(S["plan"], 1)
            dve.tensor_scalar(vals[:, 2, :], sel[:, 0:TILES], C["lo"], None, ALU.mult).then_inc(S["plan"], 1)
            dve.wait_ge(S["sums"], SUMS["cut"])
            dve.wait_ge(S["plan"], PLAN["cut_cnt"])
            dve.tensor_copy(C["cutc"], ps[:, 3, 3:4]).then_inc(S["plan"], 1)
            dve.wait_ge(S["plan"], PLAN["cut"])
            dve.tensor_scalar(vals[:, 3, :], sel[:, 0:TILES], C["cutc"], None, ALU.mult).then_inc(S["plan"], 1)
            dve.wait_ge(S["sums"], SUMS["table"])
            table = ps[:, 5, 0:4 * TILES].rearrange("p (a n) -> p a n", a=4)
            dve.tensor_scalar(rowt[:, :], table[:, 0, :], float(DUMMY), None, ALU.add).then_inc(S["plan"], 1)
            dve.tensor_copy(expt[:, :], table[:, 1, :]).then_inc(S["plan"], 1)
            dve.tensor_copy(tct[:, :, :], table[:, 2:4, :]).then_inc(S["plan"], 1)
            dve.wait_ge(S["st4"], 1)

            def step(s, p, r, q):
                if within(s, 0):
                    x = xr[:, r, :]
                    dve.wait_ge(S[f"x4_in{r}"], 16 * (q + 1))
                    wait(dve, S["x_hi"], 2 * (s - 1))
                    wait(dve, S["x_lo"], s - 1)
                    wait(dve, S["base"], s - 1)
                    dve.tensor_scalar(xn4[:, p, :], x[:, 0:D], x[:, D:D + 1], x[:, D + 1:D + 2], ALU.subtract, ALU.mult).then_inc(S["xn4"], 1)
                if within(s, 3):
                    o = (r + 1) % 4
                    dve.wait_ge(S["y_ps"], s - 2)
                    dve.wait_ge(S["kept"], 7 * (s - 3) + 6)
                    dve.wait_ge(S["base"], s - 2)
                    if not isinstance(s, int) or s >= 5:
                        dve.wait_ge(S[f"y_out{(r + 3) % 4}"], 16 * (q if r else q - 1))
                    dve.scalar_tensor_tensor(out=orow[:, 1 - p, :], in0=ps[:, 6 + 1 - p, 0:D], scalar=keepp[:, o, 0:1], in1=base[:, o, :],
                                             op0=ALU.mult, op1=ALU.add).then_inc(S["fin"], 1)
                if within(s, 0):
                    dve.wait_ge(S["x_hi"], 2 * s + 1)
                    dve.wait_ge(S["xn4"], s + 1)
                    wait(dve, S["t4_ps"], s - 1)
                    dve.tensor_tensor(st4[:, p, 1, 0:D], xn4[:, p, :], st4[:, p, 0, 0:D], ALU.subtract).then_inc(S["x_lo"], 1)
                    dve.wait_ge(S["kept"], 7 * s + 7)
                    wait(dve, S["fin"], s - 3)
                    dve.scalar_tensor_tensor(out=base[:, r, :], in0=xn4[:, p, :], scalar=keepp[:, r, 1:2], in1=x[:, 0:D],
                                             op0=ALU.mult, op1=ALU.add).then_inc(S["base"], 1)
                if within(s, 1):
                    for half in range(2):
                        dve.wait_ge(S["hh"], 2 * s - 1 + half)
                        wait(dve, S["y_ps"], s - 2)
                        c = slice(3 * P * half, 3 * P * (half + 1))
                        dve.tensor_tensor(hl[:, 1 - p, c], hf[:, 1 - p, c], hh[:, 1 - p, c], ALU.subtract).then_inc(S["hl"], 1)
            run_tiles(dve, step)

def constants3():
    import numpy as np
    c = np.zeros((P, N_CONST3), np.float32)
    e, k = np.arange(P) // 16, np.arange(P) % 16
    same = e[:, None] == e[None]
    c[:, K_BLOCK:K_BLOCK + P] = same
    c[:, K_BEFORE:K_BEFORE + P] = same & (k[:, None] < k[None])
    c[:, K_UPTO:K_UPTO + P] = (k[:, None] == 0) & (e[:, None] <= e[None])
    c[:, K_IOTA:K_IOTA + P] = np.arange(P)
    c[:, K_IOTA128:K_IOTA128 + P] = P * np.arange(P)
    c[:, K_SEL:K_SEL + EXPERTS] = (k[:, None] == 0) & (e[:, None] == np.arange(EXPERTS))
    c[:, K_TAIL:K_TAIL + EXPERTS] = np.arange(EXPERTS) * REGION + np.arange(P)[:, None]
    c[:, K_FIRST] = k == 0
    c[:, K_CODE] = EXPERTS - e
    c[:, K_REGION] = e * REGION - DUMMY
    c[:, K_EXPERT] = e
    c[:, K_PAD] = FAR
    return c


_OTHERS = ("L0_tok_b", "cls_tok", "L0_attn_W_qkv", "L0_attn_b_qkv", "L0_attn_W_out", "L0_attn_b_out", "L0_ffn_switch_w",
           "L0_ffn_switch_b", "L0_ffn_w1", "L0_ffn_b1", "L0_ffn_w2", "L0_ffn_b2")


def kernel(x, cls_tok, L0_tok_ln_gamma, L0_tok_ln_beta, L0_tok_W, **others):
    import numpy as np
    import concourse.bacc as bacc
    from concourse.bass_utils import run_bass_kernel_spmd

    xt, wr, gr, br, mult = lay_out(np.asarray(x), np.asarray(L0_tok_ln_gamma), np.asarray(L0_tok_ln_beta), np.asarray(L0_tok_W))
    given = {"xt": xt, "wr": wr, "gr": gr, "br": br}
    for name in _OTHERS:
        a = np.ascontiguousarray(cls_tok if name == "cls_tok" else others[name])
        given[name] = a.reshape(1, D) if name == "cls_tok" else a
    given.update(c=constants(mult), c3=constants3())
    nc = bacc.Bacc("TRN2", target_bir_lowering=False, num_devices=1)
    arrays, args = {}, []
    for name, a in given.items():
        arrays[f"in_{name}_dram"] = a
        args.append(nc.dram_tensor(f"in_{name}_dram", a.shape, mybir.dt.from_np(a.dtype), kind="ExternalInput").ap())
    args.append(nc.dram_tensor("out_0_dram", (NTOK, D), F32, kind="ExternalOutput").ap())
    build(nc, *args)
    r = run_bass_kernel_spmd(nc, [arrays], core_ids=[0])
    return r.results[0]["out_0_dram"].reshape(IMAGES, TOK, D)


def layout():
    import numpy as np
    moves = [(0, 0), (0, 1), (0, -1), (1, 0), (-1, 0)]
    where = {}
    for s, (dy, dx) in enumerate(moves):
        for y in range(PATCH):
            for x in range(PATCH):
                for c in range(CH):
                    where.setdefault((c, y - dy, x - dx), []).append(((y * PATCH + x) * 5 + s) * CH + c)
    rows, mult = [], np.zeros(KP, np.float32)
    p = 0
    for m in (5, 4, 3, 1):
        pixels = [k for k in sorted(where) if len(where[k]) == m]
        n = -(-len(pixels) // KT)
        mult[p:p + n] = m
        rows += [(p + i // KT, i % KT, k, where[k]) for i, k in enumerate(pixels)]
        p += n
    assert p == KP
    return rows, mult


def lay_out(x, ln_gamma, ln_beta, w):
    import numpy as np
    rows, mult = layout()
    pad = np.zeros((IMAGES, CH, 226, 226), np.float32)
    pad[:, :, 1:225, 1:225] = x
    xt = np.zeros((KP, KT, IMAGES, SIDE, SIDE), np.float32)
    wr = np.zeros((KP, KT, SHIFTS, D), np.float32)
    gr = np.zeros((KP, KT, SHIFTS), np.float32)
    br = np.zeros((KP, KT, SHIFTS), np.float32)
    for p, k, (c, y, xx), terms in rows:
        xt[p, k] = pad[:, c, y + 1:y + 1 + 209:PATCH, xx + 1:xx + 1 + 209:PATCH]
        for s, e in enumerate(terms):
            wr[p, k, s], gr[p, k, s], br[p, k, s] = w[e], ln_gamma[e], ln_beta[e]
    xt = np.ascontiguousarray(xt.reshape(KP, KT, GROUPS, GT).transpose(2, 0, 1, 3))
    return xt, wr, gr, br, mult


def constants(mult):
    import numpy as np
    c = np.zeros((P, N_CONST), np.float32)
    c[:, C_ID:C_ID + P] = np.eye(P)
    c[:, C_TRI:C_TRI + P] = np.triu(np.ones((P, P)))
    place = np.zeros((2, P), np.int64)
    place[0] = 1 + np.arange(P)
    place[1, :REST] = 1 + P + np.arange(REST)
    freqs = np.arange(TOK, dtype=np.float32)[:, None] / np.float32(10000.0) ** (np.arange(0, HD, 2, dtype=np.float32) / np.float32(HD))[None]
    emb = np.concatenate([freqs, freqs], -1).astype(np.float32)
    sign = np.tile(np.array([-1.0, 1.0], np.float32), HD // 2)
    for t in range(2):
        c[:, C_COS + t * 2 * D:C_COS + (t + 1) * 2 * D] = np.tile(np.cos(emb[place[t]]), (1, 2 * HEADS))
        c[:, C_SIN + t * 2 * D:C_SIN + (t + 1) * 2 * D] = np.tile(np.sin(emb[place[t]]) * sign, (1, 2 * HEADS))
    c[:KP, C_MULT] = mult
    c[:, C_TOKN:C_TOKN + 2] = place.T
    c[:, C_VALID] = 1
    c[:REST + 1, C_VALID + 1] = 1
    c[REST + 1:, C_FAR + 1] = FAR
    c[:, C_SLOT:C_SLOT + EXPERTS] = np.arange(EXPERTS) * REGION - 1
    c[:, C_IOTA:C_IOTA + EXPERTS] = EXPERTS - np.arange(EXPERTS)
    return c
```

```python
from contextlib import ExitStack

import concourse.bass as bass
from concourse import mybir

F32, F16, U32 = mybir.dt.float32, mybir.dt.float16, mybir.dt.uint32
ALU, ACT, AX = mybir.AluOpType, mybir.ActivationFunctionType, mybir.AxisListType

P = 128
IMAGES, SIDE, PATCH, CH = 64, 14, 16, 3
PATCHES = SIDE * SIDE
TOK = PATCHES + 1
REST = PATCHES - P
D, HEADS, HD = 192, 12, 16
TERMS = PATCH * PATCH * CH * 5
KP, KT, SHIFTS = 121, 8, 5
GT = 256
GROUPS = IMAGES * PATCHES // GT
EXPERTS, FF = 8, 768
NTOK = IMAGES * TOK
CAP = int(1.25 * NTOK / EXPERTS)
REC = 196
EPS = 1e-5
NW = 3 * D + D + EXPERTS
W_OUT, W_SW = 3 * D, 4 * D
FAR = float(1 << 22)
TILES = (NTOK + EXPERTS * (P - 1)) // P
REGION = (NTOK // P + 3) * P
DUMMY = EXPERTS * REGION
CHUNK = NTOK // 16
FT = FF // P
STEPS = 29

C_ID, C_TRI, C_COS, C_SIN, C_MULT, C_TOKN, C_VALID, C_FAR, C_SLOT, C_IOTA = 0, 128, 256, 1024, 1792, 1793, 1795, 1797, 1799, 1807
N_CONST = 1816
K_BLOCK, K_BEFORE, K_UPTO, K_IOTA, K_IOTA128, K_SEL, K_TAIL = 0, 128, 256, 384, 512, 640, 648
K_FIRST, K_CODE, K_REGION, K_EXPERT, K_PAD, N_CONST3 = 656, 657, 658, 659, 660, 661


def after(*steps):
    done, total = {}, 0
    for s in steps:
        name, n = s if isinstance(s, tuple) else (s, 1)
        total += n
        done[name] = total
    return done


PLAN = after("onef", "one788", ("prow", 6), "pe_e", "n_cnt", "n_e", "ntile", "dn", "end", "tails", "start", "g_cnt", "tie", "tied",
             "room", "lim", "cut_cnt", "sel_a", "vrow", "sel", ("vals", 3), "cut", "vals_all", ("tables", 3))
SUMS = after("n", "end", "tail", "g", "before", "cut", "table")


class Sems:

    def __init__(self, nc, ctx):
        self._made, self._nc, self._ctx = {}, nc, ctx

    def __getitem__(self, name):
        if name not in self._made:
            self._made[name] = self._ctx.enter_context(self._nc.semaphore(name))
        return self._made[name]


def wait(eng, sem, value):
    if not (isinstance(value, int) and value <= 0):
        eng.wait_ge(sem, value)


def build(nc, xt, wraw, graw, braw, tokb, cls, wqkv, bqkv, wout, bout, wsw, bsw, w1, b1, w2, b2, consts, consts3, out):
    ctx = ExitStack()
    with ctx:
        sb = lambda name, shape, dt=F32: area.enter_context(nc.sbuf_tensor(name, shape, dt))
        area = ctx
        S = Sems(nc, ctx)
        hp = nc.dram_tensor("hp", (IMAGES * PATCHES, D), F32).ap()

        cst = sb("cst", [P, N_CONST])
        ident = cst[:, C_ID:C_ID + P]
        idh = sb("idh", [P, P], F16)
        oneh = sb("oneh", [P, P], F16)
        pall = sb("pall", [P, 2, 2, IMAGES])
        ps = ctx.enter_context(nc.psum_tensor("ps", [P, 8, 512], F32))
        area = early = ctx.enter_context(ExitStack())
        xb = sb("xb", [KP, 2, KT, GT])
        xsq = sb("xsq", [KP, KT, GT])
        xss = sb("xss", [KP, GT])
        wr = sb("wr", [KP, KT, SHIFTS, D])
        gb = sb("gb", [KP, 2, KT, SHIFTS])
        wg = sb("wg", [KP, 2, SHIFTS, D])
        wf = sb("wf", [KP, KT, D + 1])
        ones = sb("ones", [P, P])
        gsum = sb("gsum", [P, D])
        brow = sb("brow", [P, D])
        brow0 = sb("brow0", [P, D])
        xst = sb("xst", [P, 2, 4, 2])
        hm = sb("hm", [P, 2, D])
        ho = sb("ho", [P, 2, 2, D])
        mhalf = sb("mhalf", [P, 2])

        hx = sb("hx", [P, 2, 2, D])
        hr = sb("hr", [P, 2, 2, D])
        rec = sb("rec", [P, 2, 2, REC])
        wstage = sb("wstage", [P, 3, NW])
        wst = sb("wst", [P, 4, NW], F16)
        st = {n: sb(n, [P, 2, 2, 256], F16) for n in ("s1", "s2", "s3")}
        tt = {n: sb(n, [P, 1 + (n == "t1"), 4, 256], F16) for n in ("t1", "t2", "t3")}
        trih = sb("trih", [P, P], F16)
        mvs = sb("mvs", [P, 2, 2, 6])
        mv = sb("mv", [P, 2, 2, 2])
        mve = sb("mve", [P, 2, 2])
        rstd1 = sb("rstd1", [P, 2])
        hn = sb("hn", [P, 2, D])
        xn = sb("xn", [P, 2, D])
        cn = sb("cn", [P, 2, D])
        rc = sb("rc", [P, 2, HEADS])
        ra = sb("ra", [P, 2, 2 * D])
        rb = sb("rb", [P, 2, 2 * D])
        qk = sb("qk", [P, 2, 2 * D])
        qks = sb("qks", [P, 2, 2, 2 * HEADS, 4, HD], F16)
        kms = sb("kms", [P, 2, 6, 2, 256], F16)
        qt = sb("qt", [P, 6, 256], F16)
        q2t = sb("q2t", [P, 6, 256], F16)
        va = sb("va", [P, 2, 2, HEADS, 32])
        pt = sb("pt", [P, 2, HEADS, TOK])
        ctxt = sb("ctxt", [P, 3, 256])
        mx = sb("mx", [P, 2, HEADS])
        lmx = sb("lmx", [P, 2])
        ld = sb("ld", [P, 2, EXPERTS])
        le = sb("le", [P, 2, EXPERTS])
        lsum = sb("lsum", [P, 2])
        c8 = sb("c8", [P, 2, EXPERTS])
        code = sb("code", [P, 2, 2])
        oh = sb("oh", [P, 2, 2, EXPERTS], F16)
        cum = sb("cum", [P, 2, 2, EXPERTS], F16)
        sl = sb("sl", [P, 2, EXPERTS])
        sl2 = sb("sl2", [P, 2, EXPERTS])
        slot = sb("slot", [P, 2])
        idx = sb("idx", [P, 2, 2], U32)
        tokn = sb("tokn", [P, 2])
        records = nc.dram_tensor("records", (DUMMY + P, REC), F32).ap()
        pflat = nc.dram_tensor("pflat", (2, IMAGES, TOK), F32).ap()
        half6 = ps[:, 6, :].bitcast(F16).rearrange("p (s c) -> p s c", c=256)
        half7 = ps[:, 7, :].bitcast(F16).rearrange("p (s c) -> p s c", c=256)

        early.close()
        area = ctx

        c3 = sb("c3", [P, N_CONST3])
        onef = sb("onef", [P, P])
        prow = sb("prow", [IMAGES, 2, TOK])
        eb = sb("eb", [P, 2, CHUNK])
        pe_e = sb("pe_e", [P, CHUNK])
        scr = sb("scr", [P, CHUNK])
        tie = sb("tie", [P, CHUNK])
        tied = sb("tied", [P, CHUNK])
        one788 = sb("one788", [P, CHUNK])
        cols = {n: sb(n, [P, 1]) for n in ("cnt", "n_e", "ntile", "end", "start", "vrow", "lo", "stepc", "cand", "took", "room", "lim", "cutc")}
        dn = sb("dn", [P, EXPERTS])
        tails = sb("tails", [P, EXPERTS], U32)
        padrec = sb("padrec", [P, REC])
        ended = sb("ended", [P, P])
        sel = sb("sel", [P, P])
        vals = sb("vals", [P, 4, TILES])
        rowt = sb("rowt", [P, TILES], U32)
        expt = sb("expt", [P, TILES], U32)
        tct = sb("tct", [P, 2, TILES])
        f1 = sb("f1", [P, 2, 3, FF])
        f2 = sb("f2", [P, 2, FT, D])
        fb2 = sb("fb2", [P, EXPERTS, D])
        w1s = sb("w1s", [P, EXPERTS, 4 * FF], F16)
        w2s = sb("w2s", [P, EXPERTS, FT * 2 * D], F16)
        b2s = sb("b2s", [P, EXPERTS, D], F16)
        xr = sb("xr", [P, 4, REC])
        xn4 = sb("xn4", [P, 2, D])
        st4 = sb("st4", [P, 2, 2, 256], F16)
        xt4 = sb("xt4", [P, 2, 4, P], F16)
        hf = sb("hf", [P, 2, FF])
        hh = sb("hh", [P, 2, FF], F16)
        hl = sb("hl", [P, 2, FF], F16)
        small = sb("small", [P, 2, 8])
        keepp = sb("keepp", [P, 4, 2])
        base = sb("base", [P, 4, D])
        orow = sb("orow", [P, 2, D])

        block = ctx.enter_context(nc.Block())

        def run_images(eng, step):
            for s in range(7):
                step(s, s % 2, s // 2)
            with eng.Fori(0, (IMAGES - 8) // 2) as i:
                step(2 * i + 7, 1, i + 3)
                step(2 * i + 8, 0, i + 4)
            for s in range(IMAGES - 1, IMAGES + 4):
                step(s, s % 2, s // 2)

        def carried(eng):
            eng.sem_inc(S["carried"], 1)

        def images_of(s):
            n = [s - k for k in range(5)]
            return n, [not isinstance(x, int) or 0 <= x < IMAGES for x in n]

        def upto(n):
            return min(n, IMAGES) if isinstance(n, int) else n

        def groups(eng, body):
            for g in range(3):
                body(g, g % 2, g // 2)
            with eng.Fori(0, (GROUPS - 3) // 2) as i:
                body(2 * i + 3, 1, i + 1)
                body(2 * i + 4, 0, i + 2)

        @block.sync
        def _(sp):
            sp.dma_start(wr[:, :, :, :], wraw).then_inc(S["w_in"], 16)
            sp.dma_start(gb[:, 0, :, :], graw).then_inc(S["g_in"], 16)
            sp.dma_start(gb[:, 1, :, :], braw).then_inc(S["b_in"], 16)
            sp.dma_start(cst[:, :], consts).then_inc(S["c_in"], 16)
            sp.dma_start(brow0[:, :], tokb.partition_broadcast(P)).then_inc(S["tb_in"], 16)

            def load(g, p, half):
                wait(sp, S["acc"], 2 * (g - 1))
                wait(sp, S["sq"], g - 1)
                sp.dma_start(xb[:, p, :, :], xt[bass.ds(g, 1), :, :, :].rearrange("g p k t -> (g p) k t")).then_inc(S[f"x_in{p}"], 16)
            groups(sp, load)
            sp.wait_ge(S["wz"], 1)
            for c, n, w, b in ((0, 3 * D, wqkv, bqkv), (W_OUT, D, wout, bout), (W_SW, EXPERTS, wsw, bsw)):
                sp.dma_start(wstage[:, 0, c:c + n], w[0:P, :]).then_inc(S["ws_in"], 16)
                for r in (0, 64):
                    sp.dma_start(wstage[r:r + 64, 1, c:c + n], w[P:D, :]).then_inc(S["ws_in"], 16)
                for r in (64, 96):
                    sp.dma_start(wstage[r:r + 1, 2, c:c + n], b.rearrange("(a n) -> a n", a=1)).then_inc(S["ws_in"], 16)
            sp.wait_ge(S["mem"], 1)
            for q in range(2):
                for a in (hx, hr):
                    sp.dma_start(a[REST:REST + 1, q, 1, :], cls).then_inc(S["cls_in"], 16)
            sp.wait_ge(S["hp_out0"], 16 * ((GROUPS + 1) // 2))
            sp.wait_ge(S["hp_out1"], 16 * (GROUPS // 2))

            def tokens(n, q, to, name):
                sp.dma_start(to[:, q, 0, :], hp[bass.ds(PATCHES * n, P), :]).then_inc(S[f"{name}{q}"], 16)
                sp.dma_start(to[0:REST, q, 1, :], hp[bass.ds(PATCHES * n + P, REST), :]).then_inc(S[f"{name}{q}"], 16)

            def image_in(s, p, half):
                (a, b, m, c, d), (on_a, on_b, on_m, on_c, on_d) = images_of(s)
                if on_a:
                    wait(sp, S["ln1_hn"], 2 * (a - 1))
                    tokens(a, p, hx, "h_in")
                if on_c:
                    wait(sp, S["h2"], c - 1)
                    tokens(c, 1 - p, hr, "hr_in")
            run_images(sp, image_in)

        @block.gpsimd
        def _(pool):
            pool.memset(mhalf[:, :], -0.5).then_inc(S["mhalf"], 1)
            pool.wait_ge(S["mhalf"], 1)

            def power(g, p, half):
                pool.wait_ge(S["var"], g + 1)
                pool.tensor_tensor(xst[:, p, 3, :], xst[:, p, 2, :], mhalf[:, :], ALU.pow).then_inc(S["rstd"], 1)
            for a in (hx, hr, qks, kms, qt, va, *st.values(), *tt.values(), cum):
                pool.memset(a.ap() if hasattr(a, "ap") and callable(a.ap) else a, 0.0).then_inc(S["zero"], 1)
            pool.wait_ge(S["zero"], 13)
            for a in st.values():
                pool.memset(a[:, :, 0, D:256:32], 1.0).then_inc(S["one"], 1)
            pool.memset(qks[:, :, :, HEADS:, 3, 0:2].rearrange("p a t h r -> p (a t) h r"), 1.0).then_inc(S["one"], 1)
            pool.memset(va[:, :, :, :, HD:HD + 1].rearrange("p a t h r -> p (a t) h r"), 1.0).then_inc(S["one"], 1)
            pool.memset(ctxt[:, :, :], 1.0).then_inc(S["one"], 1)
            pool.memset(oneh[:, :], 1.0).then_inc(S["one"], 1)
            pool.wait_ge(S["c_in"], 16)
            pool.tensor_copy(tokn[:, :], cst[:, C_TOKN:C_TOKN + 2]).then_inc(S["one"], 1)
            pool.wait_ge(S["one"], 8)
            pool.drain().then_inc(S["mem"], 1)
            groups(pool, power)
            pool.wait_ge(S["wst"], 6)

            def step(s, p, half):
                (a, b, m, c, d), (on_a, on_b, on_m, on_c, on_d) = images_of(s)

                def low(on, name, x, n, src, rows):
                    if on:
                        wait(pool, S[name + "_ps"], n)
                        pool.wait_ge(S[rows], 2 * (n + 1))
                        pool.wait_ge(S[x + "_hi"], 2 * (n + 1))
                        pool.tensor_tensor(st[x][:, :, 1, 0:D], src[:, :, :], st[x][:, :, 0, 0:D], ALU.subtract).then_inc(S[x + "_lo"], 1)

                def no_maxima():
                    if on_b:
                        wait(pool, S["q2_ps"], 2 * (b - 1))
                        carried(pool)
                        pool.memset(qks[:, 1 - p, :, 0:HEADS, 3, 0:2], 0.0).then_inc(S["m_zero"], 1)

                def numbers():
                    if on_d:
                        wait(pool, S[f"sc_done{p}"], 32 * (half - 2))
                        carried(pool)
                        pool.tensor_copy(rec[:, p, :, REC - 1].bitcast(U32), tokn[:, :]).then_inc(S["tok"], 1)
                        pool.wait_ge(S["tok"], 2 * d + 1)
                        carried(pool)
                        pool.tensor_scalar(tokn[:, :], tokn[:, :], float(TOK), None, ALU.add).then_inc(S["tok"], 1)

                def rstd_2():
                    if on_d:
                        pool.wait_ge(S["ln2_var"], d + 1)
                        pool.tensor_tensor(rec[:, p, :, D + 1], mve[:, 1, :], mhalf[:, :], ALU.pow).then_inc(S["ln2_rstd"], 1)
                        pool.tensor_copy(rec[:, p, :, D], mv[:, 1, :, 0]).then_inc(S["rec_m"], 1)

                def rstd_1():
                    if on_a:
                        pool.wait_ge(S["ln1_var"], a + 1)
                        pool.tensor_tensor(rstd1[:, :], mve[:, 0, :], mhalf[:, :], ALU.pow).then_inc(S["ln1_rstd"], 1)

                def rotated_low(t):
                    if on_b:
                        pool.wait_ge(S["qk_hi"], 2 * b + t + 1)
                        src = qk[:, t, :].rearrange("p (w h r) -> p w h r", w=2, r=HD)
                        hi = qks[:, 1 - p, t, :, 0, :].rearrange("p (w h) r -> p w h r", w=2)
                        for w in range(2):
                            pool.tensor_tensor(qks[:, 1 - p, t, HEADS * w:HEADS * (w + 1), 1 + w, :], src[:, w, :, :], hi[:, w, :, :],
                                               ALU.subtract).then_inc(S["qk_lo"], 1)

                def counted():
                    if on_d:
                        pool.wait_ge(S["onehot"], d + 1)
                        wait(pool, S["prefix"], d)
                        pool.tensor_tensor(cum[:, p, 1, :], cum[:, p, 0, :], oh[:, p, 0, :], ALU.add).then_inc(S["cum"], 1)
                        pool.wait_ge(S["cum"], 2 * d + 1)
                        pool.tensor_tensor(cum[:, 1 - p, 0, :], cum[:, p, 1, :], oh[:, p, 1, :], ALU.add).then_inc(S["cum"], 1)

                def noted():
                    if on_d:
                        pool.wait_ge(S["prob"], d + 1)
                        carried(pool)
                        pool.tensor_copy(pall[:, 0, :, bass.ds(d, 1)], rec[:, p, :, D + 2:D + 3]).then_inc(S["pall"], 1)
                        pool.tensor_copy(pall[:, 1, :, bass.ds(d, 1)], code[:, 1, :].unsqueeze(2)).then_inc(S["pall"], 1)

                def scattered():
                    if on_d:
                        pool.wait_ge(S["prob"], d + 1)
                        pool.wait_ge(S["slot"], d + 1)
                        pool.wait_ge(S["tok"], 2 * d + 1)
                        pool.wait_ge(S["rec_m"], d + 1)
                        pool.wait_ge(S["ln2_rstd"], d + 1)
                        carried(pool)
                        for t in range(2):
                            pool.indirect_dma_start(records, bass.IndirectOffsetOnAxis(ap=idx[:, p, t:t + 1], axis=0), rec[:, p, t, :],
                                                    None, bounds_check=EXPERTS * REGION - 1, oob_is_err=False).then_inc(S[f"sc_done{p}"], 16)

                no_maxima()
                rstd_2()
                rstd_1()
                low(on_a, "t1", "s1", a, hn, "ln1_hn")
                low(on_d, "t3", "s3", d, xn, "xn")
                numbers()
                low(on_c, "t2", "s2", c, cn, "cn")
                rotated_low(0)
                counted()
                rotated_low(1)
                scattered()
                noted()
            run_images(pool, step)

        @block.scalar
        def _(act):
            def store(g, p, half):
                act.wait_ge(S["ho"], 2 * (g + 1))
                act.dma_start(hp[bass.ds(GT * g, GT), :].rearrange("(t p) d -> p t d", p=P), ho[:, p, :, :]).then_inc(S[f"hp_out{p}"], 16)

            def square(g, p, half):
                act.wait_ge(S[f"x_in{p}"], 16 * (half + 1))
                wait(act, S["sqs"], g)
                act.activation(xsq[:, :, :], xb[:, p, :, :], ACT.Square).then_inc(S["sq"], 1)
                if not (isinstance(g, int) and g == 0):
                    store(g - 1, 1 - p, None)
            groups(act, square)
            store(GROUPS - 1, (GROUPS - 1) % 2, None)
            act.wait_ge(S["mem"], 1)

            def step(s, p, half):
                (a, b, m, c, d), (on_a, on_b, on_m, on_c, on_d) = images_of(s)

                def high(on, name, x, n, src, rows):
                    if on:
                        act.wait_ge(S[rows], 2 * (n + 1))
                        wait(act, S[name + "_ps"], n)
                        act.activation(st[x][:, :, 0, 0:D], src[:, :, :], ACT.Copy).then_inc(S[x + "_hi"], 1)
                        act.activation(st[x][:, :, 1, D:256], src[:, :, P:D], ACT.Copy).then_inc(S[x + "_hi"], 1)

                def turned(on, name, n, q, half, used, times):
                    if on:
                        act.wait_ge(S[name + "_ps"], n + 1)
                        wait(act, S[used], times)
                        act.activation(tt[name][:, q, :, 0:TOK], half[:, :, 0:TOK], ACT.Copy).then_inc(S[name + "_cp"], 1)

                def exps(u):
                    if on_c:
                        g, kt = u // 2, u % 2
                        act.wait_ge(S["st_ps"], 12 * c + u + 1)
                        wait(act, S["ctx_ps"], 3 * (c - 1) + g // 2 + 1)
                        act.activation(pt[:, kt, 2 * g:2 * g + 2, :].rearrange("p c n -> p (c n)"), ps[:, 2 + u % 2, 0:2 * TOK],
                                       ACT.Exp, scale=HD ** -0.5).then_inc(S["exp"], 1)

                def context(g):
                    if on_c:
                        act.wait_ge(S["ctx_ps"], 3 * c + g + 1)
                        wait(act, S["ct_ps"], 2 * c)
                        act.activation(ctxt[:, g, 0:TOK], ps[:, 5, 0:TOK], ACT.Copy).then_inc(S["ctx_cp"], 1)

                def keys(u):
                    if on_m:
                        act.wait_ge(S["k_ps"], 2 * m + u + 1)
                        wait(act, S["st_ps"], 12 * (m - 1))
                        act.activation(kms[0:64, p, 3 * u:3 * u + 3, 0, 0:TOK], half6[0:64, 0:3, 0:TOK], ACT.Copy).then_inc(S["k_cpa"], 1)

                def values():
                    if on_m:
                        act.wait_ge(S["v_ps"], m + 1)
                        wait(act, S["ctx_ps"], 3 * (m - 1))
                        act.activation(va[:, p, :, :, 0:HD], ps[:, 4, 0:2 * D].rearrange("p (t h r) -> p t h r", t=2, r=HD),
                                       ACT.Copy).then_inc(S["v_cp"], 1)

                def rotated(t):
                    if on_b:
                        wait(act, S["q2_ps"], 2 * (b - 1))
                        act.wait_ge(S["rope"], 2 * b + t + 1)
                        act.activation(qks[:, 1 - p, t, :, 0, :], qk[:, t, :].rearrange("p (h r) -> p h r", r=HD), ACT.Copy).then_inc(S["qk_hi"], 1)

                def again(t):
                    if on_b:
                        for w in range(2):
                            act.activation(qks[:, 1 - p, t, HEADS * w:HEADS * (w + 1), 2 - w, :],
                                           qk[:, t, D * w:D * (w + 1)].rearrange("p (h r) -> p h r", r=HD), ACT.Copy).then_inc(S["qk_hi2"], 1)

                def chances():
                    if on_d:
                        act.wait_ge(S["ld"], d + 1)
                        act.activation(le[:, :, :], ld[:, :, :], ACT.Exp).then_inc(S["le"], 1)

                keys(0)
                values()
                exps(0)
                exps(1)
                keys(1)
                exps(2)
                exps(3)
                exps(4)
                exps(5)
                context(0)
                exps(6)
                exps(7)
                exps(8)
                exps(9)
                high(on_a, "t1", "s1", a, hn, "ln1_hn")
                context(1)
                exps(10)
                exps(11)
                high(on_d, "t3", "s3", d, xn, "xn")
                context(2)
                turned(on_d, "t3", d, 0, half7, "lg_ps", d)
                high(on_c, "t2", "s2", c, cn, "cn")
                rotated(0)
                again(0)
                rotated(1)
                turned(on_a, "t1", a, p, half6, "v_ps", a - 1)
                chances()
                turned(on_c, "t2", c, 0, half7, "wo_ps", c)
                again(1)
            run_images(act, step)

        @block.tensor
        def _(pe):
            pe.wait_ge(S["w_in"], 16)
            pe.wait_ge(S["b_in"], 16)
            n = KT * SHIFTS
            for k in range(n):
                last = pe.matmul(ps[:, 6, 0:D], gb[:, 1, k // SHIFTS, k % SHIFTS:k % SHIFTS + 1].broadcast_to([KP, P]),
                                 wr[:, k // SHIFTS, k % SHIFTS, :], start=(k == 0), stop=(k == n - 1))
            last.then_inc(S["bw"], 1)
            pe.wait_ge(S["wf"], KT)
            pe.wait_ge(S["ones"], 2)
            pe.wait_ge(S["c_in"], 16)
            for k in range(KT):
                last = pe.matmul(ps[:, 7, 0:D], ones[0:KP, :], wf[:, k, 0:D], start=(k == 0), stop=(k == KT - 1))
            last.then_inc(S["gs"], 1)

            def product(g, p, half):
                pe.wait_ge(S[f"x_in{p}"], 16 * (half + 1))
                wait(pe, S["ho"], 2 * (g - 1))
                for t in range(2):
                    for k in range(KT):
                        pe.matmul(ps[:, 2 * p + t, 0:D + 1], xb[:, p, k, t * P:(t + 1) * P], wf[:, k, :],
                                  start=(k == 0), stop=(k == KT - 1))
                    if t == 0:
                        pe.wait_ge(S["sqs"], g + 1)
                    pe.matmul(ps[:, 2 * p + t, D + 1:D + 2], xss[:, t * P:(t + 1) * P], cst[0:KP, C_MULT:C_MULT + 1],
                              start=True, stop=True).then_inc(S["acc"], 1)
            groups(pe, product)
            pe.wait_ge(S["mem"], 1)
            pe.wait_ge(S["wst"], 9)
            pe.wait_ge(S["ho"], 2 * GROUPS)

            def turn(name, half):
                a = st[name]
                for t in range(2):
                    for c, src in enumerate((a[:, t, 0, 0:P], a[:, t, 1, 0:P], a[:, t, 1, P:256], a[:, t, 0, P:256])):
                        last = pe.transpose(half[:, c, t * P:(t + 1) * P], src, idh[:, :])
                return last

            def stacked(o, x, q, t, c, n):
                for i, (a, w) in enumerate(((0, 0), (0, 1), (1, 0), (2, 2), (3, 3))):
                    last = pe.matmul(o, tt[x][:, q, a, t * P:(t + 1) * P], wst[:, w, c:c + n], start=(i == 0), stop=(i == 4))
                return last

            def pairs(q, w, u, half):
                for i in range(3):
                    h = HEADS * w + 2 * (3 * u + i)
                    for t in range(2):
                        last = pe.transpose(half[:, i, t * P:(t + 1) * P], qks[:, q, t, h:h + 2, :, :].rearrange("p h s r -> p (h s r)"), idh[:, :])
                return last

            def step(s, p, half):
                (a, b, m, c, d), (on_a, on_b, on_m, on_c, on_d) = images_of(s)

                def queries2(u):
                    if on_c:
                        pe.wait_ge(S["m_lo"], c + 1)
                        if u == 0:
                            wait(pe, S["t2_cp"], c)
                        else:
                            pe.wait_ge(S["q2_cp"], 2 * c + 1)
                        pairs(1 - p, 0, u, half7).then_inc(S["q2_ps"], 1)

                def scores_t(u):
                    if on_c:
                        g, kt = u // 2, u % 2
                        pe.wait_ge(S["q2_cp"], 2 * c + (1 if g < 3 else 2))
                        wait(pe, S["exp"], 12 * c + u - 1)
                        for i in range(2):
                            last = pe.matmul(ps[:, 2 + u % 2, i * TOK:(i + 1) * TOK], kms[:, 1 - p, g, i, kt * P:(kt + 1) * P],
                                             q2t[:, g, 0:TOK], start=True, stop=True)
                        last.then_inc(S["st_ps"], 1)

                def weighted(g):
                    if on_c:
                        pe.wait_ge(S["exp"], 12 * c + 4 * g + 4)
                        if g == 0:
                            pe.wait_ge(S["v_cp"], c + 1)
                            wait(pe, S["h2"], c)
                        else:
                            pe.wait_ge(S["ctx_cp"], 3 * c + g)
                        for kt in range(2):
                            n = P if kt == 0 else TOK - P
                            for i in range(4):
                                last = pe.matmul(ps[32 * i:32 * i + 32, 5, 0:TOK], va[0:n, 1 - p, kt, 4 * g + i, :], pt[0:n, kt, 4 * g + i, :],
                                                 start=(kt == 0), stop=(kt == 1), tile_position=(0, 32 * i))
                        last.then_inc(S["ctx_ps"], 1)

                def context(u):
                    if on_c:
                        pe.wait_ge(S["ctx_cp"], 3 * (c + 1))
                        if u == 1:
                            pe.wait_ge(S["cn"], 2 * c + 1)
                        for g in range(3):
                            last = pe.transpose(ps[:, 5, g * P:(g + 1) * P], ctxt[:, g, u * P:(u + 1) * P], ident)
                        last.then_inc(S["ct_ps"], 1)

                def context_turned():
                    if on_c:
                        pe.wait_ge(S["s2_lo"], c + 1)
                        wait(pe, S["t3_cp"], c)
                        turn("s2", half7).then_inc(S["t2_ps"], 1)

                def context_out():
                    if on_c:
                        pe.wait_ge(S["t2_cp"], c + 1)
                        pe.wait_ge(S["cn"], 2 * (c + 1))
                        for t in range(2):
                            last = stacked(ps[:, 5, t * D:(t + 1) * D], "t2", 0, t, W_OUT, D)
                        last.then_inc(S["wo_ps"], 1)

                def values():
                    if on_m:
                        pe.wait_ge(S["t1_cp"], m + 1)
                        wait(pe, S["slot_a"], d)
                        for t in range(2):
                            last = stacked(ps[:, 4, t * D:(t + 1) * D], "t1", p, t, 2 * D, D)
                        last.then_inc(S["v_ps"], 1)

                def keys(u):
                    if on_m:
                        if u == 0:
                            pe.wait_ge(S["qk_lo"], 4 * (m + 1))
                            pe.wait_ge(S["qk_hi2"], 4 * (m + 1))
                            pe.wait_ge(S["m_zero"], m + 1)
                            pe.wait_ge(S["t1_cp"], upto(s))
                        else:
                            pe.wait_ge(S["k_cpa"], 2 * m + 1)
                            pe.wait_ge(S["k_cpd"], 2 * m + 1)
                        pairs(p, 1, u, half6).then_inc(S["k_ps"], 1)

                def queries(u):
                    if on_m:
                        if u == 0:
                            pe.wait_ge(S["k_cpa"], 2 * m + 2)
                            pe.wait_ge(S["k_cpd"], 2 * m + 2)
                        else:
                            pe.wait_ge(S["q_cp"], 2 * m + 1)
                        pairs(p, 0, u, half6).then_inc(S["q_ps"], 1)

                def maxima(u):
                    if on_m:
                        q, g = u // 6, u % 6
                        pe.wait_ge(S["q_cp"], 2 * m + (1 if u < 3 else 2))
                        wait(pe, S["s_max"], 12 * m + u - 1)
                        pe.matmul(ps[:, u % 2, 0:2 * TOK], qt[:, g, q * P:(q + 1) * P], kms[:, p, g, :, 0:TOK], start=True, stop=True).then_inc(S["s_ps"], 1)

                def project(t):
                    if on_b:
                        pe.wait_ge(S["t1_cp"], b + 1)
                        if t == 0:
                            wait(pe, S["v_cp"], b)
                            wait(pe, S["slot_a"], d)
                        else:
                            pe.wait_ge(S["rope_b"], 2 * b + 1)
                        stacked(ps[:, 4, 0:2 * D], "t1", 1 - p, t, 0, 2 * D).then_inc(S["qk_ps"], 1)

                def arrive():
                    if on_a:
                        pe.wait_ge(S["s1_lo"], a + 1)
                        wait(pe, S["q_cp"], 2 * (a - 1))
                        turn("s1", half6).then_inc(S["t1_ps"], 1)

                def turned():
                    if on_d:
                        pe.wait_ge(S["s3_lo"], d + 1)
                        pe.wait_ge(S["q2_cp"], 2 * upto(d + 2))
                        pe.wait_ge(S["t2_cp"], d + 1)
                        turn("s3", half7).then_inc(S["t3_ps"], 1)

                def logits():
                    if on_d:
                        pe.wait_ge(S["t3_cp"], d + 1)
                        pe.wait_ge(S["rope_b"], 2 * upto(d + 4))
                        pe.wait_ge(S["v_cp"], upto(d + 3))
                        wait(pe, S["slot_a"], d)
                        for t in range(2):
                            last = stacked(ps[:, 4, t * EXPERTS:(t + 1) * EXPERTS], "t3", 0, t, W_SW, EXPERTS)
                        last.then_inc(S["lg_ps"], 1)

                def prefix():
                    if on_d:
                        pe.wait_ge(S["onehot"], d + 1)
                        pe.wait_ge(S["ld"], d + 1)
                        pe.wait_ge(S["cum"], 2 * d + 1)
                        for t in range(2):
                            o = ps[:, 4, 256 + t * EXPERTS:256 + (t + 1) * EXPERTS]
                            pe.matmul(o, trih[:, :], oh[:, p, t, :], start=True, stop=False)
                            last = pe.matmul(o, oneh[:, :], cum[:, p, t, :], start=False, stop=True)
                        last.then_inc(S["prefix"], 1)

                keys(0)
                queries2(0)
                values()
                scores_t(0)
                keys(1)
                scores_t(1)
                project(0)
                scores_t(2)
                scores_t(3)
                queries2(1)
                queries(0)
                scores_t(4)
                scores_t(5)
                weighted(0)
                scores_t(6)
                scores_t(7)
                project(1)
                scores_t(8)
                scores_t(9)
                weighted(1)
                scores_t(10)
                scores_t(11)
                queries(1)
                maxima(0)
                maxima(1)
                weighted(2)
                maxima(2)
                maxima(3)
                context(0)
                turned()
                maxima(4)
                maxima(5)
                context(1)
                logits()
                maxima(6)
                arrive()
                maxima(7)
                maxima(8)
                maxima(9)
                context_turned()
                maxima(10)
                maxima(11)
                prefix()
                context_out()
            run_images(pe, step)

        @block.vector
        def _(dve):
            dve.memset(ones[:, :], 1.0).then_inc(S["ones"], 1)
            dve.wait_ge(S["w_in"], 16)
            dve.wait_ge(S["g_in"], 16)
            for k in range(KT):
                wait(dve, S["wf"], k - 1)
                dve.tensor_tensor(wg[:, k % 2, :, :], wr[:, k, :, :], gb[:, 0, k, :].unsqueeze(2).broadcast_to([KP, SHIFTS, D]),
                                  ALU.mult).then_inc(S["wg"], 1)
                dve.wait_ge(S["wg"], k + 1)
                dve.tensor_reduce(wf[:, k, 0:D], wg[:, k % 2, :, :].rearrange("p s d -> p d s"), AX.X, ALU.add).then_inc(S["wf"], 1)
            dve.wait_ge(S["c_in"], 16)
            dve.tensor_copy(wf[:, :, D], cst[0:KP, C_MULT:C_MULT + 1].broadcast_to([KP, KT])).then_inc(S["ones"], 1)
            dve.wait_ge(S["bw"], 1)
            dve.wait_ge(S["tb_in"], 16)
            dve.tensor_tensor(brow[:, :], ps[:, 6, 0:D], brow0[:, :], ALU.add).then_inc(S["rows"], 1)
            dve.wait_ge(S["gs"], 1)
            dve.tensor_copy(gsum[:, :], ps[:, 7, 0:D]).then_inc(S["rows"], 1)
            dve.wait_ge(S["rows"], 2)

            def sums(g, p, half):
                dve.wait_ge(S["sq"], g + 1)
                wait(dve, S["acc"], 2 * g)
                dve.tensor_reduce(xss[:, :], xsq[:, :, :].rearrange("p k t -> p t k"), AX.X, ALU.add).then_inc(S["sqs"], 1)

            def finish(g, p, half):
                acc = ps[:, 2 * p:2 * p + 2, :]
                dve.wait_ge(S["acc"], 2 * (g + 1))
                dve.tensor_scalar(xst[:, p, 0, :], acc[:, :, D], -1.0 / TERMS, None, ALU.mult).then_inc(S["stat"], 1)
                dve.tensor_scalar(xst[:, p, 1, :], acc[:, :, D + 1], 1.0 / TERMS, None, ALU.mult).then_inc(S["stat"], 1)
                dve.wait_ge(S["stat"], 3 * g + 2)
                dve.tensor_tensor(xst[:, p, 2, :], xst[:, p, 0, :], xst[:, p, 0, :], ALU.mult).then_inc(S["stat"], 1)
                dve.wait_ge(S["stat"], 3 * g + 3)
                dve.scalar_tensor_tensor(out=xst[:, p, 2, :], in0=xst[:, p, 1, :], scalar=EPS, in1=xst[:, p, 2, :],
                                         op0=ALU.add, op1=ALU.subtract).then_inc(S["var"], 1)
                for t in range(2):
                    dve.scalar_tensor_tensor(out=hm[:, t, :], in0=gsum[:, :], scalar=xst[:, p, 0, t:t + 1], in1=acc[:, t, 0:D],
                                             op0=ALU.mult, op1=ALU.add).then_inc(S["hm"], 1)
                dve.wait_ge(S["rstd"], g + 1)
                wait(dve, S[f"hp_out{p}"], 16 * half)
                for t in range(2):
                    dve.wait_ge(S["hm"], 2 * g + t + 1)
                    dve.scalar_tensor_tensor(out=ho[:, p, t, :], in0=hm[:, t, :], scalar=xst[:, p, 3, t:t + 1], in1=brow[:, :],
                                             op0=ALU.mult, op1=ALU.add).then_inc(S["ho"], 1)

            def step(g, p, half):
                sums(g, p, half)
                if not (isinstance(g, int) and g == 0):
                    finish(g - 1, 1 - p, half - 1 if p == 0 else half)
            groups(dve, step)
            finish(GROUPS - 1, 0, GROUPS // 2)

            dve.memset(wstage[:, 2, :], 0.0).then_inc(S["wz"], 1)
            dve.tensor_copy(idh[:, :], ident).then_inc(S["wst"], 1)
            dve.tensor_copy(trih[:, :], cst[:, C_TRI:C_TRI + P]).then_inc(S["wst"], 1)
            dve.wait_ge(S["ws_in"], 16 * 15)
            dve.tensor_copy(wst[:, 0, :], wstage[:, 0, :]).then_inc(S["wst"], 1)
            dve.tensor_copy(wst[:, 2, :], wstage[:, 1, :]).then_inc(S["wst"], 1)
            dve.tensor_copy(wst[64:P, 3, :], wstage[64:P, 2, :]).then_inc(S["wst"], 1)
            dve.wait_ge(S["wst"], 5)
            dve.tensor_tensor(wst[:, 1, :], wstage[:, 0, :], wst[:, 0, :], ALU.subtract).then_inc(S["wst"], 1)
            dve.tensor_tensor(wst[0:64, 3, :], wstage[0:64, 1, :], wst[0:64, 2, :], ALU.subtract).then_inc(S["wst"], 1)
            dve.tensor_tensor(wst[96:P, 3, :], wstage[96:P, 2, :], wst[96:P, 3, :], ALU.subtract).then_inc(S["wst"], 1)
            dve.wait_ge(S["mem"], 1)
            dve.wait_ge(S["cls_in"], 64)
            dve.wait_ge(S["wst"], 8)
            dve.tensor_copy(code[:, 0, :], cst[:, C_VALID:C_VALID + 2]).then_inc(S["wst"], 1)

            class Norm:

                def __init__(self, x, i, n, name):
                    self.x, self.i, self.n, self.name = x, i, n, name

                def sums(self):
                    for t in range(2):
                        dve.bn_stats(mvs[:, self.i, t, :], self.x(t)).then_inc(S[self.name + "_st"], 1)

                def mean(self):
                    dve.wait_ge(S[self.name + "_st"], 2 * self.n)
                    carried(dve)
                    for t in range(2):
                        dve.bn_aggr(mv[:, self.i, t, :], mvs[:, self.i, t, :]).then_inc(S[self.name + "_mv"], 1)

                def variance(self):
                    dve.wait_ge(S[self.name + "_mv"], 2 * self.n)
                    dve.tensor_scalar(mve[:, self.i, :], mv[:, self.i, :, 1], EPS, None, ALU.add).then_inc(S[self.name + "_var"], 1)

            def step(s, p, half):
                (a, b, m, c, d), (on_a, on_b, on_m, on_c, on_d) = images_of(s)
                norm1 = Norm(lambda t: hx[:, p, t, :], 0, s + 1, "ln1")
                norm2 = Norm(lambda t: rec[:, p, t, 0:D], 1, d + 1, "ln2")

                def queries(u, second):
                    if on_c if second else on_m:
                        n, sem, dst = (c, "q2", q2t) if second else (m, "q", qt)
                        dve.wait_ge(S[sem + "_ps"], 2 * n + u + 1)
                        wait(dve, S["st_ps" if second else "s_ps"], 12 * n)
                        dve.tensor_copy(dst[:, 3 * u:3 * u + 3, 0:TOK], (half7 if second else half6)[:, 0:3, 0:TOK]).then_inc(S[sem + "_cp"], 1)

                def keys(u):
                    if on_m:
                        dve.wait_ge(S["k_ps"], 2 * m + u + 1)
                        wait(dve, S["st_ps"], 12 * (m - 1))
                        dve.tensor_copy(kms[64:P, p, 3 * u:3 * u + 3, 1, 0:TOK], half6[64:P, 0:3, 0:TOK]).then_inc(S["k_cpd"], 1)

                def largest(u):
                    if on_m:
                        q, g = u // 6, u % 6
                        dve.wait_ge(S["s_ps"], 12 * m + u + 1)
                        dve.tensor_reduce(mx[:, q, 2 * g:2 * g + 2], ps[:, u % 2, 0:2 * TOK].rearrange("p (b n) -> p b n", b=2), AX.X, ALU.max).then_inc(S["s_max"], 1)

                def rotate(t):
                    if on_b:
                        dve.wait_ge(S["qk_ps"], 2 * b + t + 1)
                        dve.tensor_tensor(ra[:, t, :], ps[:, 4, 0:2 * D], cst[:, C_COS + t * 2 * D:C_COS + (t + 1) * 2 * D], ALU.mult).then_inc(S["rope_a"], 1)
                        dve.tensor_tensor(rb[:, t, :].rearrange("p (a b) -> p a b", b=2),
                                          ps[:, 4, 0:2 * D].rearrange("p (a b) -> p a b", b=2)[:, :, ::-1],
                                          cst[:, C_SIN + t * 2 * D:C_SIN + (t + 1) * 2 * D].rearrange("p (a b) -> p a b", b=2), ALU.mult).then_inc(S["rope_b"], 1)

                def rotated(t):
                    if on_b:
                        dve.wait_ge(S["rope_a"], 2 * b + t + 1)
                        dve.wait_ge(S["rope_b"], 2 * b + t + 1)
                        wait(dve, S["qk_lo"], 4 * b)
                        wait(dve, S["qk_hi2"], 4 * b)
                        dve.tensor_tensor(qk[:, t, :], ra[:, t, :], rb[:, t, :], ALU.add).then_inc(S["rope"], 1)

                tok = ps[:, 5, 0:3 * P].rearrange("p (h r) -> p h r", r=32)

                def sums(u):
                    if on_c:
                        dve.wait_ge(S["ct_ps"], 2 * c + u + 1)
                        dve.reciprocal(rc[:, u, :], tok[:, :, HD]).then_inc(S["den"], 1)

                def divided(u):
                    if on_c:
                        dve.wait_ge(S["den"], 2 * c + u + 1)
                        wait(dve, S["s2_hi"], 2 * c)
                        wait(dve, S["s2_lo"], c)
                        dve.tensor_tensor(cn[:, u, :].rearrange("p (h r) -> p h r", r=HD), tok[:, :, 0:HD],
                                          rc[:, u, :].unsqueeze(2).broadcast_to([P, HEADS, HD]), ALU.mult).then_inc(S["cn"], 1)

                lg = ps[:, 4, 0:2 * EXPERTS].rearrange("p (t e) -> p t e", t=2)
                iota = cst[:, C_IOTA:C_IOTA + EXPERTS].unsqueeze(1).broadcast_to([P, 2, EXPERTS])
                wide = lambda x: x.unsqueeze(2).broadcast_to([P, 2, EXPERTS])

                def route(n):
                    if not on_d:
                        return
                    if n == 0:
                        dve.wait_ge(S["lg_ps"], d + 1)
                        dve.tensor_reduce(lmx[:, :], lg, AX.X, ALU.max).then_inc(S["lmx"], 1)
                    elif n == 1:
                        dve.wait_ge(S["lmx"], d + 1)
                        wait(dve, S["le"], d)
                        dve.tensor_tensor(ld[:, :, :], lg, wide(lmx[:, :]), ALU.subtract).then_inc(S["ld"], 1)
                    elif n == 2:
                        dve.wait_ge(S["ld"], d + 1)
                        dve.scalar_tensor_tensor(out=c8[:, :, :], in0=ld[:, :, :], scalar=0.0, in1=iota, op0=ALU.is_equal, op1=ALU.mult).then_inc(S["c8"], 1)
                    elif n == 3:
                        dve.wait_ge(S["c8"], d + 1)
                        dve.tensor_reduce(lsum[:, :], c8[:, :, :], AX.X, ALU.max).then_inc(S["cm"], 1)
                    elif n == 4:
                        dve.wait_ge(S["cm"], d + 1)
                        wait(dve, S["pall"], 2 * d)
                        dve.tensor_tensor(code[:, 1, :], lsum[:, :], code[:, 0, :], ALU.mult).then_inc(S["code"], 1)
                    elif n == 5:
                        dve.wait_ge(S["code"], d + 1)
                        wait(dve, S["cum"], 2 * (d - 1))
                        dve.tensor_tensor(oh[:, p, :, :], iota, wide(code[:, 1, :]), ALU.is_equal).then_inc(S["onehot"], 1)
                    elif n == 6:
                        dve.wait_ge(S["le"], d + 1)
                        dve.tensor_reduce(lmx[:, :], le[:, :, :], AX.X, ALU.add).then_inc(S["lsum"], 1)
                    elif n == 7:
                        dve.wait_ge(S["lsum"], d + 1)
                        dve.reciprocal(rec[:, p, :, D + 2], lmx[:, :]).then_inc(S["prob"], 1)
                    elif n == 8:
                        dve.wait_ge(S["prefix"], d + 1)
                        dve.tensor_tensor(sl[:, :, :], ps[:, 4, 256:256 + 2 * EXPERTS].rearrange("p (t e) -> p t e", t=2),
                                          cst[:, C_SLOT:C_SLOT + EXPERTS].unsqueeze(1).broadcast_to([P, 2, EXPERTS]), ALU.add).then_inc(S["slot_a"], 1)
                    elif n == 9:
                        dve.wait_ge(S["slot_a"], d + 1)
                        dve.tensor_tensor(sl2[:, :, :], sl[:, :, :], oh[:, p, :, :], ALU.mult).then_inc(S["slot_b"], 1)
                    elif n == 10:
                        dve.wait_ge(S["slot_b"], d + 1)
                        dve.tensor_reduce(slot[:, :], sl2[:, :, :], AX.X, ALU.add).then_inc(S["slot_c"], 1)
                    elif n == 11:
                        dve.wait_ge(S["slot_c"], d + 1)
                        dve.tensor_tensor(idx[:, p, :], slot[:, :], cst[:, C_FAR:C_FAR + 2], ALU.add).then_inc(S["slot"], 1)

                def sums1():
                    if on_a:
                        dve.wait_ge(S[f"h_in{p}"], 32 * (half + 1))
                        norm1.sums()

                def mean1():
                    if on_a:
                        norm1.mean()

                def variance1():
                    if on_a:
                        norm1.variance()

                def normal1():
                    if on_a:
                        dve.wait_ge(S["ln1_rstd"], a + 1)
                        wait(dve, S["s1_hi"], 2 * a)
                        wait(dve, S["s1_lo"], a)
                        for t in range(2):
                            dve.tensor_scalar(hn[:, t, :], hx[:, p, t, :], mv[:, 0, t, 0:1], rstd1[:, t:t + 1], ALU.subtract, ALU.mult).then_inc(S["ln1_hn"], 1)

                def added():
                    if on_d:
                        dve.wait_ge(S["wo_ps"], d + 1)
                        dve.wait_ge(S[f"hr_in{p}"], 32 * (half - 1))
                        wait(dve, S[f"sc_done{p}"], 32 * (half - 2))
                        dve.tensor_tensor(rec[:, p, :, 0:D], ps[:, 5, 0:2 * D].rearrange("p (t d) -> p t d", t=2), hr[:, p, :, :], ALU.add).then_inc(S["h2"], 1)

                def sums2():
                    if on_d:
                        dve.wait_ge(S["h2"], d + 1)
                        wait(dve, S["rec_m"], d)
                        norm2.sums()

                def mean2():
                    if on_d:
                        norm2.mean()

                def variance2():
                    if on_d:
                        norm2.variance()

                def normal2():
                    if on_d:
                        dve.wait_ge(S["ln2_rstd"], d + 1)
                        wait(dve, S["s3_hi"], 2 * d)
                        wait(dve, S["s3_lo"], d)
                        for t in range(2):
                            dve.tensor_scalar(xn[:, t, :], rec[:, p, t, 0:D], mv[:, 1, t, 0:1], rec[:, p, t, D + 1:D + 2], ALU.subtract, ALU.mult).then_inc(S["xn"], 1)

                def minus_maxima():
                    if on_m:
                        dve.wait_ge(S["s_max"], 12 * (m + 1))
                        dve.wait_ge(S["q_ps"], 2 * (m + 1))
                        dve.tensor_scalar(qks[:, p, :, 0:HEADS, 3, 0], mx[:, :, :], -1.0, None, ALU.mult).then_inc(S["m_hi"], 1)
                        dve.wait_ge(S["m_hi"], m + 1)
                        dve.scalar_tensor_tensor(out=qks[:, p, :, 0:HEADS, 3, 1], in0=mx[:, :, :], scalar=-1.0, in1=qks[:, p, :, 0:HEADS, 3, 0],
                                                 op0=ALU.mult, op1=ALU.subtract).then_inc(S["m_lo"], 1)

                added()
                keys(0)
                queries(0, True)
                sums1()
                sums2()
                mean2()
                keys(1)
                mean1()
                variance2()
                rotate(0)
                variance1()
                queries(0, False)
                queries(1, True)
                normal1()
                rotate(1)
                rotated(0)
                normal2()
                rotated(1)
                largest(0)
                queries(1, False)
                largest(1)
                largest(2)
                largest(3)
                sums(0)
                divided(0)
                largest(4)
                sums(1)
                divided(1)
                route(0)
                largest(5)
                largest(6)
                route(1)
                route(2)
                largest(7)
                route(3)
                largest(8)
                route(4)
                largest(9)
                route(5)
                route(6)
                largest(10)
                largest(11)
                route(7)
                route(8)
                minus_maxima()
                route(9)
                route(10)
                route(11)
            run_images(dve, step)

        def early_done(eng):
            eng.wait_ge(S["early"], 4)

        def run_tiles(eng, step):
            for s in range(8):
                step(s, s % 2, s % 4, s // 4)
            whole = (TILES - 8) // 4
            with eng.Fori(0, whole) as i:
                for r in range(4):
                    step(4 * i + (8 + r), r % 2, r, i + 2)
            for s in range(8 + 4 * whole, TILES + 3):
                step(s, s % 2, s % 4, s // 4)

        def within(s, back):
            return not isinstance(s, int) or 0 <= s - back < TILES

        @block.sync
        def _(sp):
            early_done(sp)
            sp.dma_start(c3[:, :], consts3).then_inc(S["c3_in"], 16)
            sp.wait_ge(S["f_zero"], 2)
            for r in (0, 32):
                sp.dma_start(fb2[r:r + 1, :, :], b2.rearrange("(a e) d -> a e d", a=1)).then_inc(S["b2_in"], 16)

            def weights(e):
                q = e % 2
                wait(sp, S["f_hi"], 4 * (e - 1))
                wait(sp, S["f_lo"], 4 * (e - 1))
                sp.dma_start(f1[:, q, 0, :], w1[e, 0:P, :]).then_inc(S[f"f_in{q}"], 16)
                for r in (0, 64):
                    sp.dma_start(f1[r:r + 64, q, 1, :], w1[e, P:D, :]).then_inc(S[f"f_in{q}"], 16)
                for r in (64, 96):
                    sp.dma_start(f1[r:r + 1, q, 2, :], b1[e:e + 1, :]).then_inc(S[f"f_in{q}"], 16)
                sp.dma_start(f2[:, q, :, :], w2[e].rearrange("(f p) d -> p f d", p=P)).then_inc(S[f"f_in{q}"], 16)
            weights(0)
            weights(1)
            sp.wait_ge(S["plan"], PLAN["prow"])
            sp.dma_start(pflat.rearrange("a i n -> i a n"), prow[:, :, :]).then_inc(S["pf_out"], 16)
            sp.wait_ge(S["pf_out"], 16)
            for e in range(EXPERTS):
                sp.dma_start(eb[16 * e:16 * e + 16, :, :], pflat.rearrange("a i n -> a (i n)").rearrange("a (c n) -> c a n", c=16)).then_inc(S["eb_in"], 16)
            for e in range(2, EXPERTS):
                weights(e)
            sp.wait_ge(S["padrec"], 1)
            sp.dma_start(records[DUMMY:DUMMY + P, :], padrec[:, :]).then_inc(S["pad_out"], 16)
            for q in range(2):
                sp.wait_ge(S[f"sc_done{q}"], 16 * IMAGES)
            sp.wait_ge(S["tail_out"], 16 * EXPERTS)
            sp.wait_ge(S["pad_out"], 16)
            sp.wait_ge(S["plan"], PLAN["tables"])

            def step(s, p, r, q):
                if within(s, 0):
                    row = sp.value_load(rowt[0:1, bass.ds(s, 1)], min_val=0, max_val=DUMMY)
                    wait(sp, S[f"y_out{r}"], 16 * q)
                    sp.dma_start(xr[:, r, :], records[bass.ds(row, P), :]).then_inc(S[f"x4_in{r}"], 16)
            run_tiles(sp, step)
            for r in range(4):
                sp.wait_ge(S[f"y_out{r}"], 16 * len(range(r, TILES, 4)))

        @block.gpsimd
        def _(pool):
            for q in range(2):
                pool.wait_ge(S[f"sc_done{q}"], 16 * IMAGES)
            pool.drain().then_inc(S["early"], 1)
            early_done(pool)
            for a in (f1[:, 0, 2, :], f1[:, 1, 2, :]):
                pool.memset(a, 0.0).then_inc(S["f_zero1"], 1)
            pool.memset(fb2[:, :, :], 0.0).then_inc(S["f_zero"], 1)
            pool.wait_ge(S["f_zero1"], 2)
            pool.wait_ge(S["f_zero"], 1)
            pool.memset(padrec[:, :], 0.0).then_inc(S["f_zero"], 1)
            pool.memset(st4[:, :, :, :], 0.0).then_inc(S["st4_zero"], 1)
            pool.wait_ge(S["f_zero"], 2)
            pool.wait_ge(S["st4_zero"], 1)
            pool.memset(st4[:, :, 0, D:256:32], 1.0).then_inc(S["st4"], 1)
            pool.wait_ge(S["c3_in"], 16)
            pool.tensor_copy(padrec[:, REC - 1:REC].bitcast(U32), c3[:, K_PAD:K_PAD + 1]).then_inc(S["padrec"], 1)

            def lows(e):
                q = e % 2
                pool.wait_ge(S["f_hi"], 4 * (e + 1))
                hi1, hi2 = w1s[:, e, :], w2s[:, e, :].rearrange("p (f s d) -> p f s d", f=FT, s=2)
                pool.tensor_tensor(hi1[:, FF:2 * FF], f1[:, q, 0, :], hi1[:, 0:FF], ALU.subtract).then_inc(S["f_lo"], 1)
                pool.wait_ge(S["f_lo"], 4 * e + 1)
                pool.tensor_tensor(hi1[0:64, 3 * FF:4 * FF], f1[0:64, q, 1, :], hi1[0:64, 2 * FF:3 * FF], ALU.subtract).then_inc(S["f_lo"], 1)
                pool.wait_ge(S["f_lo"], 4 * e + 2)
                pool.tensor_tensor(hi1[96:P, 3 * FF:4 * FF], f1[96:P, q, 2, :], hi1[96:P, 3 * FF:4 * FF], ALU.subtract).then_inc(S["f_lo"], 1)
                pool.wait_ge(S["f_lo"], 4 * e + 3)
                pool.tensor_tensor(hi2[:, :, 1, :], f2[:, q, :, :], hi2[:, :, 0, :], ALU.subtract).then_inc(S["f_lo"], 1)
            pool.wait_ge(S["b2_hi"], 1)
            pool.wait_ge(S["padrec"], 1)
            pool.tensor_tensor(b2s[32:64, :, :], fb2[32:64, :, :], b2s[32:64, :, :], ALU.subtract).then_inc(S["b2_lo"], 1)
            pool.wait_ge(S["b2_lo"], 1)
            lows(0)
            pool.wait_ge(S["plan"], PLAN["tails"])
            pool.wait_ge(S["padrec"], 1)
            for e in range(EXPERTS):
                pool.indirect_dma_start(records, bass.IndirectOffsetOnAxis(ap=tails[:, e:e + 1], axis=0), padrec[:, :],
                                        None, bounds_check=DUMMY - 1, oob_is_err=False).then_inc(S["tail_out"], 16)
            pool.wait_ge(S["tail_out"], 16 * EXPERTS)
            for e in range(1, EXPERTS):
                lows(e)
            pool.wait_ge(S["plan"], PLAN["tables"])

            def step(s, p, r, q):
                if within(s, 0):
                    x, v = xr[:, r, :], small[:, p, :]
                    prob, n = x[:, D + 2:D + 3], bass.ds(s, 1)
                    col = lambda i: v[:, i:i + 1]
                    pool.wait_ge(S[f"x4_in{r}"], 16 * (q + 1))
                    carried(pool)
                    pool.tensor_copy(small[:, p, 4:6], tct[:, :, n].rearrange("p a n -> p (a n)")).then_inc(S["kept"], 1)
                    pool.tensor_copy(col(0), x[:, REC - 1:REC].bitcast(U32)).then_inc(S["kept"], 1)
                    pool.wait_ge(S["kept"], 7 * s + 1)
                    carried(pool)
                    pool.tensor_scalar(col(1), col(4), prob, None, ALU.is_equal).then_inc(S["kept"], 1)
                    pool.wait_ge(S["kept"], 7 * s + 2)
                    pool.wait_ge(S["kept"], 7 * s + 3)
                    carried(pool)
                    pool.tensor_scalar(col(2), col(5), col(0), col(1), ALU.is_ge, ALU.mult).then_inc(S["kept"], 1)
                    pool.wait_ge(S["kept"], 7 * s + 4)
                    carried(pool)
                    pool.tensor_scalar(col(3), col(4), prob, col(2), ALU.is_lt, ALU.add).then_inc(S["kept"], 1)
                    pool.wait_ge(S["kept"], 7 * s + 5)
                    wait(pool, S["fin"], s - 3)
                    pool.tensor_tensor(keepp[:, r, 0:1], col(3), prob, ALU.mult).then_inc(S["kept"], 1)
                    pool.wait_ge(S["kept"], 7 * s + 6)
                    pool.tensor_tensor(keepp[:, r, 1:2], prob, keepp[:, r, 0:1], ALU.subtract).then_inc(S["kept"], 1)
                if within(s, 3):
                    o = (r + 1) % 4
                    pool.wait_ge(S["fin"], s - 2)
                    carried(pool)
                    pool.indirect_dma_start(out, bass.IndirectOffsetOnAxis(ap=xr[:, o, REC - 1:REC].bitcast(U32), axis=0), orow[:, 1 - p, :],
                                            None, bounds_check=NTOK - 1, oob_is_err=False).then_inc(S[f"y_out{o}"], 16)
            run_tiles(pool, step)

        @block.scalar
        def _(act):
            act.drain().then_inc(S["early"], 1)
            early_done(act)
            act.wait_ge(S["b2_in"], 32)
            act.activation(b2s[:, :, :], fb2[:, :, :], ACT.Copy).then_inc(S["b2_hi"], 1)
            for e in range(EXPERTS):
                q = e % 2
                act.wait_ge(S[f"f_in{q}"], 96 * (e // 2 + 1))
                hi1, hi2 = w1s[:, e, :], w2s[:, e, :].rearrange("p (f s d) -> p f s d", f=FT, s=2)
                act.activation(hi1[:, 0:FF], f1[:, q, 0, :], ACT.Copy).then_inc(S["f_hi"], 1)
                act.activation(hi1[:, 2 * FF:3 * FF], f1[:, q, 1, :], ACT.Copy).then_inc(S["f_hi"], 1)
                act.activation(hi1[64:P, 3 * FF:4 * FF], f1[64:P, q, 2, :], ACT.Copy).then_inc(S["f_hi"], 1)
                act.activation(hi2[:, :, 0, :], f2[:, q, :, :], ACT.Copy).then_inc(S["f_hi"], 1)
            act.wait_ge(S["st4"], 1)

            def step(s, p, r, q):
                def gelu(half):
                    act.wait_ge(S["h_ps"], 2 * s - 1 + half)
                    wait(act, S["hl"], 2 * (s - 3) + 2)
                    act.activation(hf[:, 1 - p, 3 * P * half:3 * P * (half + 1)], ps[:, 2 + 2 * (1 - p) + half, 0:3 * P], ACT.Gelu).then_inc(S["hf"], 1)

                def high(half):
                    act.wait_ge(S["hf"], 2 * s - 1 + half)
                    wait(act, S["y_ps"], s - 2)
                    act.activation(hh[:, 1 - p, 3 * P * half:3 * P * (half + 1)], hf[:, 1 - p, 3 * P * half:3 * P * (half + 1)], ACT.Copy).then_inc(S["hh"], 1)

                if within(s, 1):
                    gelu(0)
                if within(s, 0):
                    act.wait_ge(S["xn4"], s + 1)
                    wait(act, S["t4_ps"], s - 1)
                    act.activation(st4[:, p, 0, 0:D], xn4[:, p, :], ACT.Copy).then_inc(S["x_hi"], 1)
                    act.activation(st4[:, p, 1, D:256], xn4[:, p, P:D], ACT.Copy).then_inc(S["x_hi"], 1)
                if within(s, 1):
                    high(0)
                    gelu(1)
                    high(1)
                if within(s, 0):
                    act.wait_ge(S["t4_ps"], s + 1)
                    wait(act, S["h_ps"], 2 * (s - 1))
                    act.activation(xt4[:, p, :, :], ps[:, p, 0:256].bitcast(F16).rearrange("p (c n) -> p c n", c=4), ACT.Copy).then_inc(S["xt4"], 1)
            run_tiles(act, step)

        @block.tensor
        def _(pe):
            pe.drain().then_inc(S["early"], 1)
            early_done(pe)
            pe.wait_ge(S["pall"], 2 * IMAGES)
            for a in range(2):
                for t in range(2):
                    pe.transpose(ps[0:IMAGES, a, t * P:(t + 1) * P], pall[:, a, t, :], ident).then_inc(S["pt_ps"], 1)
            pe.wait_ge(S["c3_in"], 16)
            total = lambda o, w, x, name: pe.matmul(o, w, x, start=True, stop=True).then_inc(S[name], 1)
            block_sum = c3[:, K_BLOCK:K_BLOCK + P]
            pe.wait_ge(S["plan"], PLAN["n_cnt"])
            total(ps[:, 3, 0:1], block_sum, cols["cnt"][:, :], "sums")
            pe.wait_ge(S["plan"], PLAN["ntile"])
            total(ps[:, 3, 1:2], c3[:, K_UPTO:K_UPTO + P], cols["ntile"][:, :], "sums")
            pe.wait_ge(S["plan"], PLAN["onef"])
            pe.wait_ge(S["plan"], PLAN["dn"])
            total(ps[:, 4, 0:EXPERTS], onef[:, :], dn[:, :], "sums")
            with pe.Fori(0, STEPS) as i:
                pe.wait_ge(S["count"], i + 1)
                total(ps[:, 2, 0:1], block_sum, cols["cnt"][:, :], "sum_ps")
            pe.wait_ge(S["plan"], PLAN["g_cnt"])
            total(ps[:, 3, 2:3], block_sum, cols["cnt"][:, :], "sums")
            pe.wait_ge(S["plan"], PLAN["tied"])
            total(ps[:, 4, 8:9], c3[:, K_BEFORE:K_BEFORE + P], tied[:, CHUNK - 1:CHUNK], "sums")
            pe.wait_ge(S["plan"], PLAN["cut_cnt"])
            total(ps[:, 3, 3:4], block_sum, cols["cutc"][:, :], "sums")
            pe.wait_ge(S["plan"], PLAN["vals_all"])
            total(ps[:, 5, 0:4 * TILES], onef[:, :], vals[:, :, :].rearrange("p a n -> p (a n)"), "sums")
            pe.wait_ge(S["plan"], PLAN["tables"])
            pe.wait_ge(S["f_hi"], 4 * EXPERTS)
            pe.wait_ge(S["f_lo"], 4 * EXPERTS)
            pe.wait_ge(S["b2_lo"], 1)

            def step(s, p, r, q):
                if within(s, 1):
                    e = pe.value_load(expt[0:1, bass.ds(s - 1, 1)], min_val=0, max_val=EXPERTS - 1)
                    pe.wait_ge(S["xt4"], s)
                    wait(pe, S["hf"], 2 * (s - 3) + 2)
                    for f in range(FT):
                        for i, (a, w) in enumerate(((0, 0), (0, 1), (1, 0), (2, 2), (3, 3))):
                            last = pe.matmul(ps[:, 2 + 2 * (1 - p) + f // 3, (f % 3) * P:(f % 3 + 1) * P],
                                             w1s[:, bass.ds(e, 1), w * FF + f * P:w * FF + (f + 1) * P], xt4[:, 1 - p, a, :],
                                             start=(i == 0), stop=(i == 4))
                        if f % 3 == 2:
                            last.then_inc(S["h_ps"], 1)
                if within(s, 0):
                    pe.wait_ge(S["x_lo"], s + 1)
                    pe.wait_ge(S["x_hi"], 2 * (s + 1))
                    wait(pe, S["xt4"], s - 1)
                    o = ps[:, p, 0:256].bitcast(F16)
                    for c, src in enumerate((st4[:, p, 0, 0:P], st4[:, p, 1, 0:P], st4[:, p, 1, P:256], st4[:, p, 0, P:256])):
                        last = pe.transpose(o[:, c * P:(c + 1) * P], src, idh[:, :])
                    last.then_inc(S["t4_ps"], 1)
                if within(s, 2):
                    e = pe.value_load(expt[0:1, bass.ds(s - 2, 1)], min_val=0, max_val=EXPERTS - 1)
                    pe.wait_ge(S["hh"], 2 * (s - 1))
                    pe.wait_ge(S["hl"], 2 * (s - 1))
                    wait(pe, S["fin"], s - 3)
                    y = ps[:, 6 + p, 0:D]
                    pe.matmul(y, oneh[:, :], b2s[:, bass.ds(e, 1), :], start=True, stop=False)
                    for f in range(FT):
                        for i, (a, w) in enumerate(((hh, 0), (hh, 1), (hl, 0))):
                            last = pe.matmul(y, a[:, p, f * P:(f + 1) * P], w2s[:, bass.ds(e, 1), (2 * f + w) * D:(2 * f + w + 1) * D],
                                             start=False, stop=(f == FT - 1 and i == 2))
                    last.then_inc(S["y_ps"], 1)
            run_tiles(pe, step)

        @block.vector
        def _(dve):
            dve.drain().then_inc(S["early"], 1)
            early_done(dve)
            dve.memset(onef[:, :], 1.0).then_inc(S["plan"], 1)
            dve.memset(one788[:, :], 1.0).then_inc(S["plan"], 1)
            dve.memset(cols["lo"][:, :], 0.0).then_inc(S["lo"], 1)
            dve.memset(cols["stepc"][:, :], 1.0).then_inc(S["halved"], 1)
            dve.memset(cols["cand"][:, :], 1.0).then_inc(S["cand"], 1)
            for a in range(2):
                for n, (to, at, length) in enumerate(((1, 0, P), (1 + P, P, REST), (0, P + REST, 1))):
                    dve.wait_ge(S["pt_ps"], 2 * a + 2)
                    dve.tensor_copy(prow[:, a, to:to + length], ps[0:IMAGES, a, at:at + length]).then_inc(S["plan"], 1)
            C = {n: c[:, :] for n, c in cols.items()}
            first = c3[:, K_FIRST:K_FIRST + 1]
            iota, iota128 = c3[:, K_IOTA:K_IOTA + P], c3[:, K_IOTA128:K_IOTA128 + P]
            dve.wait_ge(S["c3_in"], 16)
            dve.wait_ge(S["eb_in"], 16 * EXPERTS)
            dve.scalar_tensor_tensor(out=pe_e[:, :], in0=eb[:, 1, :], scalar=c3[:, K_CODE:K_CODE + 1], in1=eb[:, 0, :],
                                     op0=ALU.is_equal, op1=ALU.mult).then_inc(S["plan"], 1)
            dve.wait_ge(S["plan"], PLAN["pe_e"])

            def count(src, bound, op, acc, name, n=CHUNK):
                dve.tensor_scalar(scr[:, 0:n], src, bound, None, op, ALU.add, accum_out=C[acc]).then_inc(S[name], 1)
            count(pe_e[:, :], 0.0, ALU.is_gt, "cnt", "plan")
            dve.wait_ge(S["sums"], SUMS["n"])
            dve.tensor_copy(C["n_e"], ps[:, 3, 0:1]).then_inc(S["plan"], 1)
            dve.wait_ge(S["plan"], PLAN["n_e"])
            dve.wait_ge(S["plan"], PLAN["n_cnt"])
            count(iota128, C["n_e"], ALU.is_lt, "ntile", "plan", P)
            dve.tensor_scalar(dn[:, :], c3[:, K_SEL:K_SEL + EXPERTS], C["n_e"], None, ALU.mult).then_inc(S["plan"], 1)
            dve.wait_ge(S["sums"], SUMS["end"])
            dve.wait_ge(S["plan"], PLAN["ntile"])
            dve.tensor_copy(C["end"], ps[:, 3, 1:2]).then_inc(S["plan"], 1)
            dve.wait_ge(S["sums"], SUMS["tail"])
            dve.tensor_tensor(tails[:, :], ps[:, 4, 0:EXPERTS], c3[:, K_TAIL:K_TAIL + EXPERTS], ALU.add).then_inc(S["plan"], 1)
            dve.wait_ge(S["plan"], PLAN["end"])
            dve.tensor_tensor(C["start"], C["end"], C["ntile"], ALU.subtract).then_inc(S["plan"], 1)
            with dve.Fori(0, STEPS) as i:
                dve.wait_ge(S["cand"], i + 1)
                dve.wait_ge(S["halved"], i + 1)
                count(pe_e[:, :], C["cand"], ALU.is_ge, "cnt", "count")
                dve.wait_ge(S["sum_ps"], i + 1)
                dve.scalar_tensor_tensor(out=C["took"], in0=ps[:, 2, 0:1], scalar=float(CAP), in1=C["stepc"], op0=ALU.is_ge, op1=ALU.mult).then_inc(S["took"], 1)
                dve.wait_ge(S["took"], i + 1)
                dve.tensor_scalar(C["stepc"], C["stepc"], 0.5, None, ALU.mult).then_inc(S["halved"], 1)
                dve.wait_ge(S["lo"], i + 1)
                dve.tensor_tensor(C["lo"], C["took"], C["lo"], ALU.add).then_inc(S["lo"], 1)
                dve.wait_ge(S["lo"], i + 2)
                dve.wait_ge(S["halved"], i + 2)
                dve.tensor_tensor(C["cand"], C["lo"], C["stepc"], ALU.add).then_inc(S["cand"], 1)
            dve.wait_ge(S["count"], STEPS)
            count(pe_e[:, :], C["lo"], ALU.is_gt, "cnt", "plan")
            dve.tensor_scalar(tie[:, :], pe_e[:, :], C["lo"], None, ALU.is_equal).then_inc(S["plan"], 1)
            dve.wait_ge(S["plan"], PLAN["tie"])
            dve.wait_ge(S["plan"], PLAN["one788"])
            dve.tensor_tensor_scan(tied[:, :], one788[:, :], tie[:, :], 0.0, ALU.mult, ALU.add).then_inc(S["plan"], 1)
            dve.wait_ge(S["sums"], SUMS["g"])
            dve.tensor_scalar(C["room"], ps[:, 3, 2:3], -1.0, float(CAP), ALU.mult, ALU.add).then_inc(S["plan"], 1)
            dve.wait_ge(S["sums"], SUMS["before"])
            dve.wait_ge(S["plan"], PLAN["room"])
            dve.tensor_tensor(C["lim"], C["room"], ps[:, 4, 8:9], ALU.subtract).then_inc(S["plan"], 1)
            dve.wait_ge(S["plan"], PLAN["lim"])
            dve.wait_ge(S["plan"], PLAN["tied"])
            dve.wait_ge(S["plan"], PLAN["g_cnt"])
            count(tied[:, :], C["lim"], ALU.is_lt, "cutc", "plan")
            dve.wait_ge(S["plan"], PLAN["start"])
            dve.tensor_scalar(ended[:, :], iota, C["end"], first, ALU.is_lt, ALU.mult).then_inc(S["plan"], 1)
            dve.scalar_tensor_tensor(out=C["vrow"], in0=C["start"], scalar=-float(P), in1=c3[:, K_REGION:K_REGION + 1],
                                     op0=ALU.mult, op1=ALU.add).then_inc(S["plan"], 1)
            dve.wait_ge(S["plan"], PLAN["sel_a"])
            dve.scalar_tensor_tensor(out=sel[:, :], in0=iota, scalar=C["start"], in1=ended[:, :], op0=ALU.is_ge, op1=ALU.mult).then_inc(S["plan"], 1)
            dve.wait_ge(S["plan"], PLAN["sel"])
            dve.wait_ge(S["plan"], PLAN["vrow"])
            dve.scalar_tensor_tensor(out=vals[:, 0, :], in0=iota128[:, 0:TILES], scalar=C["vrow"], in1=sel[:, 0:TILES],
                                     op0=ALU.add, op1=ALU.mult).then_inc(S["plan"], 1)
            dve.tensor_scalar(vals[:, 1, :], sel[:, 0:TILES], c3[:, K_EXPERT:K_EXPERT + 1], None, ALU.mult).then_inc(S["plan"], 1)
            dve.tensor_scalar(vals[:, 2, :], sel[:, 0:TILES], C["lo"], None, ALU.mult).then_inc(S["plan"], 1)
            dve.wait_ge(S["sums"], SUMS["cut"])
            dve.wait_ge(S["plan"], PLAN["cut_cnt"])
            dve.tensor_copy(C["cutc"], ps[:, 3, 3:4]).then_inc(S["plan"], 1)
            dve.wait_ge(S["plan"], PLAN["cut"])
            dve.tensor_scalar(vals[:, 3, :], sel[:, 0:TILES], C["cutc"], None, ALU.mult).then_inc(S["plan"], 1)
            dve.wait_ge(S["sums"], SUMS["table"])
            table = ps[:, 5, 0:4 * TILES].rearrange("p (a n) -> p a n", a=4)
            dve.tensor_scalar(rowt[:, :], table[:, 0, :], float(DUMMY), None, ALU.add).then_inc(S["plan"], 1)
            dve.tensor_copy(expt[:, :], table[:, 1, :]).then_inc(S["plan"], 1)
            dve.tensor_copy(tct[:, :, :], table[:, 2:4, :]).then_inc(S["plan"], 1)
            dve.wait_ge(S["st4"], 1)

            def step(s, p, r, q):
                if within(s, 0):
                    x = xr[:, r, :]
                    dve.wait_ge(S[f"x4_in{r}"], 16 * (q + 1))
                    wait(dve, S["x_hi"], 2 * (s - 1))
                    wait(dve, S["x_lo"], s - 1)
                    wait(dve, S["base"], s - 1)
                    dve.tensor_scalar(xn4[:, p, :], x[:, 0:D], x[:, D:D + 1], x[:, D + 1:D + 2], ALU.subtract, ALU.mult).then_inc(S["xn4"], 1)
                if within(s, 3):
                    o = (r + 1) % 4
                    dve.wait_ge(S["y_ps"], s - 2)
                    dve.wait_ge(S["kept"], 7 * (s - 3) + 6)
                    dve.wait_ge(S["base"], s - 2)
                    if not isinstance(s, int) or s >= 5:
                        dve.wait_ge(S[f"y_out{(r + 3) % 4}"], 16 * (q if r else q - 1))
                    dve.scalar_tensor_tensor(out=orow[:, 1 - p, :], in0=ps[:, 6 + 1 - p, 0:D], scalar=keepp[:, o, 0:1], in1=base[:, o, :],
                                             op0=ALU.mult, op1=ALU.add).then_inc(S["fin"], 1)
                if within(s, 0):
                    dve.wait_ge(S["x_hi"], 2 * s + 1)
                    dve.wait_ge(S["xn4"], s + 1)
                    wait(dve, S["t4_ps"], s - 1)
                    dve.tensor_tensor(st4[:, p, 1, 0:D], xn4[:, p, :], st4[:, p, 0, 0:D], ALU.subtract).then_inc(S["x_lo"], 1)
                    dve.wait_ge(S["kept"], 7 * s + 7)
                    wait(dve, S["fin"], s - 3)
                    dve.scalar_tensor_tensor(out=base[:, r, :], in0=xn4[:, p, :], scalar=keepp[:, r, 1:2], in1=x[:, 0:D],
                                             op0=ALU.mult, op1=ALU.add).then_inc(S["base"], 1)
                if within(s, 1):
                    for half in range(2):
                        dve.wait_ge(S["hh"], 2 * s - 1 + half)
                        wait(dve, S["y_ps"], s - 2)
                        c = slice(3 * P * half, 3 * P * (half + 1))
                        dve.tensor_tensor(hl[:, 1 - p, c], hf[:, 1 - p, c], hh[:, 1 - p, c], ALU.subtract).then_inc(S["hl"], 1)
            run_tiles(dve, step)

def constants3():
    import numpy as np
    c = np.zeros((P, N_CONST3), np.float32)
    e, k = np.arange(P) // 16, np.arange(P) % 16
    same = e[:, None] == e[None]
    c[:, K_BLOCK:K_BLOCK + P] = same
    c[:, K_BEFORE:K_BEFORE + P] = same & (k[:, None] < k[None])
    c[:, K_UPTO:K_UPTO + P] = (k[:, None] == 0) & (e[:, None] <= e[None])
    c[:, K_IOTA:K_IOTA + P] = np.arange(P)
    c[:, K_IOTA128:K_IOTA128 + P] = P * np.arange(P)
    c[:, K_SEL:K_SEL + EXPERTS] = (k[:, None] == 0) & (e[:, None] == np.arange(EXPERTS))
    c[:, K_TAIL:K_TAIL + EXPERTS] = np.arange(EXPERTS) * REGION + np.arange(P)[:, None]
    c[:, K_FIRST] = k == 0
    c[:, K_CODE] = EXPERTS - e
    c[:, K_REGION] = e * REGION - DUMMY
    c[:, K_EXPERT] = e
    c[:, K_PAD] = FAR
    return c


_OTHERS = ("L0_tok_b", "cls_tok", "L0_attn_W_qkv", "L0_attn_b_qkv", "L0_attn_W_out", "L0_attn_b_out", "L0_ffn_switch_w",
           "L0_ffn_switch_b", "L0_ffn_w1", "L0_ffn_b1", "L0_ffn_w2", "L0_ffn_b2")


def kernel(x, cls_tok, L0_tok_ln_gamma, L0_tok_ln_beta, L0_tok_W, **others):
    import numpy as np
    import concourse.bacc as bacc
    from concourse.bass_utils import run_bass_kernel_spmd

    xt, wr, gr, br, mult = lay_out(np.asarray(x), np.asarray(L0_tok_ln_gamma), np.asarray(L0_tok_ln_beta), np.asarray(L0_tok_W))
    given = {"xt": xt, "wr": wr, "gr": gr, "br": br}
    for name in _OTHERS:
        a = np.ascontiguousarray(cls_tok if name == "cls_tok" else others[name])
        given[name] = a.reshape(1, D) if name == "cls_tok" else a
    given.update(c=constants(mult), c3=constants3())
    nc = bacc.Bacc("TRN2", target_bir_lowering=False, num_devices=1)
    arrays, args = {}, []
    for name, a in given.items():
        arrays[f"in_{name}_dram"] = a
        args.append(nc.dram_tensor(f"in_{name}_dram", a.shape, mybir.dt.from_np(a.dtype), kind="ExternalInput").ap())
    args.append(nc.dram_tensor("out_0_dram", (NTOK, D), F32, kind="ExternalOutput").ap())
    build(nc, *args)
    r = run_bass_kernel_spmd(nc, [arrays], core_ids=[0])
    return r.results[0]["out_0_dram"].reshape(IMAGES, TOK, D)


def layout():
    import numpy as np
    moves = [(0, 0), (0, 1), (0, -1), (1, 0), (-1, 0)]
    where = {}
    for s, (dy, dx) in enumerate(moves):
        for y in range(PATCH):
            for x in range(PATCH):
                for c in range(CH):
                    where.setdefault((c, y - dy, x - dx), []).append(((y * PATCH + x) * 5 + s) * CH + c)
    rows, mult = [], np.zeros(KP, np.float32)
    p = 0
    for m in (5, 4, 3, 1):
        pixels = [k for k in sorted(where) if len(where[k]) == m]
        n = -(-len(pixels) // KT)
        mult[p:p + n] = m
        rows += [(p + i // KT, i % KT, k, where[k]) for i, k in enumerate(pixels)]
        p += n
    assert p == KP
    return rows, mult


def lay_out(x, ln_gamma, ln_beta, w):
    import numpy as np
    rows, mult = layout()
    pad = np.zeros((IMAGES, CH, 226, 226), np.float32)
    pad[:, :, 1:225, 1:225] = x
    xt = np.zeros((KP, KT, IMAGES, SIDE, SIDE), np.float32)
    wr = np.zeros((KP, KT, SHIFTS, D), np.float32)
    gr = np.zeros((KP, KT, SHIFTS), np.float32)
    br = np.zeros((KP, KT, SHIFTS), np.float32)
    for p, k, (c, y, xx), terms in rows:
        xt[p, k] = pad[:, c, y + 1:y + 1 + 209:PATCH, xx + 1:xx + 1 + 209:PATCH]
        for s, e in enumerate(terms):
            wr[p, k, s], gr[p, k, s], br[p, k, s] = w[e], ln_gamma[e], ln_beta[e]
    xt = np.ascontiguousarray(xt.reshape(KP, KT, GROUPS, GT).transpose(2, 0, 1, 3))
    return xt, wr, gr, br, mult


def constants(mult):
    import numpy as np
    c = np.zeros((P, N_CONST), np.float32)
    c[:, C_ID:C_ID + P] = np.eye(P)
    c[:, C_TRI:C_TRI + P] = np.triu(np.ones((P, P)))
    place = np.zeros((2, P), np.int64)
    place[0] = 1 + np.arange(P)
    place[1, :REST] = 1 + P + np.arange(REST)
    freqs = np.arange(TOK, dtype=np.float32)[:, None] / np.float32(10000.0) ** (np.arange(0, HD, 2, dtype=np.float32) / np.float32(HD))[None]
    emb = np.concatenate([freqs, freqs], -1).astype(np.float32)
    sign = np.tile(np.array([-1.0, 1.0], np.float32), HD // 2)
    for t in range(2):
        c[:, C_COS + t * 2 * D:C_COS + (t + 1) * 2 * D] = np.tile(np.cos(emb[place[t]]), (1, 2 * HEADS))
        c[:, C_SIN + t * 2 * D:C_SIN + (t + 1) * 2 * D] = np.tile(np.sin(emb[place[t]]) * sign, (1, 2 * HEADS))
    c[:KP, C_MULT] = mult
    c[:, C_TOKN:C_TOKN + 2] = place.T
    c[:, C_VALID] = 1
    c[:REST + 1, C_VALID + 1] = 1
    c[REST + 1:, C_FAR + 1] = FAR
    c[:, C_SLOT:C_SLOT + EXPERTS] = np.arange(EXPERTS) * REGION - 1
    c[:, C_IOTA:C_IOTA + EXPERTS] = EXPERTS - np.arange(EXPERTS)
    return c
```

```python
from contextlib import ExitStack

import concourse.bass as bass
from concourse import mybir

F32, F16, U32 = mybir.dt.float32, mybir.dt.float16, mybir.dt.uint32
ALU, ACT, AX = mybir.AluOpType, mybir.ActivationFunctionType, mybir.AxisListType

P = 128
IMAGES, SIDE, PATCH, CH = 64, 14, 16, 3
PATCHES = SIDE * SIDE
TOK = PATCHES + 1
REST = PATCHES - P
D, HEADS, HD = 192, 12, 16
TERMS = PATCH * PATCH * CH * 5
KP, KT, SHIFTS = 121, 8, 5
GT = 256
EXPERTS, FF = 8, 768
NTOK = IMAGES * TOK
CAP = int(1.25 * NTOK / EXPERTS)
REC = 196
EPS = 1e-5
SCALE = 64.0
NW = 3 * D + D + EXPERTS
W_OUT, W_SW = 3 * D, 4 * D
FAR = float(1 << 22)
PT = 2 * P
PAIRS = (NTOK + EXPERTS * (PT - 1)) // PT
REGION = (NTOK // P + 3) * P
DUMMY = EXPERTS * REGION
CHUNK = NTOK // 16
FT = FF // P
STEPS = 30

C_ID, C_TRI, C_COS, C_SIN, C_MULT, C_TOKN, C_VALID, C_FAR, C_SLOT, C_IOTA = 0, 128, 256, 1024, 1792, 1793, 1795, 1797, 1799, 1807
N_CONST = 1816
K_BLOCK, K_BEFORE, K_UPTO, K_IOTA, K_IOTA256, K_SEL, K_TAIL = 0, 128, 256, 384, 512, 640, 648
K_FIRST, K_CODE, K_REGION, K_EXPERT, K_PAD, N_CONST3 = 656, 657, 658, 659, 660, 661


def after(*steps):
    done, total = {}, 0
    for s in steps:
        name, n = s if isinstance(s, tuple) else (s, 1)
        total += n
        done[name] = total
    return done


PLAN = after("onef", "one788", ("prow", 6), "pe_e", "n_cnt", "n_e", "ntile", "dn", "end", ("tails", 2), "start", "g_cnt", "tie", "tied",
             "room", "lim", "cut_cnt", "sel_a", "vrow", "sel", ("vals", 3), "cut", "vals_all", ("tables", 3))
SUMS = after("n", "end", "tail", "g", "before", "cut", "table")


class Sems:

    def __init__(self, nc, ctx):
        self._made, self._nc, self._ctx = {}, nc, ctx

    def __getitem__(self, name):
        if name not in self._made:
            self._made[name] = self._ctx.enter_context(self._nc.semaphore(name))
        return self._made[name]


def wait(eng, sem, value):
    if not (isinstance(value, int) and value <= 0):
        eng.wait_ge(sem, value)


def build(nc, xt, wraw, graw, braw, tokb, cls, wqkv, bqkv, wout, bout, wsw, bsw, w1, b1, w2, b2, consts, consts3, out):
    ctx = ExitStack()
    with ctx:
        sb = lambda name, shape, dt=F32: area.enter_context(nc.sbuf_tensor(name, shape, dt))
        area = ctx
        S = Sems(nc, ctx)
        hp = nc.dram_tensor("hp", (IMAGES * PATCHES, D), F32).ap()

        cst = sb("cst", [P, N_CONST])
        ident = cst[:, C_ID:C_ID + P]
        idh = sb("idh", [P, P], F16)
        oneh = sb("oneh", [P, P], F16)
        pall = sb("pall", [P, 2, 2, IMAGES])
        ps = ctx.enter_context(nc.psum_tensor("ps", [P, 8, 512], F32))
        area = early = ctx.enter_context(ExitStack())
        xb = sb("xb", [KP, 2, KT, GT])
        xsq = sb("xsq", [KP, KT, GT])
        xss = sb("xss", [KP, GT])
        wr = sb("wr", [KP, KT, SHIFTS, D])
        gb = sb("gb", [KP, 2, KT, SHIFTS])
        wg = sb("wg", [KP, 2, SHIFTS, D])
        wf = sb("wf", [KP, KT, D + 1])
        ones = sb("ones", [P, P])
        wfs = sb("wfs", [KP, 2, KT, D + 1], F16)
        xs = sb("xs", [KP, 2, KT, GT], F16)
        gsum = sb("gsum", [P, D])
        brow = sb("brow", [P, D])
        brow0 = sb("brow0", [P, D])
        xst = sb("xst", [P, 2, 4, 2])
        hm = sb("hm", [P, 2, D])
        mhalf = sb("mhalf", [P, 2])

        hx = sb("hx", [P, 2, 2, D])
        hr = sb("hr", [P, 2, 2, D])
        rec = sb("rec", [P, 2, 2, REC])
        wstage = sb("wstage", [P, 3, NW])
        wst = sb("wst", [P, 4, NW], F16)
        st = {n: sb(n, [P, 2, 2, 256], F16) for n in ("s1", "s2", "s3")}
        tt = {n: sb(n, [P, 1 + (n == "t1"), 4, 256], F16) for n in ("t1", "t2", "t3")}
        trih = sb("trih", [P, P], F16)
        mvs = sb("mvs", [P, 2, 2, 6])
        mv = sb("mv", [P, 2, 2, 2])
        mve = sb("mve", [P, 2, 2])
        rstd1 = sb("rstd1", [P, 2])
        hn = sb("hn", [P, 2, D])
        xn = sb("xn", [P, 2, D])
        cn = sb("cn", [P, 2, D])
        rc = sb("rc", [P, 2, HEADS])
        ra = sb("ra", [P, 2, 2 * D])
        rb = sb("rb", [P, 2, 2 * D])
        qk = sb("qk", [P, 2, 2 * D])
        qks = sb("qks", [P, 2, 2, 2 * HEADS, 4, HD], F16)
        kms = sb("kms", [P, 2, 6, 2, 256], F16)
        qt = sb("qt", [P, 6, 256], F16)
        q2t = sb("q2t", [P, 6, 256], F16)
        va = sb("va", [P, 2, 2, HEADS, 32])
        pt = sb("pt", [P, 2, HEADS, TOK])
        ctxt = sb("ctxt", [P, 3, 256])
        mx = sb("mx", [P, 2, HEADS])
        lmx = sb("lmx", [P, 2])
        ld = sb("ld", [P, 2, EXPERTS])
        le = sb("le", [P, 2, EXPERTS])
        lsum = sb("lsum", [P, 2])
        c8 = sb("c8", [P, 2, EXPERTS])
        code = sb("code", [P, 2, 2])
        oh = sb("oh", [P, 2, 2, EXPERTS], F16)
        cum = sb("cum", [P, 2, 2, EXPERTS], F16)
        sl = sb("sl", [P, 2, EXPERTS])
        sl2 = sb("sl2", [P, 2, EXPERTS])
        slot = sb("slot", [P, 2])
        idx = sb("idx", [P, 2, 2], U32)
        tokn = sb("tokn", [P, 2])
        records = nc.dram_tensor("records", (DUMMY + PT, REC), F32).ap()
        pflat = nc.dram_tensor("pflat", (2, IMAGES, TOK), F32).ap()
        half6 = ps[:, 6, :].bitcast(F16).rearrange("p (s c) -> p s c", c=256)
        half7 = ps[:, 7, :].bitcast(F16).rearrange("p (s c) -> p s c", c=256)

        early.close()
        area = ctx

        c3 = sb("c3", [P, N_CONST3])
        onef = sb("onef", [P, P])
        prow = sb("prow", [IMAGES, 2, TOK])
        cols = {n: sb(n, [P, 1]) for n in ("cnt", "n_e", "ntile", "end", "start", "vrow", "lo", "stepc", "cand", "took", "below", "room", "lim", "cutc")}
        dn = sb("dn", [P, EXPERTS])
        tails = sb("tails", [P, 2, EXPERTS], U32)
        padrec = sb("padrec", [P, REC])
        ended = sb("ended", [P, P])
        sel = sb("sel", [P, P])
        vals = sb("vals", [P, 4, PAIRS])
        rowt = sb("rowt", [P, PAIRS], U32)
        expt = sb("expt", [P, PAIRS], U32)
        tct = sb("tct", [P, 2, PAIRS])
        f1 = sb("f1", [P, 2, 3, FF])
        f2 = sb("f2", [P, 2, FT, D])
        fb2 = sb("fb2", [P, EXPERTS, D])
        w1s = sb("w1s", [P, EXPERTS, 4 * FF], F16)
        w2s = sb("w2s", [P, EXPERTS, FT * 2 * D], F16)
        b2s = sb("b2s", [P, EXPERTS, D], F16)
        xn4 = sb("xn4", [P, 2, 2, D])
        st4 = sb("st4", [P, 2, 2, 2, 256], F16)
        xt4 = sb("xt4", [P, 2, 4, PT], F16)
        hf = sb("hf", [P, 2, FT * PT])
        hh = sb("hh", [P, 2, FT * PT], F16)
        hl = sb("hl", [P, 2, FT * PT], F16)
        small = sb("small", [P, 2, 12])
        keepp = sb("keepp", [P, 4, 2, 2])

        area = counting = ctx.enter_context(ExitStack())
        eb = sb("eb", [P, 2, CHUNK])
        pe_e = sb("pe_e", [P, CHUNK])
        scr = sb("scr", [P, CHUNK])
        tie = sb("tie", [P, CHUNK])
        tied = sb("tied", [P, CHUNK])
        one788 = sb("one788", [P, CHUNK])
        counting.close()
        area = ctx
        xr = sb("xr", [P, 8, 2, REC])
        base = sb("base", [P, 4, 2, D])
        orow = sb("orow", [P, 2, 2, D])

        block = ctx.enter_context(nc.Block())

        def run_images(eng, step):
            for s in range(-1, 7):
                step(s, s % 2, s // 2)
            with eng.Fori(0, (IMAGES - 8) // 2) as i:
                step(2 * i + 7, 1, i + 3)
                step(2 * i + 8, 0, i + 4)
            for s in range(IMAGES - 1, IMAGES + 4):
                step(s, s % 2, s // 2)

        def carried(eng):
            eng.sem_inc(S["carried"], 1)

        def images_of(s):
            n = [s - k for k in range(5)]
            return n, [not isinstance(x, int) or 0 <= x < IMAGES for x in n]

        def embeds(s):
            return not isinstance(s, int) or s + 1 < IMAGES

        def upto(n):
            return min(n, IMAGES) if isinstance(n, int) else n

        @block.sync
        def _(sp):
            sp.dma_start(wr[:, :, :, :], wraw).then_inc(S["w_in"], 16)
            sp.dma_start(gb[:, 0, :, :], graw).then_inc(S["g_in"], 16)
            sp.dma_start(gb[:, 1, :, :], braw).then_inc(S["b_in"], 16)
            sp.dma_start(cst[:, :], consts).then_inc(S["c_in"], 16)
            sp.dma_start(brow0[:, :], tokb.partition_broadcast(P)).then_inc(S["tb_in"], 16)

            sp.wait_ge(S["wz"], 1)
            for c, n, w, b in ((0, 3 * D, wqkv, bqkv), (W_OUT, D, wout, bout), (W_SW, EXPERTS, wsw, bsw)):
                sp.dma_start(wstage[:, 0, c:c + n], w[0:P, :]).then_inc(S["ws_in"], 16)
                for r in (0, 64):
                    sp.dma_start(wstage[r:r + 64, 1, c:c + n], w[P:D, :]).then_inc(S["ws_in"], 16)
                for r in (64, 96):
                    sp.dma_start(wstage[r:r + 1, 2, c:c + n], b.rearrange("(a n) -> a n", a=1)).then_inc(S["ws_in"], 16)
            sp.wait_ge(S["mem"], 1)
            for q in range(2):
                for a in (hx, hr):
                    sp.dma_start(a[REST:REST + 1, q, 1, :], cls).then_inc(S["cls_in"], 16)
            def image_in(s, p, half):
                (a, b, m, c, d), (on_a, on_b, on_m, on_c, on_d) = images_of(s)
                if embeds(s):
                    for name in ("xs_lo0", "xs_lo1"):
                        wait(sp, S[name], s)
                        carried(sp)
                    wait(sp, S["sq"], s)
                    carried(sp)
                    sp.dma_start(xb[:, 1 - p, :, 0:PATCHES], xt[bass.ds(s + 1, 1), :, :, :].rearrange("g p k t -> (g p) k t")).then_inc(S[f"x_in{1 - p}"], 16)
                if on_a:
                    sp.wait_ge(S["ho"], 2 * (a + 1))
                    carried(sp)
                    sp.dma_start(hp[bass.ds(PATCHES * a, P), :], hx[:, p, 0, :]).then_inc(S[f"hp_out{p}"], 16)
                    sp.dma_start(hp[bass.ds(PATCHES * a + P, REST), :], hx[0:REST, p, 1, :]).then_inc(S[f"hp_out{p}"], 16)
                if on_c:
                    sp.wait_ge(S[f"hp_out{1 - p}"], 32 * (half if p else half - 1))
                    carried(sp)
                    wait(sp, S["h2"], c - 1)
                    carried(sp)
                    sp.dma_start(hr[:, 1 - p, 0, :], hp[bass.ds(PATCHES * c, P), :]).then_inc(S[f"hr_in{1 - p}"], 16)
                    sp.dma_start(hr[0:REST, 1 - p, 1, :], hp[bass.ds(PATCHES * c + P, REST), :]).then_inc(S[f"hr_in{1 - p}"], 16)
            run_images(sp, image_in)

        @block.gpsimd
        def _(pool):
            pool.memset(mhalf[:, :], -0.5).then_inc(S["zero"], 1)

            for a in (hx, hr, qks, kms, qt, va, *st.values(), *tt.values(), cum, xs, xss):
                pool.memset(a.ap() if hasattr(a, "ap") and callable(a.ap) else a, 0.0).then_inc(S["zero"], 1)
            pool.wait_ge(S["zero"], 16)
            for a in st.values():
                pool.memset(a[:, :, 0, D:256:32], 1.0).then_inc(S["one"], 1)
            pool.memset(qks[:, :, :, HEADS:, 3, 0:2].rearrange("p a t h r -> p (a t) h r"), 1.0).then_inc(S["one"], 1)
            pool.memset(va[:, :, :, :, HD:HD + 1].rearrange("p a t h r -> p (a t) h r"), 1.0).then_inc(S["one"], 1)
            pool.memset(ctxt[:, :, :], 1.0).then_inc(S["one"], 1)
            pool.memset(oneh[:, :], 1.0).then_inc(S["one"], 1)
            pool.wait_ge(S["c_in"], 16)
            pool.tensor_copy(tokn[:, :], cst[:, C_TOKN:C_TOKN + 2]).then_inc(S["one"], 1)
            pool.wait_ge(S["one"], 8)
            pool.drain().then_inc(S["mem"], 1)
            pool.wait_ge(S["wst"], 6)

            def step(s, p, half):
                (a, b, m, c, d), (on_a, on_b, on_m, on_c, on_d) = images_of(s)

                def low(on, name, x, n, src, rows):
                    if on:
                        wait(pool, S[name + "_ps"], n)
                        pool.wait_ge(S[rows], 2 * (n + 1))
                        pool.wait_ge(S[x + "_hi"], 2 * (n + 1))
                        pool.tensor_tensor(st[x][:, :, 1, 0:D], src[:, :, :], st[x][:, :, 0, 0:D], ALU.subtract).then_inc(S[x + "_lo"], 1)

                def pixels_low():
                    if embeds(s):
                        pool.wait_ge(S["xs_hi"], s + 2)
                        wait(pool, S["embed"], 4 * (s + 1))
                        at = slice(KT // 2, KT)
                        pool.tensor_tensor(xs[:, 1, at, 0:PATCHES], xb[:, 1 - p, at, 0:PATCHES], xs[:, 0, at, 0:PATCHES], ALU.subtract).then_inc(S["xs_lo1"], 1)

                def pixels():
                    if embeds(s):
                        pool.wait_ge(S["sq"], s + 2)
                        wait(pool, S["acc"], 2 * (s + 1))
                        part = lambda k: xsq[:, k:k + KT // 2, 0:PATCHES]
                        pool.tensor_tensor(part(0), part(0), part(KT // 2), ALU.add).then_inc(S["sqh"], 1)
                        pool.wait_ge(S["sqh"], 2 * s + 3)
                        pool.tensor_tensor(xsq[:, 0:2, 0:PATCHES], xsq[:, 0:2, 0:PATCHES], xsq[:, 2:4, 0:PATCHES], ALU.add).then_inc(S["sqh"], 1)
                        pool.wait_ge(S["sqh"], 2 * s + 4)
                        pool.tensor_tensor(xss[:, 0:PATCHES], xsq[:, 0, 0:PATCHES], xsq[:, 1, 0:PATCHES], ALU.add).then_inc(S["sqs"], 1)

                def rstd_0():
                    if embeds(s):
                        pool.wait_ge(S["var"], s + 2)
                        pool.tensor_tensor(xst[:, 1 - p, 3, :], xst[:, 1 - p, 2, :], mhalf[:, :], ALU.pow).then_inc(S["rstd"], 1)

                def no_maxima():
                    if on_b:
                        wait(pool, S["q2_ps"], 2 * (b - 1))
                        carried(pool)
                        pool.memset(qks[:, 1 - p, :, 0:HEADS, 3, 0:2], 0.0).then_inc(S["m_zero"], 1)

                def numbers():
                    if on_d:
                        wait(pool, S[f"sc_done{p}"], 32 * (half - 2))
                        carried(pool)
                        pool.tensor_copy(rec[:, p, :, REC - 1].bitcast(U32), tokn[:, :]).then_inc(S["tok"], 1)
                        pool.wait_ge(S["tok"], 2 * d + 1)
                        carried(pool)
                        pool.tensor_scalar(tokn[:, :], tokn[:, :], float(TOK), None, ALU.add).then_inc(S["tok"], 1)

                def rstd_2():
                    if on_d:
                        pool.wait_ge(S["ln2_var"], d + 1)
                        pool.tensor_tensor(rec[:, p, :, D + 1], mve[:, 1, :], mhalf[:, :], ALU.pow).then_inc(S["ln2_rstd"], 1)
                        pool.tensor_copy(rec[:, p, :, D], mv[:, 1, :, 0]).then_inc(S["rec_m"], 1)

                def rstd_1():
                    if on_a:
                        pool.wait_ge(S["ln1_var"], a + 1)
                        pool.tensor_tensor(rstd1[:, :], mve[:, 0, :], mhalf[:, :], ALU.pow).then_inc(S["ln1_rstd"], 1)

                def rotated_low(t):
                    if on_b:
                        pool.wait_ge(S["qk_hi"], 2 * b + t + 1)
                        src = qk[:, t, :].rearrange("p (w h r) -> p w h r", w=2, r=HD)
                        hi = qks[:, 1 - p, t, :, 0, :].rearrange("p (w h) r -> p w h r", w=2)
                        for w in range(2):
                            pool.tensor_tensor(qks[:, 1 - p, t, HEADS * w:HEADS * (w + 1), 1 + w, :], src[:, w, :, :], hi[:, w, :, :],
                                               ALU.subtract).then_inc(S["qk_lo"], 1)

                def counted():
                    if on_d:
                        pool.wait_ge(S["route"], 12 * d + 6)
                        wait(pool, S["prefix"], d)
                        pool.tensor_tensor(cum[:, p, 1, :], cum[:, p, 0, :], oh[:, p, 0, :], ALU.add).then_inc(S["cum"], 1)
                        pool.wait_ge(S["cum"], 2 * d + 1)
                        pool.tensor_tensor(cum[:, 1 - p, 0, :], cum[:, p, 1, :], oh[:, p, 1, :], ALU.add).then_inc(S["cum"], 1)

                def noted():
                    if on_d:
                        pool.wait_ge(S["route"], 12 * d + 8)
                        carried(pool)
                        pool.tensor_copy(pall[:, 0, :, bass.ds(d, 1)], rec[:, p, :, D + 2:D + 3]).then_inc(S["pall"], 1)
                        pool.tensor_copy(pall[:, 1, :, bass.ds(d, 1)], code[:, 1, :].unsqueeze(2)).then_inc(S["pall"], 1)

                def scattered():
                    if on_d:
                        pool.wait_ge(S["route"], 12 * d + 8)
                        pool.wait_ge(S["route"], 12 * d + 12)
                        pool.wait_ge(S["tok"], 2 * d + 1)
                        pool.wait_ge(S["rec_m"], d + 1)
                        pool.wait_ge(S["ln2_rstd"], d + 1)
                        carried(pool)
                        for t in range(2):
                            pool.indirect_dma_start(records, bass.IndirectOffsetOnAxis(ap=idx[:, p, t:t + 1], axis=0), rec[:, p, t, :],
                                                    None, bounds_check=EXPERTS * REGION - 1, oob_is_err=False).then_inc(S[f"sc_done{p}"], 16)

                pixels_low()
                rstd_1()
                rstd_2()
                numbers()
                low(on_a, "t1", "s1", a, hn, "ln1_hn")
                low(on_d, "t3", "s3", d, xn, "xn")
                no_maxima()
                pixels()
                low(on_c, "t2", "s2", c, cn, "cn")
                rotated_low(0)
                counted()
                rotated_low(1)
                rstd_0()
                noted()
                scattered()
            run_images(pool, step)

        @block.scalar
        def _(act):
            act.wait_ge(S["mem"], 1)

            def step(s, p, half):
                (a, b, m, c, d), (on_a, on_b, on_m, on_c, on_d) = images_of(s)

                def pixels_high():
                    if embeds(s):
                        act.wait_ge(S[f"x_in{1 - p}"], 16 * (half + p + 1))
                        wait(act, S["embed"], 4 * (s + 1))
                        act.activation(xs[:, 0, :, 0:PATCHES], xb[:, 1 - p, :, 0:PATCHES], ACT.Copy).then_inc(S["xs_hi"], 1)

                def square():
                    if embeds(s):
                        act.wait_ge(S[f"x_in{1 - p}"], 16 * (half + p + 1))
                        wait(act, S["sqs"], s + 1)
                        act.activation(xsq[:, :, 0:PATCHES], xb[:, 1 - p, :, 0:PATCHES], ACT.Square).then_inc(S["sq"], 1)

                def high(on, name, x, n, src, rows):
                    if on:
                        act.wait_ge(S[rows], 2 * (n + 1))
                        wait(act, S[name + "_ps"], n)
                        act.activation(st[x][:, :, 0, 0:D], src[:, :, :], ACT.Copy).then_inc(S[x + "_hi"], 1)
                        act.activation(st[x][:, :, 1, D:256], src[:, :, P:D], ACT.Copy).then_inc(S[x + "_hi"], 1)

                def turned(on, name, n, q, half, used, times):
                    if on:
                        act.wait_ge(S[name + "_ps"], n + 1)
                        wait(act, S[used], times)
                        act.activation(tt[name][:, q, :, 0:TOK], half[:, :, 0:TOK], ACT.Copy).then_inc(S[name + "_cp"], 1)

                def exps(u):
                    if on_c:
                        g, kt = u // 2, u % 2
                        act.wait_ge(S["st_ps"], 12 * c + u + 1)
                        wait(act, S["ctx_ps"], 3 * (c - 1) + g // 2 + 1)
                        act.activation(pt[:, kt, 2 * g:2 * g + 2, :].rearrange("p c n -> p (c n)"), ps[:, 2 + u % 2, 0:2 * TOK],
                                       ACT.Exp, scale=HD ** -0.5).then_inc(S["exp"], 1)

                def context(g):
                    if on_c:
                        act.wait_ge(S["ctx_ps"], 3 * c + g + 1)
                        wait(act, S["ct_ps"], 2 * c)
                        act.activation(ctxt[:, g, 0:TOK], ps[:, 5, 0:TOK], ACT.Copy).then_inc(S["ctx_cp"], 1)

                def keys(u):
                    if on_m:
                        act.wait_ge(S["k_ps"], 2 * m + u + 1)
                        wait(act, S["st_ps"], 12 * (m - 1))
                        act.activation(kms[0:64, p, 3 * u:3 * u + 3, 0, 0:TOK], half6[0:64, 0:3, 0:TOK], ACT.Copy).then_inc(S["k_cpa"], 1)

                def values():
                    if on_m:
                        act.wait_ge(S["v_ps"], m + 1)
                        wait(act, S["ctx_ps"], 3 * (m - 1))
                        act.activation(va[:, p, :, :, 0:HD], ps[:, 4, 0:2 * D].rearrange("p (t h r) -> p t h r", t=2, r=HD),
                                       ACT.Copy).then_inc(S["v_cp"], 1)

                def rotated(t):
                    if on_b:
                        wait(act, S["q2_ps"], 2 * (b - 1))
                        act.wait_ge(S["rope"], 2 * b + t + 1)
                        act.activation(qks[:, 1 - p, t, :, 0, :], qk[:, t, :].rearrange("p (h r) -> p h r", r=HD), ACT.Copy).then_inc(S["qk_hi"], 1)

                def again(t):
                    if on_b:
                        wait(act, S["q2_ps"], 2 * (b - 1))
                        act.wait_ge(S["rope"], 2 * b + t + 1)
                        for w in range(2):
                            act.activation(qks[:, 1 - p, t, HEADS * w:HEADS * (w + 1), 2 - w, :],
                                           qk[:, t, D * w:D * (w + 1)].rearrange("p (h r) -> p h r", r=HD), ACT.Copy).then_inc(S["qk_hi2"], 1)

                def chances():
                    if on_d:
                        act.wait_ge(S["route"], 12 * d + 2)
                        act.activation(le[:, :, :], ld[:, :, :], ACT.Exp).then_inc(S["le"], 1)

                square()
                pixels_high()
                keys(0)
                values()
                exps(0)
                exps(1)
                keys(1)
                exps(2)
                exps(3)
                exps(4)
                exps(5)
                exps(6)
                exps(7)
                context(0)
                exps(8)
                exps(9)
                high(on_a, "t1", "s1", a, hn, "ln1_hn")
                context(1)
                exps(10)
                exps(11)
                high(on_d, "t3", "s3", d, xn, "xn")
                context(2)
                turned(on_a, "t1", a, p, half6, "v_ps", a - 1)
                rotated(0)
                turned(on_d, "t3", d, 0, half7, "lg_ps", d)
                again(0)
                high(on_c, "t2", "s2", c, cn, "cn")
                rotated(1)
                again(1)
                chances()
                turned(on_c, "t2", c, 0, half7, "wo_ps", c)
            run_images(act, step)

        @block.tensor
        def _(pe):
            pe.wait_ge(S["w_in"], 16)
            pe.wait_ge(S["b_in"], 16)
            n = KT * SHIFTS
            for k in range(n):
                last = pe.matmul(ps[:, 6, 0:D], gb[:, 1, k // SHIFTS, k % SHIFTS:k % SHIFTS + 1].broadcast_to([KP, P]),
                                 wr[:, k // SHIFTS, k % SHIFTS, :], start=(k == 0), stop=(k == n - 1))
            last.then_inc(S["bw"], 1)
            pe.wait_ge(S["wf"], KT)
            pe.wait_ge(S["ones"], 2)
            pe.wait_ge(S["c_in"], 16)
            for k in range(KT):
                last = pe.matmul(ps[:, 7, 0:D], ones[0:KP, :], wf[:, k, 0:D], start=(k == 0), stop=(k == KT - 1))
            last.then_inc(S["gs"], 1)

            pe.wait_ge(S["mem"], 1)
            pe.wait_ge(S["wst"], 9)
            pe.wait_ge(S["ones"], 4)
            pe.wait_ge(S["rows"], 2)

            def turn(name, half):
                a = st[name]
                for t in range(2):
                    for c, src in enumerate((a[:, t, 0, 0:P], a[:, t, 1, 0:P], a[:, t, 1, P:256], a[:, t, 0, P:256])):
                        last = pe.transpose(half[:, c, t * P:(t + 1) * P], src, idh[:, :])
                return last

            def stacked(o, x, q, t, c, n):
                for i, (a, w) in enumerate(((0, 0), (0, 1), (1, 0), (2, 2), (3, 3))):
                    last = pe.matmul(o, tt[x][:, q, a, t * P:(t + 1) * P], wst[:, w, c:c + n], start=(i == 0), stop=(i == 4))
                return last

            def pairs(q, w, u, half):
                for i in range(3):
                    h = HEADS * w + 2 * (3 * u + i)
                    for t in range(2):
                        last = pe.transpose(half[:, i, t * P:(t + 1) * P], qks[:, q, t, h:h + 2, :, :].rearrange("p h s r -> p (h s r)"), idh[:, :])
                return last

            def step(s, p, half):
                (a, b, m, c, d), (on_a, on_b, on_m, on_c, on_d) = images_of(s)

                def embed(i):
                    if embeds(s):
                        t, half_k = i // 2, i % 2
                        if i == 0:
                            wait(pe, S["hm"], 2 * (s + 1))
                            wait(pe, S["t1_cp"], s + 1)
                        if i < 2:
                            pe.wait_ge(S[f"xs_lo{i}"], s + 2)
                        for k in range(KT // 2 * half_k, KT // 2 * (half_k + 1)):
                            for j, (a, w) in enumerate(((0, 0), (0, 1), (1, 0))):
                                last = pe.matmul(ps[:, 6, t * 256:t * 256 + D + 1], xs[:, a, k, t * P:(t + 1) * P], wfs[:, w, k, :],
                                                 start=(k == 0 and j == 0), stop=(k == KT - 1 and j == 2))
                        last.then_inc(S["embed"], 1)

                def squares():
                    if embeds(s):
                        pe.wait_ge(S["sqs"], s + 2)
                        for t in range(2):
                            pe.matmul(ps[:, 6, t * 256 + D + 1:t * 256 + D + 2], xss[:, t * P:(t + 1) * P], cst[0:KP, C_MULT:C_MULT + 1],
                                      start=True, stop=True).then_inc(S["acc"], 1)

                def queries2(u):
                    if on_c:
                        pe.wait_ge(S["m_lo"], c + 1)
                        if u == 0:
                            wait(pe, S["t2_cp"], c)
                        else:
                            pe.wait_ge(S["q2_cp"], 2 * c + 1)
                        pairs(1 - p, 0, u, half7).then_inc(S["q2_ps"], 1)

                def scores_t(u):
                    if on_c:
                        g, kt = u // 2, u % 2
                        pe.wait_ge(S["q2_cp"], 2 * c + (1 if g < 3 else 2))
                        wait(pe, S["exp"], 12 * c + u - 1)
                        for i in range(2):
                            last = pe.matmul(ps[:, 2 + u % 2, i * TOK:(i + 1) * TOK], kms[:, 1 - p, g, i, kt * P:(kt + 1) * P],
                                             q2t[:, g, 0:TOK], start=True, stop=True)
                        last.then_inc(S["st_ps"], 1)

                def weighted(g):
                    if on_c:
                        pe.wait_ge(S["exp"], 12 * c + 4 * g + 4)
                        if g == 0:
                            pe.wait_ge(S["v_cp"], c + 1)
                            wait(pe, S["h2"], c)
                        else:
                            pe.wait_ge(S["ctx_cp"], 3 * c + g)
                        for kt in range(2):
                            n = P if kt == 0 else TOK - P
                            for i in range(4):
                                last = pe.matmul(ps[32 * i:32 * i + 32, 5, 0:TOK], va[0:n, 1 - p, kt, 4 * g + i, :], pt[0:n, kt, 4 * g + i, :],
                                                 start=(kt == 0), stop=(kt == 1), tile_position=(0, 32 * i))
                        last.then_inc(S["ctx_ps"], 1)

                def context(u):
                    if on_c:
                        pe.wait_ge(S["ctx_cp"], 3 * (c + 1))
                        if u == 1:
                            pe.wait_ge(S["cn"], 2 * c + 1)
                        for g in range(3):
                            last = pe.transpose(ps[:, 5, g * P:(g + 1) * P], ctxt[:, g, u * P:(u + 1) * P], ident)
                        last.then_inc(S["ct_ps"], 1)

                def context_turned():
                    if on_c:
                        pe.wait_ge(S["s2_lo"], c + 1)
                        wait(pe, S["t3_cp"], c)
                        turn("s2", half7).then_inc(S["t2_ps"], 1)

                def context_out():
                    if on_c:
                        pe.wait_ge(S["t2_cp"], c + 1)
                        pe.wait_ge(S["cn"], 2 * (c + 1))
                        for t in range(2):
                            last = stacked(ps[:, 5, t * D:(t + 1) * D], "t2", 0, t, W_OUT, D)
                        last.then_inc(S["wo_ps"], 1)

                def values():
                    if on_m:
                        pe.wait_ge(S["t1_cp"], m + 1)
                        pe.wait_ge(S["rope_b"], 2 * (m + 1))
                        wait(pe, S["route"], 12 * d - 3)
                        for t in range(2):
                            last = stacked(ps[:, 4, t * D:(t + 1) * D], "t1", p, t, 2 * D, D)
                        last.then_inc(S["v_ps"], 1)

                def keys(u):
                    if on_m:
                        if u == 0:
                            pe.wait_ge(S["qk_lo"], 4 * (m + 1))
                            pe.wait_ge(S["qk_hi2"], 4 * (m + 1))
                            pe.wait_ge(S["m_zero"], m + 1)
                            pe.wait_ge(S["t1_cp"], upto(s))
                            pe.wait_ge(S["hm"], 2 * upto(s + 1))
                        else:
                            pe.wait_ge(S["k_cpa"], 2 * m + 1)
                            pe.wait_ge(S["k_cpd"], 2 * m + 1)
                        pairs(p, 1, u, half6).then_inc(S["k_ps"], 1)

                def queries(u):
                    if on_m:
                        if u == 0:
                            pe.wait_ge(S["k_cpa"], 2 * m + 2)
                            pe.wait_ge(S["k_cpd"], 2 * m + 2)
                        else:
                            pe.wait_ge(S["q_cp"], 2 * m + 1)
                        pairs(p, 0, u, half6).then_inc(S["q_ps"], 1)

                def maxima(u):
                    if on_m:
                        q, g = u // 6, u % 6
                        pe.wait_ge(S["q_cp"], 2 * m + (1 if u < 3 else 2))
                        wait(pe, S["s_max"], 12 * m + u - 1)
                        pe.matmul(ps[:, u % 2, 0:2 * TOK], qt[:, g, q * P:(q + 1) * P], kms[:, p, g, :, 0:TOK], start=True, stop=True).then_inc(S["s_ps"], 1)

                def project(t):
                    if on_b:
                        pe.wait_ge(S["t1_cp"], b + 1)
                        if t == 0:
                            wait(pe, S["v_cp"], b)
                            wait(pe, S["route"], 12 * d - 3)
                        else:
                            pe.wait_ge(S["rope_b"], 2 * b + 1)
                        stacked(ps[:, 4, 0:2 * D], "t1", 1 - p, t, 0, 2 * D).then_inc(S["qk_ps"], 1)

                def arrive():
                    if on_a:
                        pe.wait_ge(S["s1_lo"], a + 1)
                        wait(pe, S["q_cp"], 2 * (a - 1))
                        turn("s1", half6).then_inc(S["t1_ps"], 1)

                def turned():
                    if on_d:
                        pe.wait_ge(S["s3_lo"], d + 1)
                        pe.wait_ge(S["q2_cp"], 2 * upto(d + 2))
                        pe.wait_ge(S["t2_cp"], d + 1)
                        turn("s3", half7).then_inc(S["t3_ps"], 1)

                def logits():
                    if on_d:
                        pe.wait_ge(S["t3_cp"], d + 1)
                        pe.wait_ge(S["rope_b"], 2 * upto(d + 4))
                        pe.wait_ge(S["v_cp"], upto(d + 3))
                        wait(pe, S["route"], 12 * d - 3)
                        for t in range(2):
                            last = stacked(ps[:, 4, t * EXPERTS:(t + 1) * EXPERTS], "t3", 0, t, W_SW, EXPERTS)
                        last.then_inc(S["lg_ps"], 1)

                def prefix():
                    if on_d:
                        pe.wait_ge(S["route"], 12 * d + 6)
                        pe.wait_ge(S["route"], 12 * d + 2)
                        pe.wait_ge(S["cum"], 2 * d + 1)
                        for t in range(2):
                            o = ps[:, 4, 256 + t * EXPERTS:256 + (t + 1) * EXPERTS]
                            pe.matmul(o, trih[:, :], oh[:, p, t, :], start=True, stop=False)
                            last = pe.matmul(o, oneh[:, :], cum[:, p, t, :], start=False, stop=True)
                        last.then_inc(S["prefix"], 1)

                queries2(0)
                keys(0)
                values()
                scores_t(0)
                scores_t(1)
                keys(1)
                project(0)
                scores_t(2)
                scores_t(3)
                queries2(1)
                queries(0)
                scores_t(4)
                scores_t(5)
                weighted(0)
                scores_t(6)
                maxima(0)
                scores_t(7)
                queries(1)
                maxima(1)
                scores_t(8)
                maxima(2)
                scores_t(9)
                weighted(1)
                scores_t(10)
                scores_t(11)
                maxima(3)
                maxima(4)
                project(1)
                weighted(2)
                arrive()
                maxima(5)
                maxima(6)
                context(0)
                turned()
                embed(0)
                context(1)
                maxima(7)
                embed(1)
                maxima(8)
                logits()
                maxima(9)
                embed(2)
                maxima(10)
                maxima(11)
                context_turned()
                embed(3)
                squares()
                prefix()
                context_out()
            run_images(pe, step)

        @block.vector
        def _(dve):
            dve.memset(wstage[:, 2, :], 0.0).then_inc(S["wz"], 1)
            dve.memset(ones[:, :], 1.0).then_inc(S["ones"], 1)
            dve.wait_ge(S["w_in"], 16)
            dve.wait_ge(S["g_in"], 16)
            for k in range(KT):
                wait(dve, S["wf"], k - 1)
                dve.tensor_tensor(wg[:, k % 2, :, :], wr[:, k, :, :], gb[:, 0, k, :].unsqueeze(2).broadcast_to([KP, SHIFTS, D]),
                                  ALU.mult).then_inc(S["wg"], 1)
                dve.wait_ge(S["wg"], k + 1)
                dve.tensor_reduce(wf[:, k, 0:D], wg[:, k % 2, :, :].rearrange("p s d -> p d s"), AX.X, ALU.add).then_inc(S["wf"], 1)
            dve.wait_ge(S["c_in"], 16)
            dve.tensor_copy(wf[:, :, D], cst[0:KP, C_MULT:C_MULT + 1].broadcast_to([KP, KT])).then_inc(S["ones"], 1)
            dve.wait_ge(S["wf"], KT)
            dve.wait_ge(S["ones"], 2)
            dve.tensor_scalar(wfs[:, 0, :, :], wf[:, :, :], SCALE, None, ALU.mult).then_inc(S["ones"], 1)
            dve.wait_ge(S["ones"], 3)
            dve.scalar_tensor_tensor(out=wfs[:, 1, :, :], in0=wf[:, :, :], scalar=SCALE, in1=wfs[:, 0, :, :],
                                     op0=ALU.mult, op1=ALU.subtract).then_inc(S["ones"], 1)
            dve.wait_ge(S["bw"], 1)
            dve.wait_ge(S["tb_in"], 16)
            dve.tensor_tensor(brow[:, :], ps[:, 6, 0:D], brow0[:, :], ALU.add).then_inc(S["rows"], 1)
            dve.wait_ge(S["gs"], 1)
            dve.tensor_scalar(gsum[:, :], ps[:, 7, 0:D], SCALE, None, ALU.mult).then_inc(S["rows"], 1)
            dve.wait_ge(S["rows"], 2)

            dve.tensor_copy(idh[:, :], ident).then_inc(S["wst"], 1)
            dve.tensor_copy(trih[:, :], cst[:, C_TRI:C_TRI + P]).then_inc(S["wst"], 1)
            dve.wait_ge(S["ws_in"], 16 * 15)
            dve.tensor_copy(wst[:, 0, :], wstage[:, 0, :]).then_inc(S["wst"], 1)
            dve.tensor_copy(wst[:, 2, :], wstage[:, 1, :]).then_inc(S["wst"], 1)
            dve.tensor_copy(wst[64:P, 3, :], wstage[64:P, 2, :]).then_inc(S["wst"], 1)
            dve.wait_ge(S["wst"], 5)
            dve.tensor_tensor(wst[:, 1, :], wstage[:, 0, :], wst[:, 0, :], ALU.subtract).then_inc(S["wst"], 1)
            dve.tensor_tensor(wst[0:64, 3, :], wstage[0:64, 1, :], wst[0:64, 2, :], ALU.subtract).then_inc(S["wst"], 1)
            dve.tensor_tensor(wst[96:P, 3, :], wstage[96:P, 2, :], wst[96:P, 3, :], ALU.subtract).then_inc(S["wst"], 1)
            dve.wait_ge(S["mem"], 1)
            dve.wait_ge(S["cls_in"], 64)
            dve.wait_ge(S["wst"], 8)
            dve.tensor_copy(code[:, 0, :], cst[:, C_VALID:C_VALID + 2]).then_inc(S["wst"], 1)

            class Norm:

                def __init__(self, x, i, n, name):
                    self.x, self.i, self.n, self.name = x, i, n, name

                def sums(self):
                    for t in range(2):
                        dve.bn_stats(mvs[:, self.i, t, :], self.x(t)).then_inc(S[self.name + "_st"], 1)

                def mean(self):
                    dve.wait_ge(S[self.name + "_st"], 2 * self.n)
                    carried(dve)
                    for t in range(2):
                        dve.bn_aggr(mv[:, self.i, t, :], mvs[:, self.i, t, :]).then_inc(S[self.name + "_mv"], 1)

                def variance(self):
                    dve.wait_ge(S[self.name + "_mv"], 2 * self.n)
                    dve.tensor_scalar(mve[:, self.i, :], mv[:, self.i, :, 1], EPS, None, ALU.add).then_inc(S[self.name + "_var"], 1)

            def step(s, p, half):
                (a, b, m, c, d), (on_a, on_b, on_m, on_c, on_d) = images_of(s)
                norm1 = Norm(lambda t: hx[:, p, t, :], 0, s + 1, "ln1")
                norm2 = Norm(lambda t: rec[:, p, t, 0:D], 1, d + 1, "ln2")

                acc = ps[:, 6, :].rearrange("p (t c) -> p t c", t=2)
                one = xst[:, 1 - p, :, :]
                n0 = s + 1

                def pixels_low():
                    if embeds(s):
                        dve.wait_ge(S["xs_hi"], s + 2)
                        wait(dve, S["embed"], 4 * (s + 1) - 1)
                        at = slice(0, KT // 2)
                        dve.tensor_tensor(xs[:, 1, at, 0:PATCHES], xb[:, 1 - p, at, 0:PATCHES], xs[:, 0, at, 0:PATCHES], ALU.subtract).then_inc(S["xs_lo0"], 1)

                def moments():
                    if embeds(s):
                        dve.wait_ge(S["acc"], 2 * (n0 + 1))
                        dve.tensor_scalar(one[:, 0, :], acc[:, :, D], -1.0 / (TERMS * SCALE), None, ALU.mult).then_inc(S["stat"], 1)
                        dve.tensor_scalar(one[:, 1, :], acc[:, :, D + 1], SCALE ** 2 / TERMS, None, ALU.mult).then_inc(S["stat"], 1)

                def mean_squared():
                    if embeds(s):
                        dve.wait_ge(S["stat"], 3 * n0 + 2)
                        dve.scalar_tensor_tensor(out=one[:, 2, :], in0=one[:, 0, :], scalar=SCALE ** 2, in1=one[:, 0, :],
                                                 op0=ALU.mult, op1=ALU.mult).then_inc(S["stat"], 1)

                def variance0():
                    if embeds(s):
                        dve.wait_ge(S["stat"], 3 * n0 + 3)
                        dve.scalar_tensor_tensor(out=one[:, 2, :], in0=one[:, 1, :], scalar=EPS * SCALE ** 2, in1=one[:, 2, :],
                                                 op0=ALU.add, op1=ALU.subtract).then_inc(S["var"], 1)

                def centred():
                    if embeds(s):
                        for t in range(2):
                            dve.scalar_tensor_tensor(out=hm[:, t, :], in0=gsum[:, :], scalar=one[:, 0, t:t + 1], in1=acc[:, t, 0:D],
                                                     op0=ALU.mult, op1=ALU.add).then_inc(S["hm"], 1)

                def embedded():
                    if embeds(s):
                        dve.wait_ge(S["rstd"], n0 + 1)
                        wait(dve, S[f"hp_out{1 - p}"], 32 * (half + p))
                        for t, n in enumerate((P, REST)):
                            dve.wait_ge(S["hm"], 2 * n0 + t + 1)
                            dve.scalar_tensor_tensor(out=hx[0:n, 1 - p, t, :], in0=hm[0:n, t, :], scalar=one[0:n, 3, t:t + 1], in1=brow[0:n, :],
                                                     op0=ALU.mult, op1=ALU.add).then_inc(S["ho"], 1)

                def queries(u, second):
                    if on_c if second else on_m:
                        n, sem, dst = (c, "q2", q2t) if second else (m, "q", qt)
                        dve.wait_ge(S[sem + "_ps"], 2 * n + u + 1)
                        wait(dve, S["st_ps" if second else "s_ps"], 12 * n)
                        dve.tensor_copy(dst[:, 3 * u:3 * u + 3, 0:TOK], (half7 if second else half6)[:, 0:3, 0:TOK]).then_inc(S[sem + "_cp"], 1)

                def keys(u):
                    if on_m:
                        dve.wait_ge(S["k_ps"], 2 * m + u + 1)
                        wait(dve, S["st_ps"], 12 * (m - 1))
                        dve.tensor_copy(kms[64:P, p, 3 * u:3 * u + 3, 1, 0:TOK], half6[64:P, 0:3, 0:TOK]).then_inc(S["k_cpd"], 1)

                def largest(u):
                    if on_m:
                        q, g = u // 6, u % 6
                        dve.wait_ge(S["s_ps"], 12 * m + u + 1)
                        dve.tensor_reduce(mx[:, q, 2 * g:2 * g + 2], ps[:, u % 2, 0:2 * TOK].rearrange("p (b n) -> p b n", b=2), AX.X, ALU.max).then_inc(S["s_max"], 1)

                def rotate(t):
                    if on_b:
                        dve.wait_ge(S["qk_ps"], 2 * b + t + 1)
                        dve.tensor_tensor(ra[:, t, :], ps[:, 4, 0:2 * D], cst[:, C_COS + t * 2 * D:C_COS + (t + 1) * 2 * D], ALU.mult).then_inc(S["rope_a"], 1)
                        dve.tensor_tensor(rb[:, t, :].rearrange("p (a b) -> p a b", b=2),
                                          ps[:, 4, 0:2 * D].rearrange("p (a b) -> p a b", b=2)[:, :, ::-1],
                                          cst[:, C_SIN + t * 2 * D:C_SIN + (t + 1) * 2 * D].rearrange("p (a b) -> p a b", b=2), ALU.mult).then_inc(S["rope_b"], 1)

                def rotated(t):
                    if on_b:
                        dve.wait_ge(S["rope_a"], 2 * b + t + 1)
                        dve.wait_ge(S["rope_b"], 2 * b + t + 1)
                        wait(dve, S["qk_lo"], 4 * b)
                        wait(dve, S["qk_hi2"], 4 * b)
                        dve.tensor_tensor(qk[:, t, :], ra[:, t, :], rb[:, t, :], ALU.add).then_inc(S["rope"], 1)

                tok = ps[:, 5, 0:3 * P].rearrange("p (h r) -> p h r", r=32)

                def sums(u):
                    if on_c:
                        dve.wait_ge(S["ct_ps"], 2 * c + u + 1)
                        dve.reciprocal(rc[:, u, :], tok[:, :, HD]).then_inc(S["den"], 1)

                def divided(u):
                    if on_c:
                        dve.wait_ge(S["den"], 2 * c + u + 1)
                        wait(dve, S["s2_hi"], 2 * c)
                        wait(dve, S["s2_lo"], c)
                        dve.tensor_tensor(cn[:, u, :].rearrange("p (h r) -> p h r", r=HD), tok[:, :, 0:HD],
                                          rc[:, u, :].unsqueeze(2).broadcast_to([P, HEADS, HD]), ALU.mult).then_inc(S["cn"], 1)

                lg = ps[:, 4, 0:2 * EXPERTS].rearrange("p (t e) -> p t e", t=2)
                iota = cst[:, C_IOTA:C_IOTA + EXPERTS].unsqueeze(1).broadcast_to([P, 2, EXPERTS])
                wide = lambda x: x.unsqueeze(2).broadcast_to([P, 2, EXPERTS])

                def route(n):
                    if not on_d:
                        return
                    if n == 0:
                        dve.wait_ge(S["lg_ps"], d + 1)
                        dve.tensor_reduce(lmx[:, :], lg, AX.X, ALU.max).then_inc(S["route"], 1)
                    elif n == 1:
                        dve.wait_ge(S["route"], 12 * d + 1)
                        wait(dve, S["le"], d)
                        dve.tensor_tensor(ld[:, :, :], lg, wide(lmx[:, :]), ALU.subtract).then_inc(S["route"], 1)
                    elif n == 2:
                        dve.wait_ge(S["route"], 12 * d + 2)
                        dve.scalar_tensor_tensor(out=c8[:, :, :], in0=ld[:, :, :], scalar=0.0, in1=iota, op0=ALU.is_equal, op1=ALU.mult).then_inc(S["route"], 1)
                    elif n == 3:
                        dve.wait_ge(S["route"], 12 * d + 3)
                        dve.tensor_reduce(lsum[:, :], c8[:, :, :], AX.X, ALU.max).then_inc(S["route"], 1)
                    elif n == 4:
                        dve.wait_ge(S["route"], 12 * d + 4)
                        wait(dve, S["pall"], 2 * d)
                        dve.tensor_tensor(code[:, 1, :], lsum[:, :], code[:, 0, :], ALU.mult).then_inc(S["route"], 1)
                    elif n == 5:
                        dve.wait_ge(S["route"], 12 * d + 5)
                        wait(dve, S["cum"], 2 * (d - 1))
                        dve.tensor_tensor(oh[:, p, :, :], iota, wide(code[:, 1, :]), ALU.is_equal).then_inc(S["route"], 1)
                    elif n == 6:
                        dve.wait_ge(S["le"], d + 1)
                        dve.tensor_reduce(lmx[:, :], le[:, :, :], AX.X, ALU.add).then_inc(S["route"], 1)
                    elif n == 7:
                        dve.wait_ge(S["route"], 12 * d + 7)
                        dve.reciprocal(rec[:, p, :, D + 2], lmx[:, :]).then_inc(S["route"], 1)
                    elif n == 8:
                        dve.wait_ge(S["prefix"], d + 1)
                        dve.tensor_tensor(sl[:, :, :], ps[:, 4, 256:256 + 2 * EXPERTS].rearrange("p (t e) -> p t e", t=2),
                                          cst[:, C_SLOT:C_SLOT + EXPERTS].unsqueeze(1).broadcast_to([P, 2, EXPERTS]), ALU.add).then_inc(S["route"], 1)
                    elif n == 9:
                        dve.wait_ge(S["route"], 12 * d + 9)
                        dve.tensor_tensor(sl2[:, :, :], sl[:, :, :], oh[:, p, :, :], ALU.mult).then_inc(S["route"], 1)
                    elif n == 10:
                        dve.wait_ge(S["route"], 12 * d + 10)
                        dve.tensor_reduce(slot[:, :], sl2[:, :, :], AX.X, ALU.add).then_inc(S["route"], 1)
                    elif n == 11:
                        dve.wait_ge(S["route"], 12 * d + 11)
                        dve.tensor_tensor(idx[:, p, :], slot[:, :], cst[:, C_FAR:C_FAR + 2], ALU.add).then_inc(S["route"], 1)

                def sums1():
                    if on_a:
                        dve.wait_ge(S["ho"], 2 * (a + 1))
                        norm1.sums()

                def mean1():
                    if on_a:
                        norm1.mean()

                def variance1():
                    if on_a:
                        norm1.variance()

                def normal1():
                    if on_a:
                        dve.wait_ge(S["ln1_rstd"], a + 1)
                        wait(dve, S["s1_hi"], 2 * a)
                        wait(dve, S["s1_lo"], a)
                        for t in range(2):
                            dve.tensor_scalar(hn[:, t, :], hx[:, p, t, :], mv[:, 0, t, 0:1], rstd1[:, t:t + 1], ALU.subtract, ALU.mult).then_inc(S["ln1_hn"], 1)

                def added():
                    if on_d:
                        dve.wait_ge(S["wo_ps"], d + 1)
                        dve.wait_ge(S[f"hr_in{p}"], 32 * (half - 1))
                        wait(dve, S[f"sc_done{p}"], 32 * (half - 2))
                        dve.tensor_tensor(rec[:, p, :, 0:D], ps[:, 5, 0:2 * D].rearrange("p (t d) -> p t d", t=2), hr[:, p, :, :], ALU.add).then_inc(S["h2"], 1)

                def sums2():
                    if on_d:
                        dve.wait_ge(S["h2"], d + 1)
                        wait(dve, S["rec_m"], d)
                        norm2.sums()

                def mean2():
                    if on_d:
                        norm2.mean()

                def variance2():
                    if on_d:
                        norm2.variance()

                def normal2():
                    if on_d:
                        dve.wait_ge(S["ln2_rstd"], d + 1)
                        wait(dve, S["s3_hi"], 2 * d)
                        wait(dve, S["s3_lo"], d)
                        for t in range(2):
                            dve.tensor_scalar(xn[:, t, :], rec[:, p, t, 0:D], mv[:, 1, t, 0:1], rec[:, p, t, D + 1:D + 2], ALU.subtract, ALU.mult).then_inc(S["xn"], 1)

                def minus_maxima():
                    if on_m:
                        dve.wait_ge(S["s_max"], 12 * (m + 1))
                        dve.wait_ge(S["q_ps"], 2 * (m + 1))
                        dve.tensor_scalar(qks[:, p, :, 0:HEADS, 3, 0], mx[:, :, :], -1.0, None, ALU.mult).then_inc(S["m_hi"], 1)
                        dve.wait_ge(S["m_hi"], m + 1)
                        dve.scalar_tensor_tensor(out=qks[:, p, :, 0:HEADS, 3, 1], in0=mx[:, :, :], scalar=-1.0, in1=qks[:, p, :, 0:HEADS, 3, 0],
                                                 op0=ALU.mult, op1=ALU.subtract).then_inc(S["m_lo"], 1)

                queries(0, True)
                keys(0)
                sums1()
                added()
                mean1()
                keys(1)
                variance1()
                rotate(0)
                queries(1, True)
                queries(0, False)
                sums2()
                normal1()
                largest(0)
                mean2()
                variance2()
                largest(1)
                queries(1, False)
                largest(2)
                normal2()
                rotated(0)
                largest(3)
                largest(4)
                pixels_low()
                rotate(1)
                sums(0)
                divided(0)
                largest(5)
                largest(6)
                sums(1)
                divided(1)
                largest(7)
                rotated(1)
                largest(8)
                largest(9)
                route(0)
                route(1)
                route(2)
                route(3)
                route(4)
                largest(10)
                route(5)
                route(6)
                largest(11)
                route(7)
                minus_maxima()
                moments()
                route(8)
                mean_squared()
                variance0()
                centred()
                route(9)
                route(10)
                route(11)
                embedded()
            run_images(dve, step)

        def early_done(eng):
            eng.wait_ge(S["early"], 4)

        def run_tiles(eng, step):
            for s in range(8):
                step(s, s % 2, s, 0)
            whole = (PAIRS - 8) // 8
            with eng.Fori(0, whole) as i:
                for r in range(8):
                    step(8 * i + (8 + r), r % 2, r, i + 1)
            for s in range(8 + 8 * whole, PAIRS + 4):
                step(s, s % 2, s % 8, s // 8)

        def within(s, back):
            return not isinstance(s, int) or 0 <= s - back < PAIRS

        @block.sync
        def _(sp):
            early_done(sp)
            sp.dma_start(c3[:, :], consts3).then_inc(S["c3_in"], 16)
            sp.wait_ge(S["f_zero"], 2)
            for r in (0, 32):
                sp.dma_start(fb2[r:r + 1, :, :], b2.rearrange("(a e) d -> a e d", a=1)).then_inc(S["b2_in"], 16)

            def weights(e):
                q = e % 2
                wait(sp, S["f_hi"], 4 * (e - 1))
                wait(sp, S["f_lo"], 4 * (e - 1))
                sp.dma_start(f1[:, q, 0, :], w1[e, 0:P, :]).then_inc(S[f"f_in{q}"], 16)
                for r in (0, 64):
                    sp.dma_start(f1[r:r + 64, q, 1, :], w1[e, P:D, :]).then_inc(S[f"f_in{q}"], 16)
                for r in (64, 96):
                    sp.dma_start(f1[r:r + 1, q, 2, :], b1[e:e + 1, :]).then_inc(S[f"f_in{q}"], 16)
                sp.dma_start(f2[:, q, :, :], w2[e].rearrange("(f p) d -> p f d", p=P)).then_inc(S[f"f_in{q}"], 16)
            weights(0)
            weights(1)
            sp.wait_ge(S["plan"], PLAN["prow"])
            sp.dma_start(pflat.rearrange("a i n -> i a n"), prow[:, :, :]).then_inc(S["pf_out"], 16)
            sp.wait_ge(S["pf_out"], 16)
            for e in range(EXPERTS):
                sp.dma_start(eb[16 * e:16 * e + 16, :, :], pflat.rearrange("a i n -> a (i n)").rearrange("a (c n) -> c a n", c=16)).then_inc(S["eb_in"], 16)
            for e in range(2, EXPERTS):
                weights(e)
            sp.wait_ge(S["padrec"], 1)
            for t in range(2):
                sp.dma_start(records[DUMMY + t * P:DUMMY + (t + 1) * P, :], padrec[:, :]).then_inc(S["pad_out"], 16)
            for q in range(2):
                sp.wait_ge(S[f"sc_done{q}"], 16 * IMAGES)
            sp.wait_ge(S["tail_out"], 32 * EXPERTS)
            sp.wait_ge(S["pad_out"], 32)
            sp.wait_ge(S["plan"], PLAN["tables"])

            def step(s, p, r, q):
                if within(s, 0):
                    row = sp.value_load(rowt[0:1, bass.ds(s, 1)], min_val=0, max_val=DUMMY)
                    wait(sp, S[f"y_out{r}"], 32 * q)
                    sp.dma_start(xr[:, r, :, :], records[bass.ds(row, PT), :].rearrange("(t p) c -> p t c", p=P)).then_inc(S[f"x4_in{r}"], 16)
            run_tiles(sp, step)
            for r in range(8):
                sp.wait_ge(S[f"y_out{r}"], 32 * len(range(r, PAIRS, 8)))

        @block.gpsimd
        def _(pool):
            for q in range(2):
                pool.wait_ge(S[f"sc_done{q}"], 16 * IMAGES)
            pool.drain().then_inc(S["early"], 1)
            early_done(pool)
            for a in (f1[:, 0, 2, :], f1[:, 1, 2, :]):
                pool.memset(a, 0.0).then_inc(S["f_zero1"], 1)
            pool.memset(fb2[:, :, :], 0.0).then_inc(S["f_zero"], 1)
            pool.wait_ge(S["f_zero1"], 2)
            pool.wait_ge(S["f_zero"], 1)
            pool.memset(padrec[:, :], 0.0).then_inc(S["f_zero"], 1)
            pool.memset(st4[:, :, :, :, :], 0.0).then_inc(S["st4_zero"], 1)
            pool.wait_ge(S["f_zero"], 2)
            pool.wait_ge(S["st4_zero"], 1)
            pool.memset(st4[:, :, :, 0, D:256:32].rearrange("p a t c -> p (a t) c"), 1.0).then_inc(S["st4"], 1)
            pool.wait_ge(S["c3_in"], 16)
            pool.tensor_copy(padrec[:, REC - 1:REC].bitcast(U32), c3[:, K_PAD:K_PAD + 1]).then_inc(S["padrec"], 1)

            def lows(e):
                q = e % 2
                pool.wait_ge(S["f_hi"], 4 * (e + 1))
                hi1, hi2 = w1s[:, e, :], w2s[:, e, :].rearrange("p (f s d) -> p f s d", f=FT, s=2)
                pool.tensor_tensor(hi1[:, FF:2 * FF], f1[:, q, 0, :], hi1[:, 0:FF], ALU.subtract).then_inc(S["f_lo"], 1)
                pool.wait_ge(S["f_lo"], 4 * e + 1)
                pool.tensor_tensor(hi1[0:64, 3 * FF:4 * FF], f1[0:64, q, 1, :], hi1[0:64, 2 * FF:3 * FF], ALU.subtract).then_inc(S["f_lo"], 1)
                pool.wait_ge(S["f_lo"], 4 * e + 2)
                pool.tensor_tensor(hi1[96:P, 3 * FF:4 * FF], f1[96:P, q, 2, :], hi1[96:P, 3 * FF:4 * FF], ALU.subtract).then_inc(S["f_lo"], 1)
                pool.wait_ge(S["f_lo"], 4 * e + 3)
                pool.tensor_tensor(hi2[:, :, 1, :], f2[:, q, :, :], hi2[:, :, 0, :], ALU.subtract).then_inc(S["f_lo"], 1)
            pool.wait_ge(S["b2_hi"], 1)
            pool.wait_ge(S["padrec"], 1)
            pool.tensor_tensor(b2s[32:64, :, :], fb2[32:64, :, :], b2s[32:64, :, :], ALU.subtract).then_inc(S["b2_lo"], 1)
            pool.wait_ge(S["b2_lo"], 1)
            lows(0)
            pool.wait_ge(S["plan"], PLAN["tails"])
            pool.wait_ge(S["padrec"], 1)
            for e in range(EXPERTS):
                for t in range(2):
                    pool.indirect_dma_start(records, bass.IndirectOffsetOnAxis(ap=tails[:, t, e:e + 1], axis=0), padrec[:, :],
                                            None, bounds_check=DUMMY - 1, oob_is_err=False).then_inc(S["tail_out"], 16)
            pool.wait_ge(S["tail_out"], 32 * EXPERTS)
            for e in range(1, EXPERTS):
                lows(e)
            pool.wait_ge(S["plan"], PLAN["tables"])

            def step(s, p, r, q):
                if within(s, 0):
                    two = lambda i: small[:, p, 2 * i:2 * i + 2]
                    prob, number = xr[:, r, :, D + 2], xr[:, r, :, REC - 1].bitcast(U32)
                    threshold, last = small[:, p, 0:1], small[:, p, 1:2]
                    pool.wait_ge(S[f"x4_in{r}"], 16 * (q + 1))
                    carried(pool)
                    pool.tensor_copy(two(0), tct[:, :, bass.ds(s, 1)].rearrange("p a n -> p (a n)")).then_inc(S["kept"], 1)
                    pool.tensor_copy(two(1), number).then_inc(S["kept"], 1)
                    pool.wait_ge(S["kept"], 9 * s + 2)
                    carried(pool)
                    pool.tensor_scalar(two(2), prob, threshold, None, ALU.is_equal).then_inc(S["kept"], 1)
                    pool.tensor_scalar(two(3), two(1), last, None, ALU.is_le).then_inc(S["kept"], 1)
                    pool.tensor_scalar(two(4), prob, threshold, None, ALU.is_gt).then_inc(S["kept"], 1)
                    pool.wait_ge(S["kept"], 9 * s + 4)
                    pool.tensor_tensor(two(5), two(2), two(3), ALU.mult).then_inc(S["kept"], 1)
                    pool.wait_ge(S["kept"], 9 * s + 6)
                    pool.tensor_tensor(two(1), two(4), two(5), ALU.add).then_inc(S["kept"], 1)
                    pool.wait_ge(S["kept"], 9 * s + 7)
                    wait(pool, S["fin"], 2 * (s - 3))
                    pool.tensor_tensor(keepp[:, r % 4, 0, :], two(1), prob, ALU.mult).then_inc(S["kept"], 1)
                    pool.wait_ge(S["kept"], 9 * s + 8)
                    pool.tensor_tensor(keepp[:, r % 4, 1, :], prob, keepp[:, r % 4, 0, :], ALU.subtract).then_inc(S["kept"], 1)
                if within(s, 4):
                    o = (r + 4) % 8
                    pool.wait_ge(S["fin"], 2 * (s - 3))
                    carried(pool)
                    for t in range(2):
                        pool.indirect_dma_start(out, bass.IndirectOffsetOnAxis(ap=xr[:, o, t, REC - 1:REC].bitcast(U32), axis=0), orow[:, p, t, :],
                                                None, bounds_check=NTOK - 1, oob_is_err=False).then_inc(S[f"y_out{o}"], 16)
            run_tiles(pool, step)

        @block.scalar
        def _(act):
            act.drain().then_inc(S["early"], 1)
            early_done(act)
            act.wait_ge(S["b2_in"], 32)
            act.activation(b2s[:, :, :], fb2[:, :, :], ACT.Copy).then_inc(S["b2_hi"], 1)
            for e in range(EXPERTS):
                q = e % 2
                act.wait_ge(S[f"f_in{q}"], 96 * (e // 2 + 1))
                hi1, hi2 = w1s[:, e, :], w2s[:, e, :].rearrange("p (f s d) -> p f s d", f=FT, s=2)
                act.activation(hi1[:, 0:FF], f1[:, q, 0, :], ACT.Copy).then_inc(S["f_hi"], 1)
                act.activation(hi1[:, 2 * FF:3 * FF], f1[:, q, 1, :], ACT.Copy).then_inc(S["f_hi"], 1)
                act.activation(hi1[64:P, 3 * FF:4 * FF], f1[64:P, q, 2, :], ACT.Copy).then_inc(S["f_hi"], 1)
                act.activation(hi2[:, :, 0, :], f2[:, q, :, :], ACT.Copy).then_inc(S["f_hi"], 1)
            act.wait_ge(S["st4"], 1)

            def step(s, p, r, q):
                def gelu(i):
                    act.wait_ge(S["h_ps"], 3 * (s - 2) + 1 + i)
                    wait(act, S["hl"], 3 * (s - 3))
                    act.activation(hf[:, p, 2 * PT * i:2 * PT * (i + 1)], ps[:, 1 + 3 * p + i, :], ACT.Gelu).then_inc(S["hf"], 1)

                def high(i):
                    act.wait_ge(S["hf"], 3 * (s - 2) + 1 + i)
                    wait(act, S["y_ps"], s - 3)
                    act.activation(hh[:, p, 2 * PT * i:2 * PT * (i + 1)], hf[:, p, 2 * PT * i:2 * PT * (i + 1)], ACT.Copy).then_inc(S["hh"], 1)

                if within(s, 2):
                    gelu(0)
                    high(0)
                if within(s, 0):
                    act.wait_ge(S["xn4"], 2 * (s + 1))
                    wait(act, S["t4_ps"], s - 1)
                    act.activation(st4[:, p, :, 0, 0:D], xn4[:, p, :, :], ACT.Copy).then_inc(S["x_hi"], 1)
                    act.activation(st4[:, p, :, 1, D:256], xn4[:, p, :, P:D], ACT.Copy).then_inc(S["x_hi"], 1)
                if within(s, 2):
                    gelu(1)
                    high(1)
                if within(s, 1):
                    act.wait_ge(S["t4_ps"], s)
                    wait(act, S["h_ps"], 3 * (s - 2))
                    act.activation(xt4[:, 1 - p, :, :], ps[:, 0, :].bitcast(F16).rearrange("p (c n) -> p c n", c=4), ACT.Copy).then_inc(S["xt4"], 1)
                if within(s, 2):
                    gelu(2)
                    high(2)
            run_tiles(act, step)

        @block.tensor
        def _(pe):
            pe.drain().then_inc(S["early"], 1)
            early_done(pe)
            pe.wait_ge(S["pall"], 2 * IMAGES)
            for a in range(2):
                for t in range(2):
                    pe.transpose(ps[0:IMAGES, a, t * P:(t + 1) * P], pall[:, a, t, :], ident).then_inc(S["pt_ps"], 1)
            pe.wait_ge(S["c3_in"], 16)
            total = lambda o, w, x, name: pe.matmul(o, w, x, start=True, stop=True).then_inc(S[name], 1)
            block_sum = c3[:, K_BLOCK:K_BLOCK + P]
            pe.wait_ge(S["plan"], PLAN["n_cnt"])
            total(ps[:, 3, 0:1], block_sum, cols["cnt"][:, :], "sums")
            pe.wait_ge(S["plan"], PLAN["ntile"])
            total(ps[:, 3, 1:2], c3[:, K_UPTO:K_UPTO + P], cols["ntile"][:, :], "sums")
            pe.wait_ge(S["plan"], PLAN["onef"])
            pe.wait_ge(S["plan"], PLAN["dn"])
            total(ps[:, 4, 0:EXPERTS], onef[:, :], dn[:, :], "sums")
            with pe.Fori(0, STEPS // 5) as i:
                for n in (5 * i + j for j in range(5)):
                    pe.wait_ge(S["count"], n + 1)
                    total(ps[:, 2, 0:1], block_sum, cols["cnt"][:, :], "sum_ps")
            pe.wait_ge(S["plan"], PLAN["g_cnt"])
            total(ps[:, 3, 2:3], block_sum, cols["cnt"][:, :], "sums")
            pe.wait_ge(S["plan"], PLAN["tied"])
            total(ps[:, 4, 8:9], c3[:, K_BEFORE:K_BEFORE + P], tied[:, CHUNK - 1:CHUNK], "sums")
            pe.wait_ge(S["plan"], PLAN["cut_cnt"])
            total(ps[:, 3, 3:4], block_sum, cols["cutc"][:, :], "sums")
            pe.wait_ge(S["plan"], PLAN["vals_all"])
            total(ps[:, 5, 0:4 * PAIRS], onef[:, :], vals[:, :, :].rearrange("p a n -> p (a n)"), "sums")
            pe.wait_ge(S["plan"], PLAN["tables"])
            pe.wait_ge(S["f_hi"], 4 * EXPERTS)
            pe.wait_ge(S["f_lo"], 4 * EXPERTS)
            pe.wait_ge(S["b2_lo"], 1)

            expert = {}

            def step(s, p, r, q):
                load = lambda n: pe.value_load(expt[0:1, bass.ds(n, 1)], min_val=0, max_val=EXPERTS - 1)
                expert["before"] = load(s - 3) if r == 0 and within(s, 3) else expert.get("last")
                if within(s, 1):
                    pe.wait_ge(S["x_lo"], s)
                    pe.wait_ge(S["x_hi"], 2 * s)
                    wait(pe, S["xt4"], s - 1)
                    o = ps[:, 0, :].bitcast(F16).rearrange("p (c n) -> p c n", c=4)
                    for t in range(2):
                        a = st4[:, 1 - p, t, :, :]
                        for c, src in enumerate((a[:, 0, 0:P], a[:, 1, 0:P], a[:, 1, P:256], a[:, 0, P:256])):
                            last = pe.transpose(o[:, c, t * P:(t + 1) * P], src, idh[:, :])
                    last.then_inc(S["t4_ps"], 1)
                if within(s, 2):
                    e = expert["last"] = load(s - 2)
                    pe.wait_ge(S["xt4"], s - 1)
                    wait(pe, S["hf"], 3 * (s - 3))
                    for f in range(FT):
                        for i, (a, w) in enumerate(((0, 0), (0, 1), (1, 0), (2, 2), (3, 3))):
                            last = pe.matmul(ps[:, 1 + 3 * p + f // 2, (f % 2) * PT:(f % 2 + 1) * PT],
                                             w1s[:, bass.ds(e, 1), w * FF + f * P:w * FF + (f + 1) * P], xt4[:, p, a, :],
                                             start=(i == 0), stop=(i == 4))
                        if f % 2 == 1:
                            last.then_inc(S["h_ps"], 1)
                if within(s, 3):
                    e = expert["before"]
                    pe.wait_ge(S["hh"], 3 * (s - 2))
                    pe.wait_ge(S["hl"], 3 * (s - 2))
                    wait(pe, S["fin"], 2 * (s - 3))
                    for t in range(2):
                        y = ps[:, 7, t * D:(t + 1) * D]
                        pe.matmul(y, oneh[:, :], b2s[:, bass.ds(e, 1), :], start=True, stop=False)
                        for f in range(FT):
                            at = f * PT + t * P
                            for i, (a, w) in enumerate(((hh, 0), (hh, 1), (hl, 0))):
                                last = pe.matmul(y, a[:, 1 - p, at:at + P], w2s[:, bass.ds(e, 1), (2 * f + w) * D:(2 * f + w + 1) * D],
                                                 start=False, stop=(f == FT - 1 and i == 2))
                    last.then_inc(S["y_ps"], 1)
            run_tiles(pe, step)

        @block.vector
        def _(dve):
            dve.drain().then_inc(S["early"], 1)
            early_done(dve)
            dve.memset(onef[:, :], 1.0).then_inc(S["plan"], 1)
            dve.memset(one788[:, :], 1.0).then_inc(S["plan"], 1)
            dve.memset(cols["lo"][:, :], 0.0).then_inc(S["lo"], 1)
            dve.memset(cols["stepc"][:, :], 1.0).then_inc(S["halved"], 1)
            dve.memset(cols["cand"][:, :], 1.0).then_inc(S["cand"], 1)
            for a in range(2):
                for n, (to, at, length) in enumerate(((1, 0, P), (1 + P, P, REST), (0, P + REST, 1))):
                    dve.wait_ge(S["pt_ps"], 2 * a + 2)
                    dve.tensor_copy(prow[:, a, to:to + length], ps[0:IMAGES, a, at:at + length]).then_inc(S["plan"], 1)
            C = {n: c[:, :] for n, c in cols.items()}
            first = c3[:, K_FIRST:K_FIRST + 1]
            iota, iota256 = c3[:, K_IOTA:K_IOTA + P], c3[:, K_IOTA256:K_IOTA256 + P]
            dve.wait_ge(S["c3_in"], 16)
            dve.wait_ge(S["eb_in"], 16 * EXPERTS)
            dve.scalar_tensor_tensor(out=pe_e[:, :], in0=eb[:, 1, :], scalar=c3[:, K_CODE:K_CODE + 1], in1=eb[:, 0, :],
                                     op0=ALU.is_equal, op1=ALU.mult).then_inc(S["plan"], 1)
            dve.wait_ge(S["plan"], PLAN["pe_e"])

            def count(src, bound, op, acc, name, n=CHUNK):
                dve.tensor_scalar(scr[:, 0:n], src, bound, None, op, ALU.add, accum_out=C[acc]).then_inc(S[name], 1)
            count(pe_e[:, :], 0.0, ALU.is_gt, "cnt", "plan")
            dve.wait_ge(S["sums"], SUMS["n"])
            dve.tensor_copy(C["n_e"], ps[:, 3, 0:1]).then_inc(S["plan"], 1)
            dve.wait_ge(S["plan"], PLAN["n_e"])
            dve.wait_ge(S["plan"], PLAN["n_cnt"])
            count(iota256, C["n_e"], ALU.is_lt, "ntile", "plan", P)
            dve.tensor_scalar(dn[:, :], c3[:, K_SEL:K_SEL + EXPERTS], C["n_e"], None, ALU.mult).then_inc(S["plan"], 1)
            dve.wait_ge(S["sums"], SUMS["end"])
            dve.wait_ge(S["plan"], PLAN["ntile"])
            dve.tensor_copy(C["end"], ps[:, 3, 1:2]).then_inc(S["plan"], 1)
            dve.wait_ge(S["sums"], SUMS["tail"])
            for t in range(2):
                dve.scalar_tensor_tensor(out=tails[:, t, :], in0=ps[:, 4, 0:EXPERTS], scalar=float(t * P), in1=c3[:, K_TAIL:K_TAIL + EXPERTS],
                                         op0=ALU.add, op1=ALU.add).then_inc(S["plan"], 1)
            dve.wait_ge(S["plan"], PLAN["end"])
            dve.tensor_tensor(C["start"], C["end"], C["ntile"], ALU.subtract).then_inc(S["plan"], 1)
            with dve.Fori(0, STEPS // 5) as i:
                for n in (5 * i + j for j in range(5)):
                    dve.wait_ge(S["cand"], n + 1)
                    count(pe_e[:, :], C["cand"], ALU.is_ge, "cnt", "count")
                    dve.tensor_scalar(C["stepc"], C["stepc"], 0.5, None, ALU.mult).then_inc(S["halved"], 1)
                    dve.wait_ge(S["halved"], 2 * n + 2)
                    dve.wait_ge(S["lo"], n + 1)
                    dve.tensor_tensor(C["below"], C["lo"], C["stepc"], ALU.add).then_inc(S["halved"], 1)
                    dve.wait_ge(S["sum_ps"], n + 1)
                    dve.scalar_tensor_tensor(out=C["took"], in0=ps[:, 2, 0:1], scalar=float(CAP), in1=C["cand"], op0=ALU.is_ge, op1=ALU.mult).then_inc(S["took"], 1)
                    dve.wait_ge(S["took"], n + 1)
                    dve.wait_ge(S["halved"], 2 * n + 3)
                    dve.scalar_tensor_tensor(out=C["cand"], in0=C["took"], scalar=C["stepc"], in1=C["below"], op0=ALU.add, op1=ALU.max).then_inc(S["cand"], 1)
                    dve.tensor_tensor(C["lo"], C["took"], C["lo"], ALU.max).then_inc(S["lo"], 1)
            dve.wait_ge(S["lo"], STEPS + 1)
            dve.wait_ge(S["count"], STEPS)
            count(pe_e[:, :], C["lo"], ALU.is_gt, "cnt", "plan")
            dve.tensor_scalar(tie[:, :], pe_e[:, :], C["lo"], None, ALU.is_equal).then_inc(S["plan"], 1)
            dve.wait_ge(S["plan"], PLAN["tie"])
            dve.wait_ge(S["plan"], PLAN["one788"])
            dve.tensor_tensor_scan(tied[:, :], one788[:, :], tie[:, :], 0.0, ALU.mult, ALU.add).then_inc(S["plan"], 1)
            dve.wait_ge(S["sums"], SUMS["g"])
            dve.tensor_scalar(C["room"], ps[:, 3, 2:3], -1.0, float(CAP), ALU.mult, ALU.add).then_inc(S["plan"], 1)
            dve.wait_ge(S["sums"], SUMS["before"])
            dve.wait_ge(S["plan"], PLAN["room"])
            dve.tensor_tensor(C["lim"], C["room"], ps[:, 4, 8:9], ALU.subtract).then_inc(S["plan"], 1)
            dve.wait_ge(S["plan"], PLAN["lim"])
            dve.wait_ge(S["plan"], PLAN["tied"])
            dve.wait_ge(S["plan"], PLAN["g_cnt"])
            count(tied[:, :], C["lim"], ALU.is_lt, "cutc", "plan")
            dve.wait_ge(S["plan"], PLAN["start"])
            dve.tensor_scalar(ended[:, :], iota, C["end"], first, ALU.is_lt, ALU.mult).then_inc(S["plan"], 1)
            dve.scalar_tensor_tensor(out=C["vrow"], in0=C["start"], scalar=-float(PT), in1=c3[:, K_REGION:K_REGION + 1],
                                     op0=ALU.mult, op1=ALU.add).then_inc(S["plan"], 1)
            dve.wait_ge(S["plan"], PLAN["sel_a"])
            dve.scalar_tensor_tensor(out=sel[:, :], in0=iota, scalar=C["start"], in1=ended[:, :], op0=ALU.is_ge, op1=ALU.mult).then_inc(S["plan"], 1)
            dve.wait_ge(S["plan"], PLAN["sel"])
            dve.wait_ge(S["plan"], PLAN["vrow"])
            dve.scalar_tensor_tensor(out=vals[:, 0, :], in0=iota256[:, 0:PAIRS], scalar=C["vrow"], in1=sel[:, 0:PAIRS],
                                     op0=ALU.add, op1=ALU.mult).then_inc(S["plan"], 1)
            dve.tensor_scalar(vals[:, 1, :], sel[:, 0:PAIRS], c3[:, K_EXPERT:K_EXPERT + 1], None, ALU.mult).then_inc(S["plan"], 1)
            dve.tensor_scalar(vals[:, 2, :], sel[:, 0:PAIRS], C["lo"], None, ALU.mult).then_inc(S["plan"], 1)
            dve.wait_ge(S["sums"], SUMS["cut"])
            dve.wait_ge(S["plan"], PLAN["cut_cnt"])
            dve.tensor_copy(C["cutc"], ps[:, 3, 3:4]).then_inc(S["plan"], 1)
            dve.wait_ge(S["plan"], PLAN["cut"])
            dve.tensor_scalar(vals[:, 3, :], sel[:, 0:PAIRS], C["cutc"], None, ALU.mult).then_inc(S["plan"], 1)
            dve.wait_ge(S["sums"], SUMS["table"])
            table = ps[:, 5, 0:4 * PAIRS].rearrange("p (a n) -> p a n", a=4)
            dve.tensor_scalar(rowt[:, :], table[:, 0, :], float(DUMMY), None, ALU.add).then_inc(S["plan"], 1)
            dve.tensor_copy(expt[:, :], table[:, 1, :]).then_inc(S["plan"], 1)
            dve.tensor_copy(tct[:, :, :], table[:, 2:4, :]).then_inc(S["plan"], 1)
            dve.wait_ge(S["st4"], 1)

            def step(s, p, r, q):
                def low(i):
                    dve.wait_ge(S["hh"], 3 * (s - 2) + 1 + i)
                    wait(dve, S["y_ps"], s - 3)
                    c = slice(2 * PT * i, 2 * PT * (i + 1))
                    dve.tensor_tensor(hl[:, p, c], hf[:, p, c], hh[:, p, c], ALU.subtract).then_inc(S["hl"], 1)

                x = xr[:, r, :, :]
                if within(s, 4):
                    dve.wait_ge(S["y_ps"], s - 3)
                    if not isinstance(s, int) or s >= 6:
                        dve.wait_ge(S[f"y_out{(r + 2) % 8}"], 32 * (q + 1 if r >= 6 else q))
                    for t in range(2):
                        dve.scalar_tensor_tensor(out=orow[:, p, t, :], in0=ps[:, 7, t * D:(t + 1) * D], scalar=keepp[:, r % 4, 0, t:t + 1],
                                                 in1=base[:, r % 4, t, :], op0=ALU.mult, op1=ALU.add).then_inc(S["fin"], 1)
                if within(s, 0):
                    dve.wait_ge(S[f"x4_in{r}"], 16 * (q + 1))
                    wait(dve, S["x_hi"], 2 * (s - 1))
                    wait(dve, S["x_lo"], s - 1)
                    for t in range(2):
                        dve.tensor_scalar(xn4[:, p, t, :], x[:, t, 0:D], x[:, t, D:D + 1], x[:, t, D + 1:D + 2], ALU.subtract, ALU.mult).then_inc(S["xn4"], 1)
                if within(s, 2):
                    low(0)
                    low(1)
                if within(s, 0):
                    dve.wait_ge(S["x_hi"], 2 * s + 1)
                    dve.wait_ge(S["xn4"], 2 * (s + 1))
                    wait(dve, S["t4_ps"], s - 1)
                    dve.tensor_tensor(st4[:, p, :, 1, 0:D], xn4[:, p, :, :], st4[:, p, :, 0, 0:D], ALU.subtract).then_inc(S["x_lo"], 1)
                if within(s, 2):
                    low(2)
                if within(s, 0):
                    dve.wait_ge(S["kept"], 9 * s + 9)
                    dve.wait_ge(S["xn4"], 2 * (s + 1))
                    for t in range(2):
                        dve.scalar_tensor_tensor(out=base[:, r % 4, t, :], in0=xn4[:, p, t, :], scalar=keepp[:, r % 4, 1, t:t + 1], in1=x[:, t, 0:D],
                                                 op0=ALU.mult, op1=ALU.add)
            run_tiles(dve, step)

def constants3():
    import numpy as np
    c = np.zeros((P, N_CONST3), np.float32)
    e, k = np.arange(P) // 16, np.arange(P) % 16
    same = e[:, None] == e[None]
    c[:, K_BLOCK:K_BLOCK + P] = same
    c[:, K_BEFORE:K_BEFORE + P] = same & (k[:, None] < k[None])
    c[:, K_UPTO:K_UPTO + P] = (k[:, None] == 0) & (e[:, None] <= e[None])
    c[:, K_IOTA:K_IOTA + P] = np.arange(P)
    c[:, K_IOTA256:K_IOTA256 + P] = PT * np.arange(P)
    c[:, K_SEL:K_SEL + EXPERTS] = (k[:, None] == 0) & (e[:, None] == np.arange(EXPERTS))
    c[:, K_TAIL:K_TAIL + EXPERTS] = np.arange(EXPERTS) * REGION + np.arange(P)[:, None]
    c[:, K_FIRST] = k == 0
    c[:, K_CODE] = EXPERTS - e
    c[:, K_REGION] = e * REGION - DUMMY
    c[:, K_EXPERT] = e
    c[:, K_PAD] = FAR
    return c


_OTHERS = ("L0_tok_b", "cls_tok", "L0_attn_W_qkv", "L0_attn_b_qkv", "L0_attn_W_out", "L0_attn_b_out", "L0_ffn_switch_w",
           "L0_ffn_switch_b", "L0_ffn_w1", "L0_ffn_b1", "L0_ffn_w2", "L0_ffn_b2")


def kernel(x, cls_tok, L0_tok_ln_gamma, L0_tok_ln_beta, L0_tok_W, **others):
    import numpy as np
    import concourse.bacc as bacc
    from concourse.bass_utils import run_bass_kernel_spmd

    xt, wr, gr, br, mult = lay_out(np.asarray(x), np.asarray(L0_tok_ln_gamma), np.asarray(L0_tok_ln_beta), np.asarray(L0_tok_W))
    given = {"xt": xt, "wr": wr, "gr": gr, "br": br}
    for name in _OTHERS:
        a = np.ascontiguousarray(cls_tok if name == "cls_tok" else others[name])
        given[name] = a.reshape(1, D) if name == "cls_tok" else a
    given.update(c=constants(mult), c3=constants3())
    nc = bacc.Bacc("TRN2", target_bir_lowering=False, num_devices=1)
    arrays, args = {}, []
    for name, a in given.items():
        arrays[f"in_{name}_dram"] = a
        args.append(nc.dram_tensor(f"in_{name}_dram", a.shape, mybir.dt.from_np(a.dtype), kind="ExternalInput").ap())
    args.append(nc.dram_tensor("out_0_dram", (NTOK, D), F32, kind="ExternalOutput").ap())
    build(nc, *args)
    r = run_bass_kernel_spmd(nc, [arrays], core_ids=[0])
    return r.results[0]["out_0_dram"].reshape(IMAGES, TOK, D)


def layout():
    import numpy as np
    moves = [(0, 0), (0, 1), (0, -1), (1, 0), (-1, 0)]
    where = {}
    for s, (dy, dx) in enumerate(moves):
        for y in range(PATCH):
            for x in range(PATCH):
                for c in range(CH):
                    where.setdefault((c, y - dy, x - dx), []).append(((y * PATCH + x) * 5 + s) * CH + c)
    rows, mult = [], np.zeros(KP, np.float32)
    p = 0
    for m in (5, 4, 3, 1):
        pixels = [k for k in sorted(where) if len(where[k]) == m]
        n = -(-len(pixels) // KT)
        mult[p:p + n] = m
        rows += [(p + i // KT, i % KT, k, where[k]) for i, k in enumerate(pixels)]
        p += n
    assert p == KP
    return rows, mult


def lay_out(x, ln_gamma, ln_beta, w):
    import numpy as np
    rows, mult = layout()
    pad = np.zeros((IMAGES, CH, 226, 226), np.float32)
    pad[:, :, 1:225, 1:225] = x
    xt = np.zeros((KP, KT, IMAGES, SIDE, SIDE), np.float32)
    wr = np.zeros((KP, KT, SHIFTS, D), np.float32)
    gr = np.zeros((KP, KT, SHIFTS), np.float32)
    br = np.zeros((KP, KT, SHIFTS), np.float32)
    for p, k, (c, y, xx), terms in rows:
        xt[p, k] = pad[:, c, y + 1:y + 1 + 209:PATCH, xx + 1:xx + 1 + 209:PATCH]
        for s, e in enumerate(terms):
            wr[p, k, s], gr[p, k, s], br[p, k, s] = w[e], ln_gamma[e], ln_beta[e]
    xt = np.ascontiguousarray(xt.reshape(KP, KT, IMAGES, PATCHES).transpose(2, 0, 1, 3))
    return xt, wr, gr, br, mult


def constants(mult):
    import numpy as np
    c = np.zeros((P, N_CONST), np.float32)
    c[:, C_ID:C_ID + P] = np.eye(P)
    c[:, C_TRI:C_TRI + P] = np.triu(np.ones((P, P)))
    place = np.zeros((2, P), np.int64)
    place[0] = 1 + np.arange(P)
    place[1, :REST] = 1 + P + np.arange(REST)
    freqs = np.arange(TOK, dtype=np.float32)[:, None] / np.float32(10000.0) ** (np.arange(0, HD, 2, dtype=np.float32) / np.float32(HD))[None]
    emb = np.concatenate([freqs, freqs], -1).astype(np.float32)
    sign = np.tile(np.array([-1.0, 1.0], np.float32), HD // 2)
    for t in range(2):
        c[:, C_COS + t * 2 * D:C_COS + (t + 1) * 2 * D] = np.tile(np.cos(emb[place[t]]), (1, 2 * HEADS))
        c[:, C_SIN + t * 2 * D:C_SIN + (t + 1) * 2 * D] = np.tile(np.sin(emb[place[t]]) * sign, (1, 2 * HEADS))
    c[:KP, C_MULT] = mult
    c[:, C_TOKN:C_TOKN + 2] = place.T
    c[:, C_VALID] = 1
    c[:REST + 1, C_VALID + 1] = 1
    c[REST + 1:, C_FAR + 1] = FAR
    c[:, C_SLOT:C_SLOT + EXPERTS] = np.arange(EXPERTS) * REGION - 1
    c[:, C_IOTA:C_IOTA + EXPERTS] = EXPERTS - np.arange(EXPERTS)
    return c
```
